# Optimizing a Trainium2 kernel written in Bass

```python
import numpy as np
import jax
import jax.numpy as jnp

def _softmax(x, axis=-1):
    return jax.nn.softmax(x, axis=axis)
def _gelu(x):
    return jax.nn.gelu(x, approximate=True)
def _silu(x):
    return jax.nn.silu(x)
def _sigmoid(x):
    return jax.nn.sigmoid(x)
def _layernorm(x, axis=-1, eps=1e-5):
    m = jnp.mean(x, axis=axis, keepdims=True)
    v = jnp.var(x, axis=axis, keepdims=True)
    return (x - m) / jnp.sqrt(v + eps)
def _scatter_add(tgt, idx, src, axis=0):
    return tgt.at[idx].add(src)
def _segment_sum(src, seg, n):
    return jax.ops.segment_sum(src, seg, n)

kernel_name = 'mk_conv_preact_d2_conv_nchw512_13c884'

def setup_inputs(seed: int = 0):
    np.random.seed(seed)
    _w = jnp.asarray
    def _rec_inputs():
        import jax
        import jax.numpy as jnp
        _gk = jax.random.key(seed)
        x = -0.0002928 + 1 * jax.random.normal(jax.random.fold_in(_gk, 1), (8, 512, 32, 32), jnp.float32)
        return x
    x = _rec_inputs()
    def _L0_conv_setup():
        import jax, jax.numpy as jnp
        import numpy as np
        B, C1, C2, N, F, HEADS, E = (8, 512, 512, 2, 32, 4, 0.5)
        C = int(C2 * E)
        HD = C // HEADS
        BN_EPS = 0.001

        def conv2d(x, w, pad):
            return jax.lax.conv_general_dilated(x, w, (1, 1), [(pad, pad), (pad, pad)], dimension_numbers=('NCHW', 'OIHW', 'NCHW'))

        def bn_eval(x, p):
            g, b, m, v = p
            s = (g / jnp.sqrt(v + BN_EPS))[:, None, None]
            return (x - m[:, None, None]) * s + b[:, None, None]

        def cbs(x, w, p, pad):
            return jax.nn.silu(bn_eval(conv2d(x, w, pad), p))

        def bot_attention(x, qkv_w, rw, rh):
            b, c, h, w = x.shape
            hw = h * w
            qkv = conv2d(x, qkv_w, 0).reshape(b, 3, HEADS, HD, hw)
            q, k, v = (qkv[:, 0], qkv[:, 1], qkv[:, 2])
            r = (rw + rh).reshape(1, HEADS, HD, hw)
            logits = jnp.einsum('bhdi,bhdj->bhij', q, k + r) * HD ** (-0.5)
            a = jax.nn.softmax(logits, axis=-1)
            out = jnp.einsum('bhij,bhdj->bhdi', a, v)
            return out.reshape(b, c, h, w)
        key = jax.random.key(seed)
        ks = iter(jax.random.split(key, 32))

        def nrm(shape, s=0.05):
            return jax.random.normal(next(ks), shape, jnp.float32) * s

        def bnp(cc):
            return jnp.stack([1.0 + 0.1 * jax.random.normal(next(ks), (cc,), jnp.float32), 0.1 * jax.random.normal(next(ks), (cc,), jnp.float32), 0.1 * jax.random.normal(next(ks), (cc,), jnp.float32), 0.5 + jax.random.uniform(next(ks), (cc,), jnp.float32)])
        return {'x': jax.random.normal(next(ks), (B, C1, F, F), jnp.float32), 'cv1_w': nrm((2 * C, C1, 1, 1)), 'cv1_bn': bnp(2 * C), 'cv2_w': nrm((C2, (2 + N) * C, 1, 1)), 'cv2_bn': bnp(C2), 'm_cv1_w': nrm((N, C, C, 3, 3)), 'm_cv1_bn': jnp.stack([bnp(C) for _ in range(N)]), 'm_qkv_w': nrm((N, 3 * C, C, 1, 1)), 'm_rw': jax.random.normal(next(ks), (N, 1, HEADS, HD, 1, F), jnp.float32), 'm_rh': jax.random.normal(next(ks), (N, 1, HEADS, HD, F, 1), jnp.float32), 'm_cv2_w': nrm((N, C, C, 1, 1)), 'm_cv2_bn': jnp.stack([bnp(C) for _ in range(N)])}
    _L0_conv_all = _L0_conv_setup()
    _L0_conv_in = {k: v for k, v in _L0_conv_all.items() if k in ('cv1_w', 'cv1_bn', 'cv2_w', 'cv2_bn', 'm_cv1_w', 'm_cv1_bn', 'm_qkv_w', 'm_rw', 'm_rh', 'm_cv2_w', 'm_cv2_bn', )}
    del _L0_conv_all

    def _L1_conv_setup():
        import jax, jax.numpy as jnp
        import numpy as np
        from jax import lax
        EPS = 1e-05
        GROUPS = 16

        def _batchnorm(x, gamma, beta):
            m = jnp.mean(x, axis=(0, 2, 3), keepdims=True)
            v = jnp.mean((x - m) ** 2, axis=(0, 2, 3), keepdims=True)
            xhat = (x - m) * lax.rsqrt(v + EPS)
            return xhat * gamma[None, :, None, None] + beta[None, :, None, None]

        @jax.custom_vjp
        def binary_act(x):
            return jnp.sign(x)

        def _ba_fwd(x):
            return (jnp.sign(x), x)

        def _ba_bwd(x, g):
            return (jnp.clip(2.0 - 2.0 * jnp.abs(x), a_min=0.0) * g,)
        binary_act.defvjp(_ba_fwd, _ba_bwd)

        @jax.custom_vjp
        def binary_weight(w):
            return jnp.sign(w)

        def _bw_fwd(w):
            return (jnp.sign(w), w)

        def _bw_bwd(w, g):
            mask = jnp.logical_or(w >= 1.0, w <= -1.0)
            return (jnp.where(mask, 0.0, g),)
        binary_weight.defvjp(_bw_fwd, _bw_bwd)

        def _weight_scale(w):
            co = w.shape[0]
            wf = w.reshape(co, -1)
            bw = wf - jnp.mean(wf, axis=-1, keepdims=True)
            std = jnp.std(wf - jnp.mean(wf, axis=-1, keepdims=True), axis=-1, ddof=1, keepdims=True)
            bw = bw / std
            sw = jnp.mean(jnp.abs(bw), axis=-1).reshape(co, 1, 1, 1)
            return lax.stop_gradient(sw)
        key = jax.random.key(seed)
        ks = jax.random.split(key, 7)
        N, C, H, W = (64, 512, 32, 32)
        k = 3
        x = jax.random.normal(ks[0], (N, C, H, W), dtype=jnp.float32)
        conv_w = jax.random.normal(ks[1], (C, C // GROUPS, k, k), dtype=jnp.float32) * 0.1
        bn1_gamma = jnp.ones((C,), jnp.float32)
        bn1_beta = jnp.zeros((C,), jnp.float32)
        bn2_gamma = jnp.ones((C,), jnp.float32)
        bn2_beta = jnp.zeros((C,), jnp.float32)
        prelu_a = jnp.full((C,), 0.25, jnp.float32)
        return {'x': x, 'conv_w': conv_w, 'bn1_gamma': bn1_gamma, 'bn1_beta': bn1_beta, 'bn2_gamma': bn2_gamma, 'bn2_beta': bn2_beta, 'prelu_a': prelu_a}
    _L1_conv_all = _L1_conv_setup()
    _L1_conv_in = {k: v for k, v in _L1_conv_all.items() if k in ('conv_w', 'bn1_gamma', 'bn1_beta', 'bn2_gamma', 'bn2_beta', 'prelu_a', )}
    del _L1_conv_all

    return {
        "x": x,
        "L0_conv_cv1_w": _L0_conv_in["cv1_w"],
        "L0_conv_cv1_bn": _L0_conv_in["cv1_bn"],
        "L0_conv_cv2_w": _L0_conv_in["cv2_w"],
        "L0_conv_cv2_bn": _L0_conv_in["cv2_bn"],
        "L0_conv_m_cv1_w": _L0_conv_in["m_cv1_w"],
        "L0_conv_m_cv1_bn": _L0_conv_in["m_cv1_bn"],
        "L0_conv_m_qkv_w": _L0_conv_in["m_qkv_w"],
        "L0_conv_m_rw": _L0_conv_in["m_rw"],
        "L0_conv_m_rh": _L0_conv_in["m_rh"],
        "L0_conv_m_cv2_w": _L0_conv_in["m_cv2_w"],
        "L0_conv_m_cv2_bn": _L0_conv_in["m_cv2_bn"],
        "L1_conv_conv_w": _L1_conv_in["conv_w"],
        "L1_conv_bn1_gamma": _L1_conv_in["bn1_gamma"],
        "L1_conv_bn1_beta": _L1_conv_in["bn1_beta"],
        "L1_conv_bn2_gamma": _L1_conv_in["bn2_gamma"],
        "L1_conv_bn2_beta": _L1_conv_in["bn2_beta"],
        "L1_conv_prelu_a": _L1_conv_in["prelu_a"],
    }

def reference(x, L0_conv_cv1_w, L0_conv_cv1_bn, L0_conv_cv2_w, L0_conv_cv2_bn, L0_conv_m_cv1_w, L0_conv_m_cv1_bn, L0_conv_m_qkv_w, L0_conv_m_rw, L0_conv_m_rh, L0_conv_m_cv2_w, L0_conv_m_cv2_bn, L1_conv_conv_w, L1_conv_bn1_gamma, L1_conv_bn1_beta, L1_conv_bn2_gamma, L1_conv_bn2_beta, L1_conv_prelu_a):
    import jax
    import jax.numpy as jnp
    def _L0_conv_ref(x, cv1_w, cv1_bn, cv2_w, cv2_bn, m_cv1_w, m_cv1_bn, m_qkv_w, m_rw, m_rh, m_cv2_w, m_cv2_bn):
        import jax, jax.numpy as jnp
        import numpy as np
        B, C1, C2, N, F, HEADS, E = (8, 512, 512, 2, 32, 4, 0.5)
        C = int(C2 * E)
        HD = C // HEADS
        BN_EPS = 0.001

        def conv2d(x, w, pad):
            return jax.lax.conv_general_dilated(x, w, (1, 1), [(pad, pad), (pad, pad)], dimension_numbers=('NCHW', 'OIHW', 'NCHW'))

        def bn_eval(x, p):
            g, b, m, v = p
            s = (g / jnp.sqrt(v + BN_EPS))[:, None, None]
            return (x - m[:, None, None]) * s + b[:, None, None]

        def cbs(x, w, p, pad):
            return jax.nn.silu(bn_eval(conv2d(x, w, pad), p))

        def bot_attention(x, qkv_w, rw, rh):
            b, c, h, w = x.shape
            hw = h * w
            qkv = conv2d(x, qkv_w, 0).reshape(b, 3, HEADS, HD, hw)
            q, k, v = (qkv[:, 0], qkv[:, 1], qkv[:, 2])
            r = (rw + rh).reshape(1, HEADS, HD, hw)
            logits = jnp.einsum('bhdi,bhdj->bhij', q, k + r) * HD ** (-0.5)
            a = jax.nn.softmax(logits, axis=-1)
            out = jnp.einsum('bhij,bhdj->bhdi', a, v)
            return out.reshape(b, c, h, w)
        t = cbs(x, cv1_w, cv1_bn, 0)
        ys = [t[:, :C], t[:, C:]]
        for i in range(N):
            yi = ys[-1]
            z = cbs(yi, m_cv1_w[i], m_cv1_bn[i], 1)
            z = bot_attention(z, m_qkv_w[i], m_rw[i], m_rh[i])
            z = jax.nn.silu(bn_eval(conv2d(z, m_cv2_w[i], 0), m_cv2_bn[i]))
            ys.append(yi + z)
        return cbs(jnp.concatenate(ys, axis=1), cv2_w, cv2_bn, 0)

    def _L1_conv_ref(x, conv_w, bn1_gamma, bn1_beta, bn2_gamma, bn2_beta, prelu_a):
        import jax, jax.numpy as jnp
        import numpy as np
        from jax import lax
        EPS = 1e-05
        GROUPS = 16

        def _batchnorm(x, gamma, beta):
            m = jnp.mean(x, axis=(0, 2, 3), keepdims=True)
            v = jnp.mean((x - m) ** 2, axis=(0, 2, 3), keepdims=True)
            xhat = (x - m) * lax.rsqrt(v + EPS)
            return xhat * gamma[None, :, None, None] + beta[None, :, None, None]

        @jax.custom_vjp
        def binary_act(x):
            return jnp.sign(x)

        def _ba_fwd(x):
            return (jnp.sign(x), x)

        def _ba_bwd(x, g):
            return (jnp.clip(2.0 - 2.0 * jnp.abs(x), a_min=0.0) * g,)
        binary_act.defvjp(_ba_fwd, _ba_bwd)

        @jax.custom_vjp
        def binary_weight(w):
            return jnp.sign(w)

        def _bw_fwd(w):
            return (jnp.sign(w), w)

        def _bw_bwd(w, g):
            mask = jnp.logical_or(w >= 1.0, w <= -1.0)
            return (jnp.where(mask, 0.0, g),)
        binary_weight.defvjp(_bw_fwd, _bw_bwd)

        def _weight_scale(w):
            co = w.shape[0]
            wf = w.reshape(co, -1)
            bw = wf - jnp.mean(wf, axis=-1, keepdims=True)
            std = jnp.std(wf - jnp.mean(wf, axis=-1, keepdims=True), axis=-1, ddof=1, keepdims=True)
            bw = bw / std
            sw = jnp.mean(jnp.abs(bw), axis=-1).reshape(co, 1, 1, 1)
            return lax.stop_gradient(sw)
        res = x
        h = _batchnorm(x, bn1_gamma, bn1_beta)
        h = binary_act(h)
        sw = _weight_scale(conv_w)
        bw = binary_weight(conv_w) * sw
        h = lax.conv_general_dilated(h, bw, window_strides=(1, 1), padding=((1, 1), (1, 1)), feature_group_count=GROUPS, dimension_numbers=('NCHW', 'OIHW', 'NCHW'))
        h = _batchnorm(h, bn2_gamma, bn2_beta)
        h = h + res
        a = prelu_a[None, :, None, None]
        return jnp.where(h > 0, h, a * h)

    def _gn(v, G=32, eps=1e-5):
        B_, C_, H_, W_ = v.shape
        g = v.reshape(B_, G, C_ // G, H_, W_)
        m = jnp.mean(g, axis=(2, 3, 4), keepdims=True)
        s = jnp.var(g, axis=(2, 3, 4), keepdims=True)
        return ((g - m) / jnp.sqrt(s + eps)).reshape(v.shape)

    def _ln_c(v, eps=1e-6):
        m = jnp.mean(v, axis=1, keepdims=True)
        s = jnp.var(v, axis=1, keepdims=True)
        return (v - m) / jnp.sqrt(s + eps)

    def _ln_t(v, eps=1e-5):
        m = jnp.mean(v, axis=-1, keepdims=True)
        s = jnp.var(v, axis=-1, keepdims=True)
        return (v - m) / jnp.sqrt(s + eps)

    def _to_tokens(v):
        B_, C_, H_, W_ = v.shape
        return v.reshape(B_, C_, H_ * W_).transpose(0, 2, 1)
    def _from_tokens(t, like):
        B_, C_, H_, W_ = like.shape
        return t.transpose(0, 2, 1).reshape(B_, C_, H_, W_)

    x = x + _L0_conv_ref(_gn(x), L0_conv_cv1_w, L0_conv_cv1_bn, L0_conv_cv2_w, L0_conv_cv2_bn, L0_conv_m_cv1_w, L0_conv_m_cv1_bn, L0_conv_m_qkv_w, L0_conv_m_rw, L0_conv_m_rh, L0_conv_m_cv2_w, L0_conv_m_cv2_bn)
    x = x + _L1_conv_ref(_gn(x), L1_conv_conv_w, L1_conv_bn1_gamma, L1_conv_bn1_beta, L1_conv_bn2_gamma, L1_conv_bn2_beta, L1_conv_prelu_a)
    return x


_drawn_inputs = setup_inputs


def setup_inputs(seed=0):
    import zlib

    import numpy as np

    out = dict(_drawn_inputs(seed))
    spreads = {'L1_conv_bn1_gamma': (1.0, 0.2),
     'L1_conv_bn1_beta': (0.0, 0.1),
     'L1_conv_bn2_gamma': (1.0, 0.2),
     'L1_conv_bn2_beta': (0.0, 0.1),
     'L1_conv_prelu_a': (0.25, 0.6)}
    factors = {}
    for name, (base, spread) in spreads.items():
        noise = np.random.default_rng([zlib.crc32(name.encode()), seed]).standard_normal(out[name].shape)
        drawn = base * np.exp(spread * noise) if base else spread * noise
        out[name] = jnp.asarray(drawn.astype(out[name].dtype))
    for name, factor in factors.items():
        out[name] = (out[name] * factor).astype(out[name].dtype)
    return out
```

```python
from contextlib import ExitStack

import concourse.bass as bass
from concourse import mybir

P = 128
F32 = mybir.dt.float32
F32R = mybir.dt.float32r
F16 = mybir.dt.float16
BF16 = mybir.dt.bfloat16
ACT = mybir.ActivationFunctionType
ALU = mybir.AluOpType
AX = mybir.AxisListType

HW, W = 1024, 32
NB = 512
NC = HW // NB
ROWS = NB // W
PW = W + 2
HEADS, HD = 4, 64
SCALE = float(HD) ** -0.5
BN0_EPS, GN_EPS, BN1_EPS = 1e-3, 1e-5, 1e-5
TAPS = 9
KT = 2
W3N, WQN, WMN = KT * TAPS * 256, KT * 768, KT * 256
WBN = W3N + WQN + WMN
PIECE = 512
MAX_AT = [2, 1, 1, 2, 1, 1, 0, 0]


def f32(ap):
    return ap.bitcast(F32)


def start_at_one(nc, sems):
    with nc.Block() as block:
        for k, engine in enumerate((block.sync, block.gpsimd, block.scalar, block.vector, block.tensor)):
            @engine
            def _(eng, k=k):
                for s in sems[k::5]:
                    eng.sem_inc(s, 1)


def alone(eng, sem):
    eng.sem_inc(sem, 1)


def images(eng, n_img, body):
    if n_img > 2:
        with eng.Fori(0, n_img // 2 - 1) as j:
            body(j, 0, 2)
            body(j, 1, 2)
    body(n_img // 2 - 1, 0, 1)
    body(n_img // 2 - 1, 1, 0)


def split_weights(sems, dram, stage, w_hi, w_lo, cols):
    d_stage, s_hi, s_lo = sems
    n_piece = (cols + PIECE - 1) // PIECE
    span = lambda i: slice(i * PIECE, min(cols, (i + 1) * PIECE))

    def load(sp):
        for i in range(n_piece):
            if i >= 2:
                sp.wait_ge(s_lo, 1 + i - 1)
            k = span(i)
            sp.dma_start(stage[:, i % 2, 0:k.stop - k.start], dram[:, k]).then_inc(d_stage[i % 2], 16)

    def hi(act):
        for i in range(n_piece):
            k = span(i)
            act.wait_ge(d_stage[i % 2], 1 + 16 * (i // 2 + 1))
            act.activation(w_hi[:, k], stage[:, i % 2, 0:k.stop - k.start], ACT.Copy).then_inc(s_hi, 1)

    def lo(dve):
        for i in range(n_piece):
            k = span(i)
            dve.wait_ge(s_hi, 1 + i + 1)
            dve.tensor_tensor(w_lo[:, k], stage[:, i % 2, 0:k.stop - k.start], f32(w_hi[:, k]),
                              ALU.subtract).then_inc(s_lo, 1)

    return load, hi, lo, n_piece


def program(nc, x, w_cv1, w_b, w_cv2, bn0, rw, rh, w1_rows, w1_t, bn1, out):
    B = x.shape[0]
    CT = x.shape[1] // P
    x_v = x.rearrange("b (t p) n -> b t p n", p=P)
    out_v = out.rearrange("b (t p) n -> b t p n", p=P)
    y_d = nc.dram_tensor("y_d", (B, 8, P, HW), F32, kind="Internal").ap()
    x1_d = nc.dram_tensor("x1_d", (B, CT, P, HW), F32, kind="Internal").ap()
    rs_d = nc.dram_tensor("rs_d", (1, HW), F32, kind="Internal").ap()

    with ExitStack() as top:
        def keep(name, shape, dt):
            return top.enter_context(nc.sbuf_tensor(name, shape, dt))

        bank = top.enter_context(nc.psum_tensor("bank", [P, 8, NB], F32))
        bn_s = keep("bn_s", [P, 16], F32)
        bn_o = keep("bn_o", [P, 16], F32)
        group_avg = keep("group_avg", [P, P], F32)
        mhalf = keep("mhalf", [P, 4 * B], F32)
        x1_mv = keep("x1_mv", [P, B, CT, 2], F32)

        phase_a(nc, B, CT, x_v, w_cv1, bn0, y_d, bank, bn_s, bn_o, group_avg, mhalf)
        phase_b(nc, B, w_b, rw, rh, y_d, rs_d, bank, bn_s, bn_o)
        phase_d(nc, B, CT, x_v, w_cv2, y_d, x1_d, bank, bn_s, bn_o, x1_mv)
        phase_l(nc, B, CT, w1_rows, w1_t, bn1, x1_d, out_v, bank, group_avg, mhalf, x1_mv)


def phase_a(nc, B, CT, x_v, w_cv1, bn0, y_d, bank, bn_s, bn_o, group_avg, mhalf):
    with ExitStack() as ctx:
        def sb(name, shape, dt):
            return ctx.enter_context(nc.sbuf_tensor("a_" + name, shape, dt))

        def sem(name):
            sems.append(ctx.enter_context(nc.semaphore("a_" + name)))
            return sems[-1]

        sems = []

        w_hi = sb("w_hi", [P, CT * 512], F32R)
        w_lo = sb("w_lo", [P, CT * 512], F32R)
        stage = sb("stage", [P, 2, PIECE], F32)
        bn_in = sb("bn_in", [P, 4, 16], F32)
        bn_t = sb("bn_t", [P, 2, 16], F32)
        xin = sb("xin", [P, 2, CT, HW], F32)
        xh = sb("xh", [P, 2, CT, HW], F32R)
        xl = sb("xl", [P, 2, CT, HW], F32R)
        stats = sb("stats", [P, CT, NC, 6], F32)
        mv = sb("mv", [P, CT, 2], F32)
        dev = sb("dev", [P, CT], F32)
        gm = sb("gm", [P, CT], F32)
        var = sb("var", [P, CT], F32)
        rg = sb("rg", [P, CT], F32)
        sh = sb("sh", [P, CT], F32)
        iota_p = sb("iota_p", [P, P], F32)
        y_sb = sb("y_sb", [P, 4, NB], F32)

        d_bn = sem("d_bn")
        s_spare = sem("s_spare")
        d_stage = [sem(f"d_stage{i}") for i in range(2)]
        s_whi, s_wlo = sem("s_whi"), sem("s_wlo")
        d_x = [sem(f"d_x{i}") for i in range(2)]
        s_chain = sem("s_chain")
        s_setup = sem("s_setup")
        s_eps, s_rs = sem("s_eps"), sem("s_rs")
        s_mv, s_gm, s_dev, s_gv = sem("s_mv"), sem("s_gm"), sem("s_dev"), sem("s_gv")
        s_xf, s_xh, s_xl = sem("s_xf"), sem("s_xh"), sem("s_xl")
        s_mm, s_y = sem("s_mm"), sem("s_y")
        d_y = [sem(f"d_y{i}") for i in range(4)]
        G8 = CT * NC
        SLOTS = 4
        stat_bank = 7
        load_w, hi_w, lo_w, n_piece = split_weights((d_stage, s_whi, s_wlo), w_cv1, stage, w_hi, w_lo, CT * 512)
        start_at_one(nc, sems)
        block = ctx.enter_context(nc.Block())

        @block.sync
        def _(sp):
            sp.dma_start(bn_in[:], bn0).then_inc(d_bn, 16)
            for t in range(CT):
                sp.dma_start(xin[:, 0, t, :], x_v[0, t]).then_inc(d_x[0], 16)
            load_w(sp)
            for t in range(CT):
                sp.dma_start(xin[:, 1, t, :], x_v[1, t]).then_inc(d_x[1], 16)

            def image(j, u, left):
                n = 2 * j + u
                if left == 2:
                    sp.wait_ge(s_xl, 1 + CT * (n + 1))
                    alone(sp, s_spare)
                    for t in range(CT):
                        sp.dma_start(xin[:, u, t, :], x_v[n + 2, t]).then_inc(d_x[u], 16)
                for g in range(G8):
                    sp.wait_ge(s_y, 1 + SLOTS + G8 * n + g + 1)
                    alone(sp, s_spare)
                    sp.dma_start(y_d[n, g // NC][:, (g % NC) * NB:(g % NC + 1) * NB],
                                 y_sb[:, g % SLOTS, :]).then_inc(d_y[g % SLOTS], 16)

            images(sp, B, image)
            for i in range(SLOTS):
                sp.wait_ge(d_y[i], 1 + 16 * B * G8 // SLOTS)

        @block.gpsimd
        def _(pool):
            pool.memset(mhalf[:], -0.5).then_inc(s_setup, 1)
            pool.memset(group_avg[:], 1.0 / 16).then_inc(s_setup, 1)
            pool.wait_ge(s_setup, 3)
            g3 = group_avg[:].rearrange("p (g c) -> p g c", c=16)
            pool.affine_select(out=g3, in_=g3, compare_op=ALU.is_ge, fill=0.0, base=0,
                               pattern=[[-16, 8], [0, 16]], channel_multiplier=1).then_inc(s_setup, 1)
            pool.wait_ge(s_setup, 4)
            pool.affine_select(out=g3, in_=g3, compare_op=ALU.is_ge, fill=0.0, base=15,
                               pattern=[[16, 8], [0, 16]], channel_multiplier=-1).then_inc(s_setup, 1)
            pool.wait_ge(s_eps, 2)
            pool.tensor_tensor(bn_t[:, 1, :], bn_t[:, 0, :], mhalf[:, 0:16] if 4 * B >= 16 else mhalf[:, 0:1].to_broadcast([P, 16]),
                               ALU.pow).then_inc(s_rs, 1)

            def stat(n):
                pool.wait_ge(s_eps, 1 + n + 2)
                pool.wait_ge(s_xf, 1 + CT * n)
                pool.tensor_tensor(rg[:], var[:], mhalf[:, 0:CT], ALU.pow).then_inc(s_rs, 1)

            stat(0)
            images(pool, B, lambda j, u, left: stat(2 * j + u + 1) if left else None)

        @block.vector
        def _(dve):
            links = [0]

            def link(ins):
                links[0] += 1
                ins.then_inc(s_chain, 1)
                dve.wait_ge(s_chain, 1 + links[0])

            dve.wait_ge(d_bn, 17)
            dve.tensor_scalar(bn_t[:, 0, :], bn_in[:, 3, :], BN0_EPS, None, ALU.add).then_inc(s_eps, 1)
            dve.wait_ge(s_rs, 2)
            link(dve.tensor_tensor(bn_s[:], bn_in[:, 0, :], bn_t[:, 1, :], ALU.mult))
            link(dve.tensor_tensor(bn_t[:, 0, :], bn_in[:, 2, :], bn_s[:], ALU.mult))
            link(dve.tensor_tensor(bn_o[:], bn_in[:, 1, :], bn_t[:, 0, :], ALU.subtract))
            LINKS = 4
            base = links[0]

            def statistics(n, pairs, u):
                dve.wait_ge(d_x[u], 1 + 16 * CT * pairs)
                c = base + LINKS * n
                for t in range(CT):
                    for k in range(NC):
                        ins = dve.bn_stats(stats[:, t, k, :], xin[:, u, t, k * NB:(k + 1) * NB])
                ins.then_inc(s_chain, 1)
                dve.wait_ge(s_chain, 1 + c + 1)
                alone(dve, s_spare)
                for t in range(CT):
                    ins = dve.bn_aggr(mv[:, t, :], stats[:, t, :, :])
                ins.then_inc(s_mv, 1)
                dve.wait_ge(s_gm, 1 + n + 1)
                dve.tensor_copy(gm[:], bank[:, stat_bank, 0:CT]).then_inc(s_chain, 1)
                dve.wait_ge(s_chain, 1 + c + 2)
                dve.tensor_tensor(dev[:], mv[:, :, 0], gm[:], ALU.subtract).then_inc(s_chain, 1)
                dve.wait_ge(s_chain, 1 + c + 3)
                dve.tensor_tensor(sh[:], dev[:], dev[:], ALU.mult).then_inc(s_chain, 1)
                dve.wait_ge(s_chain, 1 + c + 4)
                dve.tensor_tensor(dev[:], mv[:, :, 1], sh[:], ALU.add).then_inc(s_dev, 1)
                dve.wait_ge(s_gv, 1 + n + 1)
                dve.tensor_scalar(var[:], bank[:, stat_bank, 8:8 + CT], GN_EPS, None, ALU.add).then_inc(s_eps, 1)
                dve.wait_ge(s_rs, 1 + n + 2)
                for t in range(CT):
                    dve.tensor_scalar(xin[:, u, t, :], xin[:, u, t, :], gm[:, t:t + 1], rg[:, t:t + 1],
                                      ALU.subtract, ALU.mult).then_inc(s_xf, 1)
                for t in range(CT):
                    dve.wait_ge(s_xh, 1 + CT * n + t + 1)
                    dve.tensor_tensor(xl[:, u, t, :], xin[:, u, t, :], f32(xh[:, u, t, :]),
                                      ALU.subtract).then_inc(s_xl, 1)

            statistics(0, 1, 0)
            lo_w(dve)
            images(dve, B, lambda j, u, left: statistics(2 * j + u + 1, j + u + 1, 1 - u) if left else None)

        @block.scalar
        def _(act):
            def high(n, u):
                for t in range(CT):
                    act.wait_ge(s_xf, 1 + CT * n + t + 1)
                    act.activation(xh[:, u, t, :], xin[:, u, t, :], ACT.Copy).then_inc(s_xh, 1)

            def group(n, j, u, g):
                m = g // NC
                act.wait_ge(s_mm, 1 + G8 * n + g + 1)
                act.wait_ge(d_y[g % SLOTS], 1 + 32 * n + 16 * (g // SLOTS))
                act.activation(y_sb[:, g % SLOTS, :], bank[:, g % SLOTS, :], ACT.Silu, scale=bn_s[:, m:m + 1],
                               bias=bn_o[:, m:m + 1]).then_inc(s_y, 1)

            act.sem_inc(s_y, SLOTS)
            high(0, 0)
            hi_w(act)
            act.wait_ge(s_chain, 4)

            def image(j, u, left):
                n = 2 * j + u
                for g in range(G8):
                    group(n, j, u, g)
                    if g == 2 and left:
                        act.wait_ge(s_mm, 1 + G8 * n)
                        high(n + 1, 1 - u)

            images(act, B, image)

        @block.tensor
        def _(pe):
            def mean(n):
                pe.wait_ge(s_mv, 1 + n + 1)
                pe.matmul(bank[:, stat_bank, 0:CT], group_avg[:], mv[:, :, 0], start=True, stop=True).then_inc(s_gm, 1)

            def variance(n):
                pe.wait_ge(s_dev, 1 + n + 1)
                pe.matmul(bank[:, stat_bank, 8:8 + CT], group_avg[:], dev[:], start=True, stop=True).then_inc(s_gv, 1)

            def group(n, u, g):
                m, c = g // NC, g % NC
                if g == 0:
                    pe.wait_ge(s_xl, 1 + CT * (n + 1))
                pe.wait_ge(s_y, 1 + G8 * n + g + 1)
                px = slice(c * NB, (c + 1) * NB)
                ps = bank[:, g % SLOTS, :]
                for k in range(CT):
                    wk = slice(k * 512 + m * P, k * 512 + (m + 1) * P)
                    pe.matmul(ps, w_hi[:, wk], xh[:, u, k, px], start=k == 0, stop=False)
                    pe.matmul(ps, w_hi[:, wk], xl[:, u, k, px], start=False, stop=False)
                    mm = pe.matmul(ps, w_lo[:, wk], xh[:, u, k, px], start=False, stop=k == CT - 1)
                mm.then_inc(s_mm, 1)

            pe.wait_ge(s_setup, 5)
            mean(0)
            variance(0)
            pe.wait_ge(s_whi, 1 + n_piece)
            pe.wait_ge(s_wlo, 1 + n_piece)

            def image(j, u, left):
                n = 2 * j + u
                for g in range(G8):
                    group(n, u, g)
                    if left and g == 1:
                        mean(n + 1)
                    if left and g == 3:
                        variance(n + 1)

            images(pe, B, image)


def phase_b(nc, B, w_b, rw, rh, y_d, rs_d, bank, bn_s, bn_o):
    L = w_b.shape[0]
    with ExitStack() as ctx:
        def sb(name, shape, dt):
            return ctx.enter_context(nc.sbuf_tensor("b_" + name, shape, dt))

        def sem(name):
            sems.append(ctx.enter_context(nc.semaphore("b_" + name)))
            return sems[-1]

        sems = []

        def sem2(name):
            return [sem(name + "0"), sem(name + "1")]

        w_hi = sb("w_hi", [P, WBN], F32R)
        w_lo = sb("w_lo", [P, WBN], F32R)
        coef = sb("coef", [P, 2, 4], F32)
        rws = sb("rws", [P, 2, W], F32)
        rhs = sb("rhs", [P, 2, W], F32)
        y_in = sb("y_in", [P, KT, HW], F32)
        yp_h = sb("yp_h", [P, KT, PW, PW], F32R)
        yp_l = sb("yp_l", [P, KT, PW, PW], F32R)
        z_h = sb("z_h", [P, KT, HW], F32R)
        z_l = sb("z_l", [P, KT, HW], F32R)
        zf = sb("zf", [P, 2, NB], F32)
        kf = sb("kf", [P, HW], F32)
        qq = sb("qq", [P, 2, HW], F32R)
        qm = sb("qm", [P, 2, HW], F32R)
        kk = sb("kk", [P, 2, HW], F32R)
        k1 = sb("k1", [P, 2, HW], F32R)
        v_h = sb("v_h", [P, 8, 2, 3, HD], F32R)
        v_l = sb("v_l", [P, 8, 2, 3, HD], F32R)
        a_f = sb("a_f", [P, 2, HW], F32)
        a_h = sb("a_h", [P, 2, HW], F32R)
        a_l = sb("a_l", [P, 2, HW], F32R)
        mt = sb("mt", [P, 2, 8], F32R)
        os = sb("os", [P, HW], F32)
        r8 = sb("r8", [P, 8], F32)
        r8i = sb("r8i", [P, 8], F32)
        rb = kf
        o_h = sb("o_h", [P, KT, HW], F32R)
        o_l = sb("o_l", [P, KT, HW], F32R)
        res = sb("res", [P, 2, NB], F32)

        d_w = sem2("d_w")
        s_whi, s_wlo = sem("s_whi"), sem("s_wlo")
        s_coef, d_r = sem("s_coef"), sem("d_r")
        s_const, s_const_rows = sem("s_const"), sem("s_const_rows")
        s_spare, s_spare_pool = sem("s_spare"), sem("s_spare_pool")
        d_y = sem2("d_y")
        s_yhi, s_ylo = sem("s_yhi"), sem("s_ylo")
        s_cv, s_raw, s_zf, s_zhi, s_zlo = sem("s_cv"), sem("s_raw"), sem("s_zf"), sem("s_zhi"), sem("s_zlo")
        s_qk, s_v = sem("s_qk"), sem("s_v")
        s_qhi, s_qlo = sem("s_qhi"), sem("s_qlo")
        s_kr, s_kf, s_khi, s_klo = sem("s_kr"), sem("s_kf"), sem("s_khi"), sem("s_klo")
        d_qq, d_k1, d_m = sem2("d_qq"), sem2("d_k1"), sem2("d_m")
        s_vhi, s_vlo = sem("s_vhi"), sem("s_vlo")
        s_mx, s_mr = sem("s_mx"), sem("s_mr")
        s_lt, s_af, s_ah, s_al, s_av = sem("s_lt"), sem("s_af"), sem("s_ah"), sem("s_al"), sem("s_av")
        s_os, d_s8, s_rc, d_rc, d_rb = sem("s_os"), sem("d_s8"), sem("s_rc"), sem("d_rc"), sem("d_rb")
        s_om, s_ohi, s_olo = sem("s_om"), sem("s_ohi"), sem("s_olo")
        s_cm, s_cf = sem("s_cm"), sem("s_cf")
        d_res, s_res, d_out = sem2("d_res"), sem("s_res"), sem2("d_out")

        n_piece = (WBN + PIECE - 1) // PIECE
        w3 = lambda w: w[:, 0:W3N].rearrange("p (k t c) -> p k t c", k=KT, t=TAPS)
        wq = lambda w: w[:, W3N:W3N + WQN].rearrange("p (k c) -> p k c", k=KT)
        wm = lambda w: w[:, W3N + WQN:WBN].rearrange("p (k c) -> p k c", k=KT)
        w3h, w3l, wqh, wql, wmh, wml = w3(w_hi), w3(w_lo), wq(w_hi), wq(w_lo), wm(w_hi), wm(w_lo)

        W_SLOT = [(n_piece + 1) // 2, n_piece // 2]

        def span(i):
            return slice(i * PIECE, min(WBN, (i + 1) * PIECE))

        def own(h):
            return slice(HD * (h % 2), HD * (h % 2) + HD)

        def other(h):
            return own(h + 1)

        def first_other(h):
            return slice(HD * (1 - h % 2), HD * (1 - h % 2) + 1)

        def px(c):
            return slice(c * NB, (c + 1) * NB)

        def two(b0):
            return bank[:, b0:b0 + 2, :].rearrange("p a n -> p (a n)")

        def layers(eng, start, image):
            with eng.Fori(0, L) as l:
                start(l)
                if B > 2:
                    with eng.Fori(0, B - 2) as b:
                        image(l * B + b, l, b, True, True)
                image(l * B + B - 2, l, B - 2, True, False)
                image(l * B + B - 1, l, B - 1, False, False)

        start_at_one(nc, sems)
        block = ctx.enter_context(nc.Block())

        @block.tensor
        def _(pe):
            CONV_BANK = [2, 3, 4, 5]

            def conv_terms(g):
                c, m = g // 2, g % 2
                co = slice(m * P, (m + 1) * P)
                terms = []
                for k in range(KT):
                    for t in range(TAPS):
                        dy, dx = t // 3, t % 3
                        win = (slice(None), k, slice(dy + ROWS * c, dy + ROWS * (c + 1)), slice(dx, dx + W))
                        terms += [(w3h[:, k, t, co], yp_h[win]), (w3h[:, k, t, co], yp_l[win]),
                                  (w3l[:, k, t, co], yp_h[win])]
                return terms

            def conv(i, g, lo, hi):
                terms = conv_terms(g)
                ps = bank[:, CONV_BANK[g], :].rearrange("p (r c) -> p r c", c=W)
                if lo == 0:
                    pe.wait_ge(s_yhi, 1 + KT * (i + 1))
                    pe.wait_ge(s_ylo, 1 + KT * (i + 1))
                for n in range(lo, min(hi, len(terms))):
                    mm = pe.matmul(ps, terms[n][0], terms[n][1], start=n == 0, stop=n == len(terms) - 1)
                if lo < len(terms) <= hi:
                    mm.then_inc(s_cv, 1)

            def start(l):
                pe.wait_ge(s_const, 2)
                pe.wait_ge(s_const_rows, 3)
                pe.wait_ge(s_whi, 1 + n_piece * (l + 1))
                pe.wait_ge(s_wlo, 1 + n_piece * (l + 1))
                pe.wait_ge(s_cf, 1 + 4 * B * l)
                pe.wait_ge(s_mr, 1 + 32 * B * l)
                for g in range(4):
                    conv(l * B, g, 0, 54)

            def qk(it, p):
                if p == 0:
                    pe.wait_ge(s_zhi, 1 + 4 * (it + 1))
                    pe.wait_ge(s_zlo, 1 + 4 * (it + 1))
                    pe.wait_ge(s_cf, 1 + 4 * it)
                else:
                    pe.wait_ge(s_af, 1 + 32 * it + 16)
                    pe.wait_ge(s_ah, 1 + 32 * it + 16)
                for part in (1, 0):
                    co = slice(part * 256 + p * P, part * 256 + (p + 1) * P)
                    for c in range(NC):
                        ps = bank[:, 2 * part + c, :]
                        for k in range(KT):
                            pe.matmul(ps, wqh[:, k, co], z_h[:, k, px(c)], start=k == 0, stop=False)
                            pe.matmul(ps, wqh[:, k, co], z_l[:, k, px(c)], start=False, stop=False)
                            mm = pe.matmul(ps, wql[:, k, co], z_h[:, k, px(c)], start=False, stop=k == KT - 1)
                    mm.then_inc(s_qk, 1)

            def values(it, half):
                if half == 0:
                    pe.wait_ge(s_os, 1 + 4 * it)
                else:
                    pe.wait_ge(s_qhi, 1 + 4 * it + 2)
                    pe.wait_ge(s_qlo, 1 + 4 * it + 2)
                for jb in range(4):
                    j = slice((4 * half + jb) * P, (4 * half + jb + 1) * P)
                    ps = bank[:, (6 if half == 0 else 0) + jb // 2, (jb % 2) * 256:(jb % 2 + 1) * 256]
                    for k in range(KT):
                        pe.matmul(ps, z_h[:, k, j], wqh[:, k, 512:768], start=k == 0, stop=False)
                        pe.matmul(ps, z_h[:, k, j], wql[:, k, 512:768], start=False, stop=False)
                        mm = pe.matmul(ps, z_l[:, k, j], wqh[:, k, 512:768], start=False, stop=k == KT - 1)
                mm.then_inc(s_v, 1)

            def max_block(it, h, n, b0):
                for c in range(NC):
                    mm = pe.matmul(bank[:, b0 + c, :], qq[:, h % 2, n:HW:8], kk[:, h % 2, px(c)], start=True, stop=True)
                mm.then_inc(s_mx, 1)

            def logits(it, h, t):
                b0 = 2 * (t % 2)
                if t == 0:
                    pe.wait_ge(d_m[h % 2], 1 + 16 * (2 * it + h // 2 + 1))
                    pe.wait_ge(s_qlo, 1 + 4 * it + h + 1)
                    pe.wait_ge(d_k1[h % 2], 1 + 16 * (2 * it + h // 2 + 1))
                if t >= 2 or h % 2 == 1:
                    pe.wait_ge(s_af, 1 + 32 * it + 8 * h + t - 1)
                    pe.wait_ge(s_ah, 1 + 32 * it + 8 * h + t - 1)
                j = slice(t * P, (t + 1) * P)
                for c in range(NC):
                    pe.matmul(bank[:, b0 + c, :], kk[:, h % 2, j], qq[:, h % 2, px(c)], start=True, stop=False)
                for c in range(NC):
                    mm = pe.matmul(bank[:, b0 + c, :], k1[:, h % 2, j], qm[:, h % 2, px(c)], start=False, stop=True)
                mm.then_inc(s_lt, 1)

            def weighted(it, h, t):
                T = 32 * it + 8 * h + t
                first, last = t == 0, t == 7
                if h % 2 == 0:
                    vh = v_h[:, t, h // 2, 0:2, :].rearrange("p s c -> p (s c)")
                    vl, rows = v_l[:, t, h // 2, 0, :], slice(0, HD)
                else:
                    vh = v_h[:, t, h // 2, 1:3, :].rearrange("p s c -> p (s c)")
                    vl, rows = v_l[:, t, h // 2, 1:3, :].rearrange("p s c -> p (s c)"), slice(0, P)
                pe.wait_ge(s_ah, 1 + T + 1)
                for c in range(NC):
                    pe.matmul(bank[:, 6 + c, :], vh, a_h[:, t % 2, px(c)], start=first, stop=False)
                for c in range(NC):
                    pe.matmul(bank[rows, 6 + c, :], vl, a_h[:, t % 2, px(c)], start=False, stop=False)
                pe.wait_ge(s_al, 1 + T + 1)
                for c in range(NC):
                    mm = pe.matmul(bank[:, 6 + c, :], vh, a_l[:, t % 2, px(c)], start=False, stop=last)
                mm.then_inc(s_av, 1)

            def pair(it, p, filler, lead, step):
                ha, hb = 2 * p, 2 * p + 1
                if filler:
                    pe.wait_ge(s_kf, 1 + 2 * it + p + 1)
                    conv(*filler, 0, lead)
                pe.wait_ge(d_qq[0], 1 + 16 * (2 * it + p + 1))
                pe.wait_ge(s_khi, 1 + 4 * it + ha + 1)
                pe.wait_ge(s_klo, 1 + 4 * it + ha + 1)
                for n in range(8):
                    m = 32 * it + 8 * ha + n
                    if n == 0:
                        pe.wait_ge(s_mr, 1 + m)
                    elif n == 1:
                        if p == 0:
                            pe.wait_ge(s_vhi, 1 + 2 * it + 1)
                            pe.wait_ge(s_vlo, 1 + 2 * it + 1)
                        else:
                            pe.wait_ge(s_os, 1 + 4 * it + ha)
                    else:
                        pe.wait_ge(s_mr, 1 + m - 1)
                    max_block(it, ha, n, 4 if n % 2 == 0 else 6)
                    if filler:
                        conv(*filler, lead + n * step, lead + (n + 1) * step)
                if filler:
                    conv(*filler, lead + 8 * step, 54)
                if p == 0:
                    pe.wait_ge(s_vhi, 1 + 2 * it + 2)
                    pe.wait_ge(s_vlo, 1 + 2 * it + 2)
                pe.wait_ge(s_qhi, 1 + 4 * it + hb + 1)
                pe.wait_ge(s_qlo, 1 + 4 * it + hb + 1)
                logits(it, ha, 0)
                pe.wait_ge(s_kf, 1 + 2 * it + p + 1)
                if filler:
                    pe.wait_ge(s_raw, 1 + 2 * (it + 1) + p + 1)
                n = 0
                for h in (ha, hb):
                    for t in range(8):
                        if h == ha:
                            for _ in range(MAX_AT[t]):
                                if n == 0:
                                    pe.wait_ge(d_qq[1], 1 + 16 * (2 * it + p + 1))
                                    pe.wait_ge(s_khi, 1 + 4 * it + hb + 1)
                                    pe.wait_ge(s_klo, 1 + 4 * it + hb + 1)
                                pe.wait_ge(s_mr, 1 + 32 * it + 8 * hb + n)
                                max_block(it, hb, n, 4)
                                n += 1
                        if t < 7:
                            logits(it, h, t + 1)
                        elif h == ha:
                            logits(it, hb, 0)
                        if t == 0:
                            if h == ha:
                                pe.wait_ge(s_mr, 1 + 32 * it + 8 * ha + 8)
                            else:
                                pe.wait_ge(s_os, 1 + 4 * it + h)
                        weighted(it, h, t)

            def out_conv(it):
                pe.wait_ge(s_ohi, 1 + 4 * (it + 1))
                pe.wait_ge(s_olo, 1 + 4 * (it + 1))
                pe.wait_ge(s_af, 1 + 32 * (it + 1))
                pe.wait_ge(s_ah, 1 + 32 * (it + 1))
                for g in range(4):
                    c, co = g // 2, slice((g % 2) * P, (g % 2 + 1) * P)
                    for k in range(KT):
                        pe.matmul(bank[:, g, :], wmh[:, k, co], o_h[:, k, px(c)], start=k == 0, stop=False)
                        pe.matmul(bank[:, g, :], wmh[:, k, co], o_l[:, k, px(c)], start=False, stop=False)
                        mm = pe.matmul(bank[:, g, :], wml[:, k, co], o_h[:, k, px(c)], start=False, stop=k == KT - 1)
                    mm.then_inc(s_cm, 1)

            def image(it, l, b, has_next, has_next2):
                qk(it, 0)
                values(it, 0)
                values(it, 1)
                pair(it, 0, (it + 1, 0) if has_next else None, 0, 6)
                qk(it, 1)
                pair(it, 1, (it + 1, 1) if has_next else None, 20, 4)
                if has_next:
                    pe.wait_ge(s_mr, 1 + 32 * (it + 1))
                    conv(it + 1, 2, 0, 54)
                    conv(it + 1, 3, 0, 54)
                out_conv(it)

            layers(pe, start, image)

        @block.scalar
        def _(act):
            def z_raw(i, g):
                act.wait_ge(s_cv, 1 + 4 * i + g + 1)
                act.wait_ge(s_zlo, 1 + 4 * i)
                act.activation(zf[:, g, :], bank[:, 2 + g, :], ACT.Copy).then_inc(s_raw, 1)

            def z_silu(i, g):
                m = g % 2
                if g < 2:
                    act.wait_ge(s_raw, 1 + 2 * i + g + 1)
                    src = zf[:, g, :]
                else:
                    act.wait_ge(s_cv, 1 + 4 * i + g + 1)
                    act.wait_ge(s_zlo, 1 + 4 * i + g - 1)
                    src = bank[:, 2 + g, :]
                act.activation(zf[:, m, :], src, ACT.Silu, scale=coef[:, 0, m:m + 1],
                               bias=coef[:, 1, m:m + 1]).then_inc(s_zf, 1)

            def start(l):
                for i in range(n_piece):
                    act.wait_ge(d_w[i % 2], 1 + 16 * (i // 2 + 1) + 16 * W_SLOT[i % 2] * l)
                    k = span(i)
                    act.activation(w_hi[:, k], res[:, i % 2, 0:k.stop - k.start], ACT.Copy).then_inc(s_whi, 1)
                act.wait_ge(s_coef, 1 + 2 * (l + 1))
                z_raw(l * B, 0)
                z_raw(l * B, 1)
                for g in range(4):
                    z_silu(l * B, g)

            def qk_high(it, p):
                def k_high(h):
                    act.wait_ge(s_kf, 1 + 2 * it + p + 1)
                    act.activation(kk[own(h), h % 2, :], kf[own(h), :], ACT.Copy).then_inc(s_khi, 1)

                def q_high(h):
                    act.wait_ge(s_qk, 1 + 4 * it + 2 * p + 2)
                    act.activation(qq[own(h), h % 2, :], two(0)[own(h)], ACT.Copy).then_inc(s_qhi, 1)

                k_high(2 * p)
                q_high(2 * p)
                q_high(2 * p + 1)
                k_high(2 * p + 1)

            def o_high(it, h):
                act.wait_ge(s_om, 1 + 4 * it + h + 1)
                act.activation(o_h[own(h), h // 2, :], os[own(h), :], ACT.Copy).then_inc(s_ohi, 1)

            def exps(it, h, t):
                T = 32 * it + 8 * h + t
                act.wait_ge(s_lt, 1 + T + 1)
                if t < 2 and h == 0:
                    act.wait_ge(s_al, 1 + 32 * it)
                    act.wait_ge(s_res, 1 + 4 * it)
                    act.wait_ge(s_av, 1 + 32 * it)
                else:
                    act.wait_ge(s_al, 1 + T - 1)
                act.activation(a_f[:, t % 2, :], two(2 * (t % 2)), ACT.Exp, scale=SCALE).then_inc(s_af, 1)
                if not (t < 2 and h == 0):
                    act.wait_ge(s_av, 1 + T - 1)
                act.activation(a_h[:, t % 2, :], two(2 * (t % 2)), ACT.Exp, scale=SCALE).then_inc(s_ah, 1)

            def o_out(it, h):
                act.wait_ge(s_av, 1 + 32 * it + 8 * h + 8)
                act.wait_ge(s_olo, 1 + 4 * it + h)
                act.activation(os[:], two(6), ACT.Copy).then_inc(s_os, 1)

            def image(it, l, b, has_next, has_next2):
                qk_high(it, 0)
                for half in range(2):
                    act.wait_ge(s_v, 1 + 2 * it + half + 1)
                    src = two(6 if half == 0 else 0).rearrange("p (b e s c) -> p b e s c", b=4, e=2, s=2)
                    for e in range(2):
                        ins = act.activation(v_h[:, 4 * half:4 * half + 4, :, 2 * e, :], src[:, :, e, :, :], ACT.Copy)
                    ins.then_inc(s_vhi, 1)
                for p in range(2):
                    if has_next:
                        z_raw(it + 1, p)
                    exps(it, 2 * p, 0)
                    for h in (2 * p, 2 * p + 1):
                        for t in range(8):
                            if t < 7:
                                exps(it, h, t + 1)
                            elif h % 2 == 0:
                                exps(it, h + 1, 0)
                            if h > 0 and t == 6:
                                o_high(it, h - 1)
                        o_out(it, h)
                    if p == 0:
                        qk_high(it, 1)
                if has_next:
                    for g in range(4):
                        z_silu(it + 1, g)
                        if g == 2:
                            o_high(it, 3)
                else:
                    o_high(it, 3)
                for g in range(4):
                    m = g % 2
                    act.wait_ge(s_cm, 1 + 4 * it + g + 1)
                    if g < 2:
                        act.wait_ge(s_al, 1 + 32 * (it + 1))
                    else:
                        act.wait_ge(s_res, 1 + 4 * it + g - 1)
                    act.activation(a_f[:, m, 0:NB], bank[:, g, :], ACT.Silu, scale=coef[:, 0, 2 + m:3 + m],
                                   bias=coef[:, 1, 2 + m:3 + m]).then_inc(s_cf, 1)

            layers(act, start, image)

        @block.vector
        def _(dve):
            def z_low(i, g):
                c, m = g // 2, g % 2
                dve.wait_ge(s_zhi, 1 + 4 * i + g + 1)
                dve.tensor_tensor(z_l[:, m, px(c)], zf[:, m, :], f32(z_h[:, m, px(c)]), ALU.subtract).then_inc(s_zlo, 1)

            def y_low(i):
                for k in range(KT):
                    dve.wait_ge(s_yhi, 1 + KT * i + k + 1)
                    dve.tensor_tensor(yp_l[:, k, 1:1 + W, 1:1 + W], y_in[:, k, :].rearrange("p (r c) -> p r c", c=W),
                                      f32(yp_h[:, k, 1:1 + W, 1:1 + W]), ALU.subtract).then_inc(s_ylo, 1)

            def start(l):
                for i in range(n_piece):
                    dve.wait_ge(s_whi, 1 + n_piece * l + i + 1)
                    k = span(i)
                    dve.tensor_tensor(w_lo[:, k], res[:, i % 2, 0:k.stop - k.start], f32(w_hi[:, k]),
                                      ALU.subtract).then_inc(s_wlo, 1)
                dve.wait_ge(s_cf, 1 + 4 * B * l)
                dve.tensor_copy(coef[:, 0, :], bn_s[:, bass.ds(8 + 4 * l, 4)]).then_inc(s_coef, 1)
                dve.tensor_copy(coef[:, 1, :], bn_o[:, bass.ds(8 + 4 * l, 4)]).then_inc(s_coef, 1)
                y_low(l * B)
                for g in range(4):
                    z_low(l * B, g)

            def qk_out(it, p):
                def q_low(h):
                    dve.wait_ge(s_qhi, 1 + 4 * it + h + 1)
                    dve.tensor_tensor(qm[own(h), h % 2, :], two(0)[own(h)], f32(qq[own(h), h % 2, :]),
                                      ALU.subtract).then_inc(s_qlo, 1)
                dve.wait_ge(s_qk, 1 + 4 * it + 2 * p + 1)
                dve.wait_ge(s_kr, 1 + 2 * it + p + 1)
                dve.tensor_tensor(kf[:], two(2), kf[:], ALU.add).then_inc(s_kf, 1)

                def k_low(h):
                    dve.wait_ge(s_khi, 1 + 4 * it + h + 1)
                    dve.tensor_tensor(kk[other(h), h % 2, :], kf[own(h), :], f32(kk[own(h), h % 2, :]),
                                      ALU.subtract).then_inc(s_klo, 1)

                k_low(2 * p)
                q_low(2 * p)
                q_low(2 * p + 1)
                k_low(2 * p + 1)

            def reduce_block(it, h, n, b0):
                dve.wait_ge(s_mx, 1 + 32 * it + 8 * h + n + 1)
                dve.tensor_reduce(mt[:, h % 2, n:n + 1], two(b0), AX.X, ALU.max, negate=True).then_inc(s_mr, 1)

            def a_low(it, h, t):
                T = 32 * it + 8 * h + t
                dve.wait_ge(s_ah, 1 + T + 1)
                if not (h == 0 and t < 2):
                    dve.wait_ge(s_av, 1 + T - 1)
                else:
                    dve.wait_ge(s_av, 1 + 32 * it)
                dve.tensor_tensor(a_l[:, t % 2, :], a_f[:, t % 2, :], f32(a_h[:, t % 2, :]),
                                  ALU.subtract).then_inc(s_al, 1)

            def o_recip(it, h):
                dve.wait_ge(d_s8, 1 + 16 * (4 * it + h + 1))
                dve.reciprocal(r8i[:], r8[:]).then_inc(s_rc, 1)

            def o_mult(it, h):
                dve.wait_ge(d_rb, 1 + 16 * (4 * it + h + 1))
                dve.tensor_tensor(os[own(h), :], os[own(h), :], rb[own(h), :], ALU.mult).then_inc(s_om, 1)

            def o_low(it, h):
                dve.wait_ge(s_ohi, 1 + 4 * it + h + 1)
                dve.tensor_tensor(o_l[own(h), h // 2, :], os[own(h), :], f32(o_h[own(h), h // 2, :]),
                                  ALU.subtract).then_inc(s_olo, 1)

            for h in range(2):
                dve.memset(f32(qm[other(h), h, :]), 0.0)
                ins = dve.memset(f32(k1[other(h), h, :]), 0.0)
            ins.then_inc(s_const_rows, 1)
            dve.wait_ge(s_const_rows, 2)
            for h in range(2):
                ins = dve.memset(f32(k1[first_other(h), h, :]), 1.0)
            ins.then_inc(s_const_rows, 1)

            def image(it, l, b, has_next, has_next2):
                qk_out(it, 0)
                for half in range(2):
                    dve.wait_ge(s_vhi, 1 + 2 * it + half + 1)
                    src = two(6 if half == 0 else 0).rearrange("p (b e s c) -> p b e s c", b=4, e=2, s=2)
                    for e in range(2):
                        blocks = (slice(None), slice(4 * half, 4 * half + 4), slice(None), 2 * e, slice(None))
                        ins = dve.tensor_tensor(v_l[blocks], src[:, :, e, :, :], f32(v_h[blocks]), ALU.subtract)
                    ins.then_inc(s_vlo, 1)
                if has_next:
                    y_low(it + 1)
                for p in range(2):
                    if p == 1:
                        qk_out(it, 1)
                    for n in range(8):
                        reduce_block(it, 2 * p, n, 4 if n % 2 == 0 else 6)
                    n = 0
                    for h in (2 * p, 2 * p + 1):
                        for t in range(8):
                            a_low(it, h, t)
                            if h % 2 == 0:
                                for _ in range(MAX_AT[t]):
                                    reduce_block(it, h + 1, n, 4)
                                    n += 1
                            if h > 0 and t == 1:
                                o_recip(it, h - 1)
                            if h > 0 and t == 5:
                                o_mult(it, h - 1)
                            if h > 0 and t == 7:
                                o_low(it, h - 1)
                o_recip(it, 3)
                if has_next:
                    z_low(it + 1, 0)
                    z_low(it + 1, 1)
                o_mult(it, 3)
                o_low(it, 3)
                if has_next:
                    z_low(it + 1, 2)
                    z_low(it + 1, 3)

            layers(dve, start, image)

        @block.gpsimd
        def _(pool):
            def copy(dst, src):
                alone(pool, s_spare_pool)
                return pool.tensor_scalar(dst, src, 1.0, None, ALU.mult)

            for t in (yp_h, yp_l):
                pool.memset(f32(t[:]), 0.0)
            pool.memset(f32(v_l[:, :, :, 1, :]), 0.0)
            pool.memset(f32(v_h[:, :, :, 1, :]), 1.0).then_inc(s_const, 1)

            def y_high(i):
                for k in range(KT):
                    pool.wait_ge(d_y[k], 1 + 16 * (i + 1))
                    pool.wait_ge(s_cv, 1 + 4 * i)
                    copy(yp_h[:, k, 1:1 + W, 1:1 + W],
                         y_in[:, k, :].rearrange("p (r c) -> p r c", c=W)).then_inc(s_yhi, 1)

            def z_high(i, g):
                c, m = g // 2, g % 2
                pool.wait_ge(s_zf, 1 + 4 * i + g + 1)
                copy(z_h[:, m, px(c)], zf[:, m, :]).then_inc(s_zhi, 1)

            def k_rel(it, p):
                pool.wait_ge(s_klo, 1 + 4 * it + 2 * p)
                pool.wait_ge(s_om, 1 + 4 * it + p)
                pool.tensor_tensor(kf[:].rearrange("p (r c) -> p r c", c=W),
                                   rhs[:, p, :].unsqueeze(2).to_broadcast([P, W, W]),
                                   rws[:, p, :].unsqueeze(1).to_broadcast([P, W, W]), ALU.add).then_inc(s_kr, 1)

            def start(l):
                pool.wait_ge(s_const, 2)
                pool.wait_ge(d_r, 1 + 32 * (l + 1))
                y_high(l * B)
                for g in range(4):
                    z_high(l * B, g)

            def image(it, l, b, has_next, has_next2):
                k_rel(it, 0)
                if has_next:
                    y_high(it + 1)
                k_rel(it, 1)
                if has_next:
                    for g in range(4):
                        z_high(it + 1, g)
                for g in range(4):
                    pool.wait_ge(s_cf, 1 + 4 * it + g + 1)
                    pool.wait_ge(d_res[g % 2], 1 + 16 * (2 * it + g // 2 + 1))
                    pool.tensor_tensor(res[:, g % 2, :], res[:, g % 2, :], a_f[:, g % 2, 0:NB],
                                       ALU.add).then_inc(s_res, 1)

            layers(pool, start, image)

        @block.sync
        def _(sp):
            def load_y(l, i, b):
                alone(sp, s_spare)
                for k in range(KT):
                    sp.dma_start(y_in[:, k, :], y_d[b, 2 + KT * l + k]).then_inc(d_y[k], 16)

            def start(l):
                for s in range(2):
                    sp.wait_ge(d_out[s], 1 + 32 * B * l)
                alone(sp, s_spare)
                sp.wait_ge(s_kr, 1 + 2 * B * l)
                alone(sp, s_spare)
                sp.dma_start(rws[:], rw[bass.ds(l, 1)].rearrange("o p t c -> (o p) t c")).then_inc(d_r, 16)
                sp.dma_start(rhs[:], rh[bass.ds(l, 1)].rearrange("o p t c -> (o p) t c")).then_inc(d_r, 16)
                sp.wait_ge(s_ylo, 1 + KT * B * l)
                load_y(l, l * B, 0)
                for i in range(n_piece):
                    if i >= 2:
                        sp.wait_ge(s_wlo, 1 + n_piece * l + i - 1)
                    k = span(i)
                    alone(sp, s_spare)
                    sp.dma_start(res[:, i % 2, 0:k.stop - k.start],
                                 w_b[bass.ds(l, 1), :, k].rearrange("o p n -> (o p) n")).then_inc(d_w[i % 2], 16)
                sp.wait_ge(s_ylo, 1 + KT * (B * l + 1))
                load_y(l, l * B + 1, 1)
                sp.wait_ge(s_wlo, 1 + n_piece * (l + 1))
                alone(sp, s_spare)

            def stacks(it, p):
                for h in (2 * p, 2 * p + 1):
                    sp.wait_ge(s_qhi, 1 + 4 * it + h + 1)
                    sp.dma_start(f32(qq[other(h), h % 2, :]), f32(qq[own(h), h % 2, :])).then_inc(d_qq[h % 2], 16)
                for h in (2 * p, 2 * p + 1):
                    sp.wait_ge(s_khi, 1 + 4 * it + h + 1)
                    sp.dma_start(f32(k1[own(h), h % 2, :]), f32(kk[own(h), h % 2, :])).then_inc(d_k1[h % 2], 16)

            def max_row(it, h):
                sp.wait_ge(s_mr, 1 + 32 * it + 8 * h + 8)
                sp.wait_ge(s_qlo, 1 + 4 * it + h + 1)
                sp.dma_start(f32(qm[first_other(h), h % 2, :]).rearrange("o (p c) -> o p c", c=8),
                             f32(mt[:, h % 2, :])).then_inc(d_m[h % 2], 16)

            def sums(it, h):
                sp.wait_ge(s_os, 1 + 4 * it + h + 1)
                sp.dma_start(r8[:], os[first_other(h), :].rearrange("o (p c) -> o p c", c=8)).then_inc(d_s8, 16)

            def recips(it, h):
                sp.wait_ge(s_rc, 1 + 4 * it + h + 1)
                sp.dma_start(rs_d.rearrange("o (p c) -> (o p) c", c=8), r8i[:]).then_inc(d_rc, 16)
                sp.wait_ge(d_rc, 1 + 16 * (4 * it + h + 1))
                sp.dma_start(rb[own(h), :], rs_d.to_broadcast([HD, HW])).then_inc(d_rb, 16)

            def load_res(l, b, g):
                c, m = g // 2, g % 2
                alone(sp, s_spare)
                sp.dma_start(res[:, g % 2, :], y_d[b, 2 + KT * l + m][:, px(c)]).then_inc(d_res[g % 2], 16)

            def image(it, l, b, has_next, has_next2):
                stacks(it, 0)
                max_row(it, 0)
                max_row(it, 1)
                for g in range(2):
                    sp.wait_ge(d_out[g], 1 + 32 * it)
                    load_res(l, b, g)
                sums(it, 0)
                recips(it, 0)
                sums(it, 1)
                stacks(it, 1)
                max_row(it, 2)
                recips(it, 1)
                max_row(it, 3)
                sums(it, 2)
                recips(it, 2)
                if has_next2:
                    sp.wait_ge(s_ylo, 1 + KT * (it + 2))
                    load_y(l, it + 2, b + 2)
                sums(it, 3)
                recips(it, 3)
                for g in range(4):
                    c, m = g // 2, g % 2
                    sp.wait_ge(s_res, 1 + 4 * it + g + 1)
                    alone(sp, s_spare)
                    sp.dma_start(y_d[b, 4 + KT * l + m][:, px(c)], res[:, m, :]).then_inc(d_out[m], 16)
                    if g < 2:
                        sp.wait_ge(d_out[m], 1 + 32 * it + 16)
                        load_res(l, b, g + 2)

            layers(sp, start, image)
            for s in range(2):
                sp.wait_ge(d_out[s], 1 + 32 * B * L)


def phase_d(nc, B, CT, x_v, w_cv2, y_d, x1_d, bank, bn_s, bn_o, x1_mv):
    K8 = 8
    G8 = CT * NC
    with ExitStack() as ctx:
        def sb(name, shape, dt):
            return ctx.enter_context(nc.sbuf_tensor("d_" + name, shape, dt))

        def sem(name):
            sems.append(ctx.enter_context(nc.semaphore("d_" + name)))
            return sems[-1]

        sems = []

        w_hi = sb("w_hi", [P, K8 * 512], F32R)
        w_lo = sb("w_lo", [P, K8 * 512], F32R)
        stage = sb("stage", [P, 2, PIECE], F32)
        YS = 4
        yin = sb("yin", [P, YS, HW], F32)
        yh = sb("yh", [P, 2, K8, HW], F32R)
        yl = sb("yl", [P, 2, K8, HW], F32R)
        sf = sb("sf", [P, 2, NB], F32)
        XS = 4
        xr = sb("xr", [P, XS, NB], F32)
        stats = sb("stats", [P, CT, NC, 6], F32)
        mv = sb("mv", [P, CT, 2], F32)

        d_stage = [sem(f"d_stage{i}") for i in range(2)]
        s_whi, s_wlo = sem("s_whi"), sem("s_wlo")
        s_spare = sem("s_spare")
        d_y = [sem(f"d_y{i}") for i in range(YS)]
        s_yh, s_yl = sem("s_yh"), sem("s_yl")
        s_mm, s_sf, s_x1, s_st, s_ag = sem("s_mm"), sem("s_sf"), sem("s_x1"), sem("s_st"), sem("s_ag")
        s_mv = sem("s_mv")
        d_x = [sem(f"d_x{i}") for i in range(XS)]
        d_o = [sem(f"d_o{i}") for i in range(XS)]
        load_w, hi_w, lo_w, n_piece = split_weights((d_stage, s_whi, s_wlo), w_cv2, stage, w_hi, w_lo, K8 * 512)
        start_at_one(nc, sems)
        block = ctx.enter_context(nc.Block())

        @block.sync
        def _(sp):
            def load_y(n, per, k):
                alone(sp, s_spare)
                sp.dma_start(yin[:, k % YS, :], y_d[n, k]).then_inc(d_y[k % YS], 16)

            def load_x(n, g):
                alone(sp, s_spare)
                sp.dma_start(xr[:, g % XS, :], x_v[n, g // NC][:, (g % NC) * NB:(g % NC + 1) * NB]).then_inc(d_x[g % XS], 16)

            for k in range(YS):
                load_y(0, 0, k)
            load_w(sp)
            for k in range(YS, K8):
                sp.wait_ge(s_yl, 1 + k - YS + 1)
                load_y(0, 1, k)
            for g in range(XS):
                load_x(0, g)

            def image(j, u, left):
                n = 2 * j + u
                for g in range(G8):
                    if left:
                        sp.wait_ge(s_yl, 1 + K8 * (n + 1) + g - YS + 1)
                        load_y(n + 1, 0, g)
                    sp.wait_ge(s_x1, 1 + G8 * n + g + 1)
                    alone(sp, s_spare)
                    sp.dma_start(x1_d[n, g // NC][:, (g % NC) * NB:(g % NC + 1) * NB], xr[:, g % XS, :]).then_inc(d_o[g % XS], 16)
                    if g >= 1 and g - 1 + XS < G8:
                        q = g - 1
                        sp.wait_ge(d_o[q % XS], 1 + 32 * n + 16 * (q // XS + 1))
                        sp.wait_ge(s_st, 1 + G8 * n + q + 1)
                        load_x(n, q + XS)
                    if g >= XS + 1 and left:
                        q = g - 1
                        sp.wait_ge(d_o[q % XS], 1 + 32 * n + 16 * (q // XS + 1))
                        sp.wait_ge(s_st, 1 + G8 * n + q + 1)
                        load_x(n + 1, q - XS)
                if left:
                    q = G8 - 1
                    sp.wait_ge(d_o[q % XS], 1 + 32 * n + 16 * (q // XS + 1))
                    sp.wait_ge(s_st, 1 + G8 * n + q + 1)
                    load_x(n + 1, q - XS)

            images(sp, B, image)
            for i in range(XS):
                sp.wait_ge(d_o[i], 1 + 16 * B * G8 // XS)

        @block.scalar
        def _(act):
            def high(n, u, k):
                act.wait_ge(d_y[k % YS], 1 + 32 * n + 16 * (k // YS + 1))
                act.activation(yh[:, u, k, :], yin[:, k % YS, :], ACT.Copy).then_inc(s_yh, 1)

            for k in range(YS):
                high(0, 0, k)
            hi_w(act)
            for k in range(YS, K8):
                high(0, 0, k)

            def image(j, u, left):
                n = 2 * j + u
                for g in range(G8):
                    m = g // NC
                    act.wait_ge(s_mm, 1 + G8 * n + g + 1)
                    act.wait_ge(s_x1, 1 + G8 * n + max(g - 1, 0))
                    act.activation(sf[:, g % 2, :], bank[:, g % 8, :], ACT.Silu, scale=bn_s[:, 4 + m:5 + m],
                                   bias=bn_o[:, 4 + m:5 + m]).then_inc(s_sf, 1)
                    if left:
                        high(n + 1, 1 - u, g)

            images(act, B, image)

        @block.vector
        def _(dve):
            def low(n, u, k):
                dve.wait_ge(s_yh, 1 + K8 * n + k + 1)
                dve.tensor_tensor(yl[:, u, k, :], yin[:, k % YS, :], f32(yh[:, u, k, :]), ALU.subtract).then_inc(s_yl, 1)

            for k in range(YS):
                low(0, 0, k)
            lo_w(dve)
            for k in range(YS, K8):
                low(0, 0, k)

            def image(j, u, left):
                n = 2 * j + u
                for g in range(G8):
                    if left:
                        low(n + 1, 1 - u, g)
                    dve.wait_ge(s_x1, 1 + G8 * n + g + 1)
                    dve.wait_ge(s_mv, 1 + n)
                    dve.bn_stats(stats[:, g // NC, g % NC, :], xr[:, g % XS, :]).then_inc(s_st, 1)
                dve.wait_ge(s_st, 1 + G8 * (n + 1))
                alone(dve, s_spare)
                for t in range(CT):
                    ins = dve.bn_aggr(mv[:, t, :], stats[:, t, :, :])
                ins.then_inc(s_ag, 1)
                dve.wait_ge(s_ag, 1 + n + 1)
                dve.tensor_copy(x1_mv[:, bass.ds(n, 1), :, :].rearrange("p o t s -> p (o t s)"),
                                mv[:].rearrange("p t s -> p (t s)")).then_inc(s_mv, 1)

            images(dve, B, image)

        @block.gpsimd
        def _(pool):
            def image(j, u, left):
                n = 2 * j + u
                for g in range(G8):
                    pool.wait_ge(s_sf, 1 + G8 * n + g + 1)
                    pool.wait_ge(d_x[g % XS], 1 + 32 * n + 16 * (g // XS + 1))
                    pool.tensor_tensor(xr[:, g % XS, :], xr[:, g % XS, :], sf[:, g % 2, :], ALU.add).then_inc(s_x1, 1)

            images(pool, B, image)

        @block.tensor
        def _(pe):
            pe.wait_ge(s_whi, 1 + n_piece)
            pe.wait_ge(s_wlo, 1 + n_piece)

            def image(j, u, left):
                n = 2 * j + u
                for g in range(G8):
                    m, c = g // NC, g % NC
                    px = slice(c * NB, (c + 1) * NB)
                    pe.wait_ge(s_sf, 1 + G8 * n)
                    for k in range(K8):
                        if g == 0:
                            pe.wait_ge(s_yl, 1 + K8 * n + k + 1)
                        wk = slice(k * 512 + m * P, k * 512 + (m + 1) * P)
                        pe.matmul(bank[:, g, :], w_hi[:, wk], yh[:, u, k, px], start=k == 0, stop=False)
                        pe.matmul(bank[:, g, :], w_hi[:, wk], yl[:, u, k, px], start=False, stop=False)
                        mm = pe.matmul(bank[:, g, :], w_lo[:, wk], yh[:, u, k, px], start=False, stop=k == K8 - 1)
                    mm.then_inc(s_mm, 1)

            images(pe, B, image)


def phase_l(nc, B, CT, w1_rows, w1_t, bn1, x1_d, out_v, bank, group_avg, mhalf, x1_mv):
    N = B * CT
    CIN = 32
    with ExitStack() as ctx:
        def sb(name, shape, dt):
            return ctx.enter_context(nc.sbuf_tensor("l_" + name, shape, dt))

        def sem(name):
            sems.append(ctx.enter_context(nc.semaphore("l_" + name)))
            return sems[-1]

        sems = []

        wr = sb("wr", [P, CT, CIN * TAPS], F32)
        wt = sb("wt", [P, CT, TAPS, CIN], F32)
        wb = sb("wb", [P, CT, TAPS, P], BF16)
        bnp = sb("bnp", [P, 5, CT], F32)
        wst = sb("wst", [P, CT, 6], F32)
        wmv = sb("wmv", [P, CT, 2], F32)
        wab = sb("wab", [P, CT], F32)
        sw = sb("sw", [P, CT], F32)
        t1 = sb("t1", [P, N], F32)
        t2 = sb("t2", [P, N], F32)
        gmean = sb("gmean", [P, B, CT], F32)
        r_g = sb("r_g", [P, B, CT], F32)
        t_g = sb("t_g", [P, B, CT], F32)
        cm = sb("cm", [P, B, CT], F32)
        cv = sb("cv", [P, B, CT], F32)
        m1 = sb("m1", [P, CT], F32)
        v1 = sb("v1", [P, CT], F32)
        i1 = sb("i1", [P, CT], F32)
        a1 = sb("a1", [P, CT], F32)
        sa = sb("sa", [P, B, CT], F32)
        sc = sb("sc", [P, B, CT], F32)
        XB = 2
        xs = sb("xs", [P, XB, CT, HW], F32)
        sg = sb("sg", [P, 2, CT, PW, PW], BF16)
        h = sb("h", [P, CT, B, HW], F16)
        hst = sb("hst", [P, CT, B * NC, 6], F32)
        hmv = sb("hmv", [P, CT, 2], F32)
        a2 = sb("a2", [P, CT], F32)
        b2 = sb("b2", [P, CT], F32)
        u_ = sb("u_", [P, 2, HW], F32)
        p_ = sb("p_", [P, 2, HW], F32)

        d_w, s_c, s_eps, s_rs = sem("d_w"), sem("s_c"), sem("s_eps"), sem("s_rs")
        s_aff, s_gs, s_gm = sem("s_aff"), sem("s_gs"), sem("s_gm")
        s_wz, s_wb = sem("s_wz"), sem("s_wb")
        d_x = [sem(f"d_x{i}") for i in range(XB)]
        s_sg, s_mm, s_h, s_hs = sem("s_sg"), sem("s_mm"), sem("s_h"), sem("s_hs")
        s_spare = sem("s_spare")
        d_z = [sem(f"d_z{i}") for i in range(XB)]
        s_u, s_v, s_q, s_p, s_o = sem("s_u"), sem("s_v"), sem("s_q"), sem("s_p"), sem("s_o")
        s_t2 = sem("s_t2")
        d_o = [sem(f"d_o{i}") for i in range(XB)]
        G8 = CT * NC

        def h_chunk(n, g):
            return h[:, g // NC, bass.ds(n, 1), (g % NC) * NB:(g % NC + 1) * NB].rearrange("p o n -> p (o n)")

        flat = lambda t: t[:].rearrange("p b c -> p (b c)")
        over_b = lambda t: t[:].unsqueeze(1).to_broadcast([P, B, CT])
        start_at_one(nc, sems)
        block = ctx.enter_context(nc.Block())

        @block.sync
        def _(sp):
            sp.dma_start(bnp[:], bn1).then_inc(d_w, 16)
            sp.dma_start(wr[:], w1_rows).then_inc(d_w, 16)
            sp.dma_start(wt[:], w1_t).then_inc(d_w, 16)

            def load(n, u, d):
                alone(sp, s_spare)
                for t in range(CT):
                    sp.dma_start(xs[:, u, t, :], x1_d[n, t]).then_inc(d[u], 16)

            load(0, 0, d_x)
            load(1, 1, d_x)

            def image(j, u, left):
                if left == 2:
                    sp.wait_ge(s_sg, 1 + CT * (2 * j + u + 1))
                    load(2 * j + u + 2, u, d_x)

            images(sp, B, image)
            for u in range(XB):
                sp.wait_ge(s_sg, 1 + CT * (B - XB + u + 1))
                load(u, u, d_z)

            def store(j, u, left):
                n = 2 * j + u
                for t in range(CT):
                    sp.wait_ge(s_o, 1 + CT * n + t + 1)
                    alone(sp, s_spare)
                    sp.dma_start(out_v[n, t], xs[:, u, t, :]).then_inc(d_o[u], 16)
                if left == 2:
                    sp.wait_ge(d_o[u], 1 + 16 * CT * (j + 1))
                    load(n + 2, u, d_z)

            images(sp, B, store)
            for u in range(XB):
                sp.wait_ge(d_o[u], 1 + 16 * CT * B // 2)

        @block.vector
        def _(dve):
            links = [0]

            def link(ins):
                links[0] += 1
                ins.then_inc(s_c, 1)
                dve.wait_ge(s_c, 1 + links[0])

            rsq = [0]

            def rsqrt(dst, src, eps):
                rsq[0] += 1
                dve.tensor_scalar(t1[:, 0:src.free_size()], src, eps, None, ALU.add).then_inc(s_eps, 1)
                dve.wait_ge(s_rs, 1 + rsq[0])
                link(dve.tensor_copy(dst, t2[:, 0:src.free_size()]))

            link(dve.tensor_copy(flat(cm), x1_mv[:, :, :, 0].rearrange("p b c -> p (b c)")))
            dve.tensor_copy(flat(cv), x1_mv[:, :, :, 1].rearrange("p b c -> p (b c)")).then_inc(s_gs, 1)
            dve.wait_ge(s_gm, 2)
            link(dve.tensor_copy(flat(gmean), bank[:, 7, 0:N]))
            link(dve.tensor_tensor(flat(t_g), flat(cm), flat(gmean), ALU.subtract))
            link(dve.tensor_tensor(flat(r_g), flat(t_g), flat(t_g), ALU.mult))
            dve.tensor_tensor(flat(sa), flat(r_g), flat(cv), ALU.add).then_inc(s_gs, 1)
            dve.wait_ge(s_gm, 3)
            rsqrt(flat(r_g), bank[:, 7, 64:64 + N], GN_EPS)
            link(dve.tensor_tensor(flat(cm), flat(t_g), flat(r_g), ALU.mult))
            link(dve.scalar_tensor_tensor(flat(t_g), flat(gmean), -1.0, flat(r_g), ALU.mult, ALU.mult))
            link(dve.tensor_tensor(flat(cv), flat(cv), flat(r_g), ALU.mult))
            link(dve.tensor_tensor(flat(cv), flat(cv), flat(r_g), ALU.mult))
            link(dve.tensor_reduce(m1[:], cm[:].rearrange("p b c -> p c b"), AX.X, ALU.add))
            link(dve.tensor_scalar(m1[:], m1[:], 1.0 / B, None, ALU.mult))
            link(dve.tensor_tensor(cm[:], cm[:], over_b(m1), ALU.subtract))
            link(dve.tensor_tensor(flat(cm), flat(cm), flat(cm), ALU.mult))
            link(dve.tensor_tensor(flat(cm), flat(cm), flat(cv), ALU.add))
            link(dve.tensor_reduce(v1[:], cm[:].rearrange("p b c -> p c b"), AX.X, ALU.add))
            link(dve.tensor_scalar(v1[:], v1[:], 1.0 / B, None, ALU.mult))
            rsqrt(i1[:], v1[:], BN1_EPS)
            dve.wait_ge(d_w, 49)
            link(dve.tensor_tensor(a1[:], i1[:], bnp[:, 0, :], ALU.mult))
            link(dve.tensor_tensor(sa[:], r_g[:], over_b(a1), ALU.mult))
            link(dve.tensor_tensor(sc[:], t_g[:], over_b(m1), ALU.subtract))
            link(dve.tensor_tensor(sc[:], sc[:], over_b(a1), ALU.mult))
            dve.tensor_tensor(sc[:], sc[:], bnp[:, 1:2, :].to_broadcast([P, B, CT]), ALU.add).then_inc(s_aff, 1)

            n_w = CIN * TAPS
            for t in range(CT):
                ins = dve.bn_stats(wst[:, t, :], wr[:, t, :])
            link(ins)
            for t in range(CT):
                ins = dve.bn_aggr(wmv[:, t, :], wst[:, t, :])
            link(ins)
            link(dve.tensor_tensor(wr[:], wr[:], wmv[:, :, 0:1].to_broadcast([P, CT, n_w]), ALU.subtract))
            link(dve.tensor_reduce(wab[:], wr[:], AX.X, ALU.add, apply_absolute_value=True))
            link(dve.tensor_scalar(sw[:], wmv[:, :, 1], float(n_w) / (n_w - 1), None, ALU.mult))
            rsqrt(sw[:], sw[:], 0.0)
            link(dve.tensor_tensor(sw[:], sw[:], wab[:], ALU.mult))
            link(dve.tensor_scalar(sw[:], sw[:], 1.0 / n_w, None, ALU.mult))

            def stats(j, u, left):
                n = 2 * j + u
                for g in range(G8):
                    dve.wait_ge(s_h, 1 + G8 * n + g + 1)
                    dve.bn_stats(hst[:, g // NC, bass.ds(NC * n + g % NC, 1), :].rearrange("p o s -> p (o s)"),
                                 h_chunk(n, g)).then_inc(s_hs, 1)

            images(dve, B, stats)
            dve.wait_ge(s_hs, 1 + G8 * B)
            for t in range(CT):
                ins = dve.bn_aggr(hmv[:, t, :], hst[:, t, :, :])
            link(ins)
            link(dve.tensor_tensor(v1[:], sw[:], sw[:], ALU.mult))
            link(dve.tensor_tensor(v1[:], v1[:], hmv[:, :, 1], ALU.mult))
            rsqrt(i1[:], v1[:], BN1_EPS)
            link(dve.tensor_tensor(a2[:], i1[:], sw[:], ALU.mult))
            link(dve.tensor_tensor(a2[:], a2[:], bnp[:, 2, :], ALU.mult))
            link(dve.tensor_tensor(b2[:], a2[:], hmv[:, :, 0], ALU.mult))
            link(dve.tensor_tensor(b2[:], bnp[:, 3, :], b2[:], ALU.subtract))
            dve.tensor_tensor(t_g[:], t_g[:], over_b(b2), ALU.add).then_inc(s_t2, 1)

            def image(j, u, left):
                n = 2 * j + u
                for t in range(CT):
                    T = CT * n + t
                    ut, pt = u_[:, t % 2, :], p_[:, t % 2, :]
                    dve.wait_ge(s_u, 1 + T + 1)
                    dve.scalar_tensor_tensor(ut, h[:, t, bass.ds(n, 1), :].rearrange("p o n -> p (o n)"),
                                             a2[:, t:t + 1], ut, ALU.mult, ALU.add).then_inc(s_v, 1)
                    dve.wait_ge(s_v, 1 + T + 1)
                    dve.wait_ge(s_o, 1 + CT * n + max(0, t - 1))
                    dve.tensor_scalar(pt, ut, 0.0, bnp[:, 4, t:t + 1], ALU.min, ALU.mult).then_inc(s_q, 1)
                    dve.wait_ge(s_q, 1 + T + 1)
                    dve.scalar_tensor_tensor(pt, ut, 0.0, pt, ALU.max, ALU.add).then_inc(s_p, 1)

            images(dve, B, image)

        @block.gpsimd
        def _(pool):
            pool.memset(wb[:], 0.0).then_inc(s_wz, 1)
            pool.memset(sg[:], 0.0).then_inc(s_wz, 1)
            for k, n in enumerate((N, CT, CT, CT)):
                pool.wait_ge(s_eps, 1 + k + 1)
                pool.tensor_tensor(t2[:, 0:n], t1[:, 0:n], mhalf[:, 0:n], ALU.pow).then_inc(s_rs, 1)

            def image(j, u, left):
                n = 2 * j + u
                for t in range(CT):
                    pool.wait_ge(s_p, 1 + CT * n + t + 1)
                    pool.tensor_tensor(xs[:, u, t, :], xs[:, u, t, :], p_[:, t % 2, :], ALU.add).then_inc(s_o, 1)

            images(pool, B, image)

        @block.scalar
        def _(act):
            act.wait_ge(d_w, 49)
            act.wait_ge(s_wz, 3)
            for g in range(4):
                rows = slice(32 * g, 32 * g + 32)
                act.activation(wb[rows, :, :, 32 * g:32 * g + 32], wt[rows, :, :, :], ACT.Sign).then_inc(s_wb, 1)
            act.wait_ge(s_aff, 2)

            def signs(j, u):
                n = 2 * j + u
                act.wait_ge(d_x[u], 1 + 16 * CT * (j + 1))
                for t in range(CT):
                    act.activation(sg[:, u, t, 1:1 + W, 1:1 + W], xs[:, u, t, :].rearrange("p (r c) -> p r c", c=W),
                                   ACT.Sign, scale=sa[:, bass.ds(n, 1), t], bias=sc[:, bass.ds(n, 1), t]).then_inc(s_sg, 1)

            signs(0, 0)

            def conv_out(j, u, left):
                n = 2 * j + u
                if left:
                    act.wait_ge(s_mm, 1 + G8 * n)
                    signs(j + u, 1 - u)
                for g in range(G8):
                    act.wait_ge(s_mm, 1 + G8 * n + g + 1)
                    act.activation(h_chunk(n, g), bank[:, g, :], ACT.Copy).then_inc(s_h, 1)

            images(act, B, conv_out)
            act.wait_ge(s_t2, 2)

            def image(j, u, left):
                n = 2 * j + u
                act.wait_ge(d_z[u], 1 + 16 * CT * (j + 1))
                for t in range(CT):
                    act.wait_ge(s_p, 1 + CT * n + max(0, t - 1))
                    act.activation(u_[:, t % 2, :], xs[:, u, t, :], ACT.Identity, scale=r_g[:, bass.ds(n, 1), t],
                                   bias=t_g[:, bass.ds(n, 1), t]).then_inc(s_u, 1)

            images(act, B, image)

        @block.tensor
        def _(pe):
            pe.wait_ge(s_gs, 2)
            pe.matmul(bank[:, 7, 0:N], group_avg[:], flat(cm), start=True, stop=True).then_inc(s_gm, 1)
            pe.wait_ge(s_gs, 3)
            pe.matmul(bank[:, 7, 64:64 + N], group_avg[:], flat(sa), start=True, stop=True).then_inc(s_gm, 1)
            pe.wait_ge(s_wb, 5)
            pe.wait_ge(s_eps, 2)

            def image(j, u, left):
                n = 2 * j + u
                for g in range(G8):
                    t, c = g // NC, g % NC
                    pe.wait_ge(s_h, 1 + G8 * n)
                    pe.wait_ge(s_sg, 1 + CT * n + t + 1)
                    for k in range(TAPS):
                        dy, dx = k // 3, k % 3
                        mm = pe.matmul(bank[:, g, :].rearrange("p (r c) -> p r c", c=W), wb[:, t, k, :],
                                       sg[:, u, t, dy + ROWS * c:dy + ROWS * (c + 1), dx:dx + W],
                                       start=k == 0, stop=k == TAPS - 1)
                    mm.then_inc(s_mm, 1)

            images(pe, B, image)


def kernel(x, L0_conv_cv1_w, L0_conv_cv1_bn, L0_conv_cv2_w, L0_conv_cv2_bn, L0_conv_m_cv1_w, L0_conv_m_cv1_bn,
           L0_conv_m_qkv_w, L0_conv_m_rw, L0_conv_m_rh, L0_conv_m_cv2_w, L0_conv_m_cv2_bn, L1_conv_conv_w,
           L1_conv_bn1_gamma, L1_conv_bn1_beta, L1_conv_bn2_gamma, L1_conv_bn2_beta, L1_conv_prelu_a):
    import numpy as np
    import concourse.bacc as bacc
    from concourse.bass_utils import run_bass_kernel_spmd as run

    x = np.ascontiguousarray(x)
    shape = x.shape
    B, C = shape[0], shape[1]

    def cols(a):
        a = np.asarray(a)
        return np.moveaxis(a.reshape(a.shape[:-1] + (-1, P)), -1, 0)

    def conv_t(w):
        w = np.asarray(w)
        o, i = w.shape[:2]
        w = w.reshape(o, i // P, P, -1)
        return w.transpose(2, 1, 3, 0).reshape(P, -1)

    cv1_bn, cv2_bn = cols(L0_conv_cv1_bn), cols(L0_conv_cv2_bn)
    m1_bn, m2_bn = cols(L0_conv_m_cv1_bn), cols(L0_conv_m_cv2_bn)
    bn0 = np.concatenate([cv1_bn, cv2_bn] + [q[:, l] for l in range(2) for q in (m1_bn, m2_bn)], axis=2)
    qkv = np.asarray(L0_conv_m_qkv_w).reshape(2, 12, HD, 256)
    qkv = qkv[:, [0, 1, 2, 3, 4, 5, 6, 7, 8, 10, 9, 11]].reshape(2, 768, 256)
    w3 = np.asarray(L0_conv_m_cv1_w)
    wm = np.asarray(L0_conv_m_cv2_w)
    w_b = np.stack([np.concatenate([conv_t(w3[l].reshape(256, 256, 9)), conv_t(qkv[l]), conv_t(wm[l])], axis=1)
                    for l in range(2)])

    def rel(r):
        r = np.asarray(r).reshape(2, 2, P, W)
        return r.transpose(0, 2, 1, 3)

    w1 = np.asarray(L1_conv_conv_w).reshape(C // P, P, 32, 9)
    w1_rows = w1.reshape(C // P, P, 288).transpose(1, 0, 2)
    w1_t = w1.reshape(C // P, 4, 32, 32, 9).transpose(1, 3, 0, 4, 2).reshape(P, C // P, 9, 32)
    bn1 = np.stack([cols(v) for v in (L1_conv_bn1_gamma, L1_conv_bn1_beta, L1_conv_bn2_gamma, L1_conv_bn2_beta,
                                      L1_conv_prelu_a)], axis=1)
    data = {
        "x": x.reshape(B, C, HW), "w_cv1": conv_t(L0_conv_cv1_w), "w_b": w_b, "w_cv2": conv_t(L0_conv_cv2_w),
        "bn0": bn0, "rw": rel(L0_conv_m_rw), "rh": rel(L0_conv_m_rh), "w1_rows": w1_rows, "w1_t": w1_t, "bn1": bn1,
    }
    data = {k: np.ascontiguousarray(v) for k, v in data.items()}
    nc = bacc.Bacc("TRN2", target_bir_lowering=False, num_devices=1)
    args = [nc.dram_tensor(k, v.shape, mybir.dt.from_np(v.dtype), kind="ExternalInput").ap() for k, v in data.items()]
    out = nc.dram_tensor("out", (B, C, HW), F32, kind="ExternalOutput").ap()
    program(nc, *args, out)
    result = run(nc, [data], core_ids=[0])
    return result.results[0]["out"].reshape(shape)
```

```python
from contextlib import ExitStack

import concourse.bass as bass
from concourse import mybir

P = 128
F32 = mybir.dt.float32
F32R = mybir.dt.float32r
F16 = mybir.dt.float16
BF16 = mybir.dt.bfloat16
ACT = mybir.ActivationFunctionType
ALU = mybir.AluOpType
AX = mybir.AxisListType

HW, W = 1024, 32
NB = 512
NC = HW // NB
ROWS = NB // W
PW = W + 2
HEADS, HD = 4, 64
SCALE = float(HD) ** -0.5
BN0_EPS, GN_EPS, BN1_EPS = 1e-3, 1e-5, 1e-5
TAPS = 9
KT = 2
W3N, WQN, WMN = KT * TAPS * 256, KT * 768, KT * 256
WBN = W3N + WQN + WMN
PIECE = 512
LEAD, STEP = [20, 24], [3, 3]


def f32(ap):
    return ap.bitcast(F32)


def start_at_one(nc, sems):
    with nc.Block() as block:
        for k, engine in enumerate((block.sync, block.gpsimd, block.scalar, block.vector, block.tensor)):
            @engine
            def _(eng, k=k):
                for s in sems[k::5]:
                    eng.sem_inc(s, 1)


def alone(eng, sem):
    eng.sem_inc(sem, 1)


def images(eng, n_img, body):
    if n_img > 2:
        with eng.Fori(0, n_img // 2 - 1) as j:
            body(j, 0, 2)
            body(j, 1, 2)
    body(n_img // 2 - 1, 0, 1)
    body(n_img // 2 - 1, 1, 0)


class Split:

    def __init__(self, d_stage, s_hi, s_lo, stage):
        self.d_stage, self.s_hi, self.s_lo, self.stage = d_stage, s_hi, s_lo, stage
        self.pieces = []

    def add(self, dram, w_hi, w_lo, lo, hi):
        first = len(self.pieces)
        for a in range(lo, hi, PIECE):
            b = min(hi, a + PIECE)
            self.pieces.append((dram[:, a:b], w_hi[:, a:b], w_lo[:, a:b], b - a))
        return range(first, len(self.pieces))

    def load(self, queue, i):
        src, _, _, n = self.pieces[i]
        if i >= 2:
            queue.wait_ge(self.s_lo, 1 + i - 1)
        queue.dma_start(self.stage[:, i % 2, 0:n], src).then_inc(self.d_stage[i % 2], 16)

    def high(self, act, i):
        _, w_hi, _, n = self.pieces[i]
        act.wait_ge(self.d_stage[i % 2], 1 + 16 * (i // 2 + 1))
        act.activation(w_hi, self.stage[:, i % 2, 0:n], ACT.Copy).then_inc(self.s_hi, 1)

    def low(self, dve, i):
        _, w_hi, w_lo, n = self.pieces[i]
        dve.wait_ge(self.s_hi, 1 + i + 1)
        dve.tensor_tensor(w_lo, self.stage[:, i % 2, 0:n], f32(w_hi), ALU.subtract).then_inc(self.s_lo, 1)


def program(nc, x, w_cv1, w_b, bn0, rw, rh, w1_rows, w1_t, bn1, out):
    B = x.shape[0]
    CT = x.shape[1] // P
    x_v = x.rearrange("b (t p) n -> b t p n", p=P)
    out_v = out.rearrange("b (t p) n -> b t p n", p=P)
    y_d = nc.dram_tensor("y_d", (B, 8, P, HW), F32, kind="Internal").ap()
    x1_d = nc.dram_tensor("x1_d", (B, CT, P, HW), F32, kind="Internal").ap()
    rs_d = nc.dram_tensor("rs_d", (1, HW), F32, kind="Internal").ap()

    with ExitStack() as top:
        def keep(name, shape, dt):
            return top.enter_context(nc.sbuf_tensor(name, shape, dt))

        bank = top.enter_context(nc.psum_tensor("bank", [P, 8, NB], F32))
        bn_s = keep("bn_s", [P, 16], F32)
        bn_o = keep("bn_o", [P, 16], F32)
        group_avg = keep("group_avg", [P, P], F32)
        mhalf = keep("mhalf", [P, 4 * B], F32)
        x1_mv = keep("x1_mv", [P, B, CT, 2], F32)

        weights = ExitStack()
        w_hi = weights.enter_context(nc.sbuf_tensor("w_hi", [P, WBN], F32R))
        w_lo = weights.enter_context(nc.sbuf_tensor("w_lo", [P, WBN], F32R))
        sems = []

        def sem(name):
            sems.append(top.enter_context(nc.semaphore(name)))
            return sems[-1]

        layer0 = [
            phase_a(nc, sem, B, CT, x_v, w_cv1, w_b, w_hi, w_lo, bn0, y_d, bank, bn_s, bn_o, group_avg, mhalf),
            phase_b(nc, sem, B, w_b, w_hi, w_lo, rw, rh, y_d, rs_d, bank, bn_s, bn_o),
            phase_d(nc, sem, B, CT, x_v, w_hi, w_lo, y_d, x1_d, bank, bn_s, bn_o, x1_mv),
        ]
        layer1 = phase_l(nc, sem, B, CT, w1_rows, w1_t, bn1, x1_d, out_v, bank, group_avg, mhalf, x1_mv)
        for phase in layer0 + [layer1]:
            next(phase)
        start_at_one(nc, sems)
        with weights:
            for phase in layer0:
                next(phase, None)
        next(layer1, None)


def phase_a(nc, sem_, B, CT, x_v, w_cv1, w_b, wb_hi, wb_lo, bn0, y_d, bank, bn_s, bn_o, group_avg, mhalf):
    def sem(name):
        return sem_("a_" + name)

    d_bn = sem("d_bn")
    s_spare = sem("s_spare")
    d_stage = [sem(f"d_stage{i}") for i in range(2)]
    s_whi, s_wlo = sem("s_whi"), sem("s_wlo")
    d_x = [sem(f"d_x{i}") for i in range(2)]
    s_chain = sem("s_chain")
    s_setup = sem("s_setup")
    s_eps, s_rs = sem("s_eps"), sem("s_rs")
    s_mv, s_gm, s_dev, s_gv = sem("s_mv"), sem("s_gm"), sem("s_dev"), sem("s_gv")
    s_xf, s_xh, s_xl = sem("s_xf"), sem("s_xh"), sem("s_xl")
    s_mm, s_y = sem("s_mm"), sem("s_y")
    d_y = [sem(f"d_y{i}") for i in range(4)]
    yield

    with ExitStack() as ctx:
        def sb(name, shape, dt):
            return ctx.enter_context(nc.sbuf_tensor("a_" + name, shape, dt))

        w_hi = sb("w_hi", [P, CT * 512], F32R)
        w_lo = sb("w_lo", [P, CT * 512], F32R)
        stage = sb("stage", [P, 2, PIECE], F32)
        bn_in = sb("bn_in", [P, 4, 16], F32)
        bn_t = sb("bn_t", [P, 2, 16], F32)
        xin = sb("xin", [P, 2, CT, HW], F32)
        xh = sb("xh", [P, 2, CT, HW], F32R)
        xl = sb("xl", [P, 2, CT, HW], F32R)
        stats = sb("stats", [P, CT, NC, 6], F32)
        mv = sb("mv", [P, CT, 2], F32)
        dev = sb("dev", [P, CT], F32)
        gm = sb("gm", [P, CT], F32)
        var = sb("var", [P, CT], F32)
        rg = sb("rg", [P, CT], F32)
        sh = sb("sh", [P, CT], F32)
        y_sb = sb("y_sb", [P, 4, NB], F32)

        G8 = CT * NC
        SLOTS = 4
        stat_bank = 7
        split = Split(d_stage, s_whi, s_wlo, stage)
        own = split.add(w_cv1, w_hi, w_lo, 0, CT * 512)
        ahead = split.add(w_b[0], wb_hi, wb_lo, 0, W3N)

        LATE = 2

        def piece_at(left, g, late=0):
            k = (1 - left) * G8 + g - (2 * G8 - len(ahead) - LATE) - late
            return ahead[k] if left < 2 and 0 <= k < len(ahead) else None

        block = ctx.enter_context(nc.Block())

        @block.sync
        def _(sp):
            sp.dma_start(bn_in[:], bn0).then_inc(d_bn, 16)
            for t in range(CT):
                sp.dma_start(xin[:, 0, t, :], x_v[0, t]).then_inc(d_x[0], 16)
            for i in own:
                split.load(sp, i)
            for t in range(CT):
                sp.dma_start(xin[:, 1, t, :], x_v[1, t]).then_inc(d_x[1], 16)

            def image(j, u, left):
                n = 2 * j + u
                if left == 2:
                    sp.wait_ge(s_xl, 1 + CT * (n + 1))
                    alone(sp, s_spare)
                    for t in range(CT):
                        sp.dma_start(xin[:, u, t, :], x_v[n + 2, t]).then_inc(d_x[u], 16)
                for g in range(G8):
                    sp.wait_ge(s_y, 1 + SLOTS + G8 * n + g + 1)
                    alone(sp, s_spare)
                    sp.dma_start(y_d[n, g // NC][:, (g % NC) * NB:(g % NC + 1) * NB],
                                 y_sb[:, g % SLOTS, :]).then_inc(d_y[g % SLOTS], 16)
                    if piece_at(left, g) is not None:
                        split.load(sp, piece_at(left, g))

            images(sp, B, image)
            for i in range(SLOTS):
                sp.wait_ge(d_y[i], 1 + 16 * B * G8 // SLOTS)

        @block.gpsimd
        def _(pool):
            pool.memset(mhalf[:], -0.5).then_inc(s_setup, 1)
            pool.memset(group_avg[:], 1.0 / 16).then_inc(s_setup, 1)
            pool.wait_ge(s_setup, 3)
            g3 = group_avg[:].rearrange("p (g c) -> p g c", c=16)
            pool.affine_select(out=g3, in_=g3, compare_op=ALU.is_ge, fill=0.0, base=0,
                               pattern=[[-16, 8], [0, 16]], channel_multiplier=1).then_inc(s_setup, 1)
            pool.wait_ge(s_setup, 4)
            pool.affine_select(out=g3, in_=g3, compare_op=ALU.is_ge, fill=0.0, base=15,
                               pattern=[[16, 8], [0, 16]], channel_multiplier=-1).then_inc(s_setup, 1)
            pool.wait_ge(s_eps, 2)
            pool.tensor_tensor(bn_t[:, 1, :], bn_t[:, 0, :], mhalf[:, 0:16] if 4 * B >= 16 else mhalf[:, 0:1].to_broadcast([P, 16]),
                               ALU.pow).then_inc(s_rs, 1)

            def stat(n):
                pool.wait_ge(s_eps, 1 + n + 2)
                pool.wait_ge(s_xf, 1 + CT * n)
                pool.tensor_tensor(rg[:], var[:], mhalf[:, 0:CT], ALU.pow).then_inc(s_rs, 1)

            stat(0)
            images(pool, B, lambda j, u, left: stat(2 * j + u + 1) if left else None)

        @block.vector
        def _(dve):
            links = [0]

            def link(ins):
                links[0] += 1
                ins.then_inc(s_chain, 1)
                dve.wait_ge(s_chain, 1 + links[0])

            dve.wait_ge(d_bn, 17)
            dve.tensor_scalar(bn_t[:, 0, :], bn_in[:, 3, :], BN0_EPS, None, ALU.add).then_inc(s_eps, 1)
            dve.wait_ge(s_rs, 2)
            link(dve.tensor_tensor(bn_s[:], bn_in[:, 0, :], bn_t[:, 1, :], ALU.mult))
            link(dve.tensor_tensor(bn_t[:, 0, :], bn_in[:, 2, :], bn_s[:], ALU.mult))
            link(dve.tensor_tensor(bn_o[:], bn_in[:, 1, :], bn_t[:, 0, :], ALU.subtract))
            LINKS = 4
            base = links[0]

            def statistics(n, pairs, u, early=(), late=()):
                dve.wait_ge(d_x[u], 1 + 16 * CT * pairs)
                c = base + LINKS * n
                for t in range(CT):
                    for k in range(NC):
                        ins = dve.bn_stats(stats[:, t, k, :], xin[:, u, t, k * NB:(k + 1) * NB])
                ins.then_inc(s_chain, 1)
                dve.wait_ge(s_chain, 1 + c + 1)
                alone(dve, s_spare)
                for t in range(CT):
                    ins = dve.bn_aggr(mv[:, t, :], stats[:, t, :, :])
                ins.then_inc(s_mv, 1)
                for i in early:
                    split.low(dve, i)
                dve.wait_ge(s_gm, 1 + n + 1)
                dve.tensor_copy(gm[:], bank[:, stat_bank, 0:CT]).then_inc(s_chain, 1)
                dve.wait_ge(s_chain, 1 + c + 2)
                dve.tensor_tensor(dev[:], mv[:, :, 0], gm[:], ALU.subtract).then_inc(s_chain, 1)
                dve.wait_ge(s_chain, 1 + c + 3)
                dve.tensor_tensor(sh[:], dev[:], dev[:], ALU.mult).then_inc(s_chain, 1)
                dve.wait_ge(s_chain, 1 + c + 4)
                dve.tensor_tensor(dev[:], mv[:, :, 1], sh[:], ALU.add).then_inc(s_dev, 1)
                dve.wait_ge(s_gv, 1 + n + 1)
                dve.tensor_scalar(var[:], bank[:, stat_bank, 8:8 + CT], GN_EPS, None, ALU.add).then_inc(s_eps, 1)
                dve.wait_ge(s_rs, 1 + n + 2)
                for t in range(CT):
                    dve.tensor_scalar(xin[:, u, t, :], xin[:, u, t, :], gm[:, t:t + 1], rg[:, t:t + 1],
                                      ALU.subtract, ALU.mult).then_inc(s_xf, 1)
                for t in range(CT):
                    dve.wait_ge(s_xh, 1 + CT * n + t + 1)
                    dve.tensor_tensor(xl[:, u, t, :], xin[:, u, t, :], f32(xh[:, u, t, :]),
                                      ALU.subtract).then_inc(s_xl, 1)
                    if t < len(late):
                        split.low(dve, late[t])

            statistics(0, 1, 0, early=own[:2], late=own[2:])
            images(dve, B, lambda j, u, left: statistics(2 * j + u + 1, j + u + 1, 1 - u) if left else None)
            for i in ahead:
                split.low(dve, i)

        @block.scalar
        def _(act):
            def high(n, u, late=()):
                for t in range(CT):
                    act.wait_ge(s_xf, 1 + CT * n + t + 1)
                    act.activation(xh[:, u, t, :], xin[:, u, t, :], ACT.Copy).then_inc(s_xh, 1)
                    if t < len(late):
                        split.high(act, late[t])

            def group(n, j, u, g):
                m = g // NC
                act.wait_ge(s_mm, 1 + G8 * n + g + 1)
                act.wait_ge(d_y[g % SLOTS], 1 + 32 * n + 16 * (g // SLOTS))
                act.activation(y_sb[:, g % SLOTS, :], bank[:, g % SLOTS, :], ACT.Silu, scale=bn_s[:, m:m + 1],
                               bias=bn_o[:, m:m + 1]).then_inc(s_y, 1)

            act.sem_inc(s_y, SLOTS)
            for i in own[:2]:
                split.high(act, i)
            high(0, 0, own[2:])
            act.wait_ge(s_chain, 4)

            def image(j, u, left):
                n = 2 * j + u
                for g in range(G8):
                    group(n, j, u, g)
                    if piece_at(left, g, LATE) is not None:
                        split.high(act, piece_at(left, g, LATE))
                    if g == 2 and left:
                        act.wait_ge(s_mm, 1 + G8 * n)
                        high(n + 1, 1 - u)

            images(act, B, image)

        @block.tensor
        def _(pe):
            def mean(n):
                pe.wait_ge(s_mv, 1 + n + 1)
                pe.matmul(bank[:, stat_bank, 0:CT], group_avg[:], mv[:, :, 0], start=True, stop=True).then_inc(s_gm, 1)

            def variance(n):
                pe.wait_ge(s_dev, 1 + n + 1)
                pe.matmul(bank[:, stat_bank, 8:8 + CT], group_avg[:], dev[:], start=True, stop=True).then_inc(s_gv, 1)

            def group(n, u, g):
                m, c = g // NC, g % NC
                pe.wait_ge(s_y, 1 + G8 * n + g + 1)
                px = slice(c * NB, (c + 1) * NB)
                ps = bank[:, g % SLOTS, :]
                for k in range(CT):
                    wk = slice(k * 512 + m * P, k * 512 + (m + 1) * P)
                    if g == 0:
                        pe.wait_ge(s_xl, 1 + CT * n + k + 1)
                        pe.wait_ge(s_wlo, 1 + own[k] + 1)
                    pe.matmul(ps, w_hi[:, wk], xh[:, u, k, px], start=k == 0, stop=False)
                    pe.matmul(ps, w_hi[:, wk], xl[:, u, k, px], start=False, stop=False)
                    mm = pe.matmul(ps, w_lo[:, wk], xh[:, u, k, px], start=False, stop=k == CT - 1)
                mm.then_inc(s_mm, 1)

            pe.wait_ge(s_setup, 5)
            mean(0)
            variance(0)
            def image(j, u, left):
                n = 2 * j + u
                for g in range(G8):
                    group(n, u, g)
                    if left and g == 1:
                        mean(n + 1)
                    if left and g == 3:
                        variance(n + 1)

            images(pe, B, image)


def phase_b(nc, sem_, B, w_b, w_hi, w_lo, rw, rh, y_d, rs_d, bank, bn_s, bn_o):
    L = w_b.shape[0] - 1

    def sem(name):
        return sem_("b_" + name)

    def sem2(name):
        return [sem(name + "0"), sem(name + "1")]

    s_table = sem("s_table")
    d_w = sem2("d_w")
    s_whi, s_wlo = sem("s_whi"), sem("s_wlo")
    s_coef, d_r = sem("s_coef"), sem("d_r")
    s_const, s_const_rows = sem("s_const"), sem("s_const_rows")
    s_spare, s_spare_pool, s_spare_pe = sem("s_spare"), sem("s_spare_pool"), sem("s_spare_pe")
    d_y = sem2("d_y")
    s_yhi, s_ylo = sem("s_yhi"), sem("s_ylo")
    s_cv, s_raw, s_zf, s_zhi, s_zlo = sem("s_cv"), sem("s_raw"), sem("s_zf"), sem("s_zhi"), sem("s_zlo")
    s_qk, s_v = sem("s_qk"), sem("s_v")
    s_qhi, s_qlo = sem("s_qhi"), sem("s_qlo")
    s_kr, s_kf, s_khi, s_klo = sem("s_kr"), sem("s_kf"), sem("s_khi"), sem("s_klo")
    d_qq, d_k1, d_m = sem2("d_qq"), sem2("d_k1"), sem2("d_m")
    s_vhi, s_vlo = sem("s_vhi"), sem("s_vlo")
    s_mx, s_mr = sem("s_mx"), sem("s_mr")
    s_lt, s_af, s_ah, s_al = sem("s_lt"), sem("s_af"), sem("s_ah"), sem("s_al")
    s_avh, s_avl = sem("s_avh"), sem("s_avl")
    s_os, d_s8, s_rc, d_rc, d_rb = sem("s_os"), sem("d_s8"), sem("s_rc"), sem("d_rc"), sem("d_rb")
    s_om, s_ohi, s_olo = sem("s_om"), sem("s_ohi"), sem("s_olo")
    s_cm, s_cf = sem("s_cm"), sem("s_cf")
    d_res, s_res, d_out = sem2("d_res"), sem("s_res"), sem2("d_out")
    yield

    with ExitStack() as ctx:
        def sb(name, shape, dt):
            return ctx.enter_context(nc.sbuf_tensor("b_" + name, shape, dt))

        coef = sb("coef", [P, 2, 4], F32)
        rws = sb("rws", [P, 2, W], F32)
        rhs = sb("rhs", [P, 2, W], F32)
        y_in = sb("y_in", [P, KT, HW], F32)
        yp_h = sb("yp_h", [P, KT, PW, PW], F32R)
        yp_l = sb("yp_l", [P, KT, PW, PW], F32R)
        z_h = sb("z_h", [P, KT, HW], F32R)
        z_l = sb("z_l", [P, KT, HW], F32R)
        zf = sb("zf", [P, 2, NB], F32)
        kf = sb("kf", [P, HW], F32)
        qq = sb("qq", [P, 2, HW], F32R)
        qm = sb("qm", [P, 2, HW], F32R)
        kk = sb("kk", [P, 2, HW], F32R)
        k1 = sb("k1", [P, 2, HW], F32R)
        v_h = sb("v_h", [P, 8, 2, 3, HD], F32R)
        v_l = sb("v_l", [P, 8, 2, 3, HD], F32R)
        a_f = sb("a_f", [P, 2, HW], F32)
        a_h = sb("a_h", [P, 2, HW], F32R)
        a_l = sb("a_l", [P, 2, HW], F32R)
        mt = sb("mt", [P, 2, 8], F32R)
        os = sb("os", [P, HW], F32)
        r8 = sb("r8", [P, 8], F32)
        r8i = sb("r8i", [P, 8], F32)
        rb = kf
        o_h = sb("o_h", [P, KT, HW], F32R)
        o_l = sb("o_l", [P, KT, HW], F32R)
        res = sb("res", [P, 2, NB], F32)

        zero = sb("zero", [P, 2], F32)

        N_OWN, N_NEXT = (WBN - W3N) // PIECE, W3N // PIECE
        N_ALL = N_OWN + N_NEXT
        w3 = lambda w: w[:, 0:W3N].rearrange("p (k t c) -> p k t c", k=KT, t=TAPS)
        wq = lambda w: w[:, W3N:W3N + WQN].rearrange("p (k c) -> p k c", k=KT)
        wm = lambda w: w[:, W3N + WQN:WBN].rearrange("p (k c) -> p k c", k=KT)
        w3h, w3l, wqh, wql, wmh, wml = w3(w_hi), w3(w_lo), wq(w_hi), wq(w_lo), wm(w_hi), wm(w_lo)

        W_SLOT = [N_ALL - N_ALL // 2, N_ALL // 2]

        def piece(i):
            if i < N_OWN:
                return slice(W3N + i * PIECE, W3N + (i + 1) * PIECE), res[:, i % 2, :]
            return slice((i - N_OWN) * PIECE, (i - N_OWN + 1) * PIECE), y_in[:, i % 2, 0:PIECE]

        NEXT_AT = {(1, 2): 4, (1, 3): 5, (1, 4): 6, (1, 5): 7, (1, 6): 8, (3, 2): 9, (3, 3): 10, (3, 4): 11, (3, 5): 12}
        assert sorted(NEXT_AT.values()) == list(range(N_OWN, N_ALL))

        def load_piece(sp, l, l_w, i):
            cols, stage = piece(i)
            if i >= 2:
                sp.wait_ge(s_wlo, 1 + N_ALL * l + i - 1)
            alone(sp, s_spare)
            sp.dma_start(stage, w_b[bass.ds(l_w, 1), :, cols].rearrange("o p n -> (o p) n")).then_inc(d_w[i % 2], 16)

        def piece_high(act, l, i):
            cols, stage = piece(i)
            act.wait_ge(d_w[i % 2], 1 + 16 * (i // 2 + 1) + 16 * W_SLOT[i % 2] * l)
            act.activation(w_hi[:, cols], stage, ACT.Copy).then_inc(s_whi, 1)

        def piece_low(dve, l, i):
            cols, stage = piece(i)
            dve.wait_ge(s_whi, 1 + N_ALL * l + i + 1)
            dve.tensor_tensor(w_lo[:, cols], stage, f32(w_hi[:, cols]), ALU.subtract).then_inc(s_wlo, 1)

        def own(h):
            return slice(HD * (h % 2), HD * (h % 2) + HD)

        def other(h):
            return own(h + 1)

        def first_other(h):
            return slice(HD * (1 - h % 2), HD * (1 - h % 2) + 1)

        def px(c):
            return slice(c * NB, (c + 1) * NB)

        def two(b0):
            return bank[:, b0:b0 + 2, :].rearrange("p a n -> p (a n)")

        def layers(eng, start, image):
            with eng.Fori(0, L) as l:
                start(l)
                if B > 2:
                    with eng.Fori(0, B - 2) as b:
                        image(l * B + b, l, b, True, True)
                image(l * B + B - 2, l, B - 2, True, False)
                image(l * B + B - 1, l, B - 1, False, False)

        block = ctx.enter_context(nc.Block())

        @block.tensor
        def _(pe):
            CONV_BANK = [2, 3, 4, 5]

            def conv_terms(g):
                c, m = g // 2, g % 2
                co = slice(m * P, (m + 1) * P)
                terms = []
                for k in range(KT):
                    for t in range(TAPS):
                        dy, dx = t // 3, t % 3
                        win = (slice(None), k, slice(dy + ROWS * c, dy + ROWS * (c + 1)), slice(dx, dx + W))
                        terms += [(w3h[:, k, t, co], yp_h[win]), (w3h[:, k, t, co], yp_l[win]),
                                  (w3l[:, k, t, co], yp_h[win])]
                return terms

            def conv(i, g, lo, hi):
                terms = conv_terms(g)
                ps = bank[:, CONV_BANK[g], :].rearrange("p (r c) -> p r c", c=W)
                if lo == 0:
                    pe.wait_ge(s_yhi, 1 + KT * (i + 1))
                    pe.wait_ge(s_ylo, 1 + KT * (i + 1))
                for n in range(lo, min(hi, len(terms))):
                    mm = pe.matmul(ps, terms[n][0], terms[n][1], start=n == 0, stop=n == len(terms) - 1)
                if lo < len(terms) <= hi:
                    mm.then_inc(s_cv, 1)

            def start(l):
                pe.wait_ge(s_whi, 1 + N_ALL * l)
                pe.wait_ge(s_wlo, 1 + N_ALL * l)
                pe.wait_ge(s_cf, 1 + 4 * B * l)
                pe.wait_ge(s_mr, 1 + 32 * B * l)
                for g in range(4):
                    conv(l * B, g, 0, 54)
                pe.wait_ge(s_const, 3)
                pe.wait_ge(s_const_rows, 3)
                pe.wait_ge(s_whi, 1 + N_ALL * l + N_OWN)
                pe.wait_ge(s_wlo, 1 + N_ALL * l + N_OWN)
                alone(pe, s_spare_pe)

            def qk(it, p, part, c):
                if c == 0 and p == 0:
                    pe.wait_ge(s_cf, 1 + 4 * it)
                elif c == 0:
                    pe.wait_ge(s_af, 1 + 32 * it + 15 + part)
                    pe.wait_ge(s_ah, 1 + 32 * it + 15 + part)
                co = slice(part * 256 + p * P, part * 256 + (p + 1) * P)
                ps = bank[:, 2 * part + c, :]
                for k in range(KT):
                    pe.matmul(ps, wqh[:, k, co], z_h[:, k, px(c)], start=k == 0, stop=False)
                    pe.matmul(ps, wqh[:, k, co], z_l[:, k, px(c)], start=False, stop=False)
                    mm = pe.matmul(ps, wql[:, k, co], z_h[:, k, px(c)], start=False, stop=k == KT - 1)
                if c == NC - 1:
                    mm.then_inc(s_qk, 1)

            def values(it, half):
                if half == 0:
                    pe.wait_ge(s_zhi, 1 + 4 * (it + 1))
                    pe.wait_ge(s_zlo, 1 + 4 * (it + 1))
                    pe.wait_ge(s_os, 1 + 4 * it)
                else:
                    pe.wait_ge(s_mr, 1 + 32 * it)
                for jb in range(4):
                    j = slice((4 * half + jb) * P, (4 * half + jb + 1) * P)
                    ps = bank[:, (6 if half == 0 else 4) + jb // 2, (jb % 2) * 256:(jb % 2 + 1) * 256]
                    for k in range(KT):
                        pe.matmul(ps, z_h[:, k, j], wqh[:, k, 512:768], start=k == 0, stop=False)
                        pe.matmul(ps, z_h[:, k, j], wql[:, k, 512:768], start=False, stop=False)
                        mm = pe.matmul(ps, z_l[:, k, j], wqh[:, k, 512:768], start=False, stop=k == KT - 1)
                mm.then_inc(s_v, 1)

            def max_block(it, h, n, b0):
                for c in range(NC):
                    mm = pe.matmul(bank[:, b0 + c, :], qq[:, h % 2, n:HW:8], kk[:, h % 2, px(c)], start=True, stop=True)
                mm.then_inc(s_mx, 1)

            def logits(it, h, t):
                b0 = 2 * (t % 2)
                if t >= 2 or h % 2 == 1:
                    pe.wait_ge(s_af, 1 + 32 * it + 8 * h + t - 1)
                    pe.wait_ge(s_ah, 1 + 32 * it + 8 * h + t - 1)
                j = slice(t * P, (t + 1) * P)
                for c in range(NC):
                    pe.matmul(bank[:, b0 + c, :], kk[:, h % 2, j], qq[:, h % 2, px(c)], start=True, stop=False)
                if t == 0:
                    pe.wait_ge(s_qlo, 1 + 4 * it + h + 1)
                    pe.wait_ge(d_k1[h % 2], 1 + 16 * (2 * it + h // 2 + 1))
                    pe.wait_ge(d_m[h % 2], 1 + 16 * (2 * it + h // 2 + 1))
                for c in range(NC):
                    mm = pe.matmul(bank[:, b0 + c, :], k1[:, h % 2, j], qm[:, h % 2, px(c)], start=False, stop=True)
                mm.then_inc(s_lt, 1)

            def weighted_high(it, h, t):
                if h % 2 == 0:
                    vl, rows = v_l[:, t, h // 2, 0, :], slice(0, HD)
                else:
                    vl, rows = v_l[:, t, h // 2, 1:3, :].rearrange("p s c -> p (s c)"), slice(0, P)
                vh = v_h[:, t, h // 2, h % 2:h % 2 + 2, :].rearrange("p s c -> p (s c)")
                pe.wait_ge(s_ah, 1 + 32 * it + 8 * h + t + 1)
                for c in range(NC):
                    pe.matmul(bank[:, 6 + c, :], vh, a_h[:, t % 2, px(c)], start=t == 0, stop=False)
                for c in range(NC):
                    mm = pe.matmul(bank[rows, 6 + c, :], vl, a_h[:, t % 2, px(c)], start=False, stop=False)
                mm.then_inc(s_avh, 1)

            def weighted_low(it, h, t):
                vh = v_h[:, t, h // 2, h % 2:h % 2 + 2, :].rearrange("p s c -> p (s c)")
                pe.wait_ge(s_al, 1 + 32 * it + 8 * h + t + 1)
                for c in range(NC):
                    mm = pe.matmul(bank[:, 6 + c, :], vh, a_l[:, t % 2, px(c)], start=False, stop=t == 7)
                mm.then_inc(s_avl, 1)

            def pair(it, p, filler, between=0):
                ha, hb = 2 * p, 2 * p + 1
                lead, step = LEAD[p], STEP[p]
                if filler:
                    pe.wait_ge(s_kf, 1 + 2 * it + p + 1)
                    conv(*filler, 0, lead)
                pe.wait_ge(d_qq[0], 1 + 16 * (2 * it + p + 1))
                pe.wait_ge(s_khi, 1 + 4 * it + ha + 1)
                pe.wait_ge(s_klo, 1 + 4 * it + ha + 1)
                for n in range(8):
                    m = 32 * it + 8 * ha + n
                    if n == 0:
                        pe.wait_ge(s_qhi, 1 + 4 * it + hb + 1)
                        pe.wait_ge(s_qlo, 1 + 4 * it + hb + 1)
                    elif n == 1 and p == 0:
                        pe.wait_ge(s_vhi, 1 + 2 * it + 1)
                        pe.wait_ge(s_vlo, 1 + 2 * it + 1)
                    elif n == 1:
                        pe.wait_ge(s_os, 1 + 4 * it + ha)
                    else:
                        pe.wait_ge(s_mr, 1 + m - 1)
                    max_block(it, ha, n, 0 if n % 2 == 0 else 6)
                    if filler:
                        conv(*filler, lead + n * step, lead + (n + 1) * step)

                def max_of_second(n):
                    if n == 0:
                        pe.wait_ge(d_qq[1], 1 + 16 * (2 * it + p + 1))
                        pe.wait_ge(s_khi, 1 + 4 * it + hb + 1)
                        pe.wait_ge(s_klo, 1 + 4 * it + hb + 1)
                        if p == 0:
                            pe.wait_ge(s_vhi, 1 + 2 * it + 2)
                            pe.wait_ge(s_vlo, 1 + 2 * it + 2)
                    else:
                        pe.wait_ge(s_mr, 1 + 32 * it + 8 * hb + n)
                    max_block(it, hb, n, 4)

                max_of_second(0)
                if filler:
                    conv(*filler, lead + 8 * step, 54)
                max_of_second(1)
                pe.wait_ge(s_mr, 1 + 32 * it + 8 * ha + 7)
                logits(it, ha, 0)
                pe.wait_ge(s_kf, 1 + 2 * it + p + 1)
                if filler:
                    pe.wait_ge(s_raw, 1 + 2 * (it + 1) + p + 1)
                for h in (ha, hb):
                    for t in range(8 if h == ha else 7):
                        if h == ha and 2 <= t <= 5:
                            max_of_second(t + 2)
                        if h == hb and t == 0:
                            weighted_low(it, ha, 7)
                        if t < 7:
                            logits(it, h, t + 1)
                        elif h == ha:
                            logits(it, hb, 0)
                        if t <= 1 and h == ha:
                            max_of_second(t + 2)
                        if t == 0 and h == ha:
                            pe.wait_ge(s_mr, 1 + 32 * it + 8 * ha + 8)
                        elif t == 0:
                            if between:
                                pe.wait_ge(s_mr, 1 + 32 * (it + 1))
                                conv(it + 1, 2, 0, between)
                            pe.wait_ge(s_os, 1 + 4 * it + h)
                        weighted_high(it, h, t)
                        if t > 0:
                            weighted_low(it, h, t - 1)

            def out_conv(it):
                pe.wait_ge(s_ohi, 1 + 4 * (it + 1))
                pe.wait_ge(s_olo, 1 + 4 * (it + 1))
                pe.wait_ge(s_af, 1 + 32 * (it + 1))
                pe.wait_ge(s_ah, 1 + 32 * (it + 1))
                for g in range(4):
                    c, co = g // 2, slice((g % 2) * P, (g % 2 + 1) * P)
                    for k in range(KT):
                        pe.matmul(bank[:, g, :], wmh[:, k, co], o_h[:, k, px(c)], start=k == 0, stop=False)
                        pe.matmul(bank[:, g, :], wmh[:, k, co], o_l[:, k, px(c)], start=False, stop=False)
                        mm = pe.matmul(bank[:, g, :], wml[:, k, co], o_h[:, k, px(c)], start=False, stop=k == KT - 1)
                    mm.then_inc(s_cm, 1)

            def image(it, l, b, has_next, has_next2):
                values(it, 0)
                for part in (1, 0):
                    for c in range(NC):
                        qk(it, 0, part, c)
                values(it, 1)
                pair(it, 0, (it + 1, 0) if has_next else None)
                qk(it, 1, 0, 0)
                weighted_high(it, 1, 7)
                weighted_low(it, 1, 6)
                qk(it, 1, 1, 0)
                weighted_low(it, 1, 7)
                qk(it, 1, 1, 1)
                qk(it, 1, 0, 1)
                pair(it, 1, (it + 1, 1) if has_next else None, 4 if has_next else 0)
                if has_next:
                    conv(it + 1, 2, 4, 9)
                weighted_high(it, 3, 7)
                weighted_low(it, 3, 6)
                if has_next:
                    conv(it + 1, 2, 9, 14)
                weighted_low(it, 3, 7)
                if has_next:
                    conv(it + 1, 2, 14, 54)
                    conv(it + 1, 3, 0, 54)
                out_conv(it)

            layers(pe, start, image)

        @block.scalar
        def _(act):
            def z_raw(i, g):
                act.wait_ge(s_cv, 1 + 4 * i + g + 1)
                act.wait_ge(s_zlo, 1 + 4 * i)
                act.activation(zf[:, g, :], bank[:, 2 + g, :], ACT.Copy).then_inc(s_raw, 1)

            def z_silu(i, g):
                m = g % 2
                if g < 2:
                    act.wait_ge(s_raw, 1 + 2 * i + g + 1)
                    src = zf[:, g, :]
                else:
                    act.wait_ge(s_cv, 1 + 4 * i + g + 1)
                    act.wait_ge(s_zlo, 1 + 4 * i + g - 1)
                    src = bank[:, 2 + g, :]
                act.activation(zf[:, m, :], src, ACT.Silu, scale=coef[:, 0, m:m + 1],
                               bias=coef[:, 1, m:m + 1]).then_inc(s_zf, 1)

            act.wait_ge(s_const, 2)
            for k in range(KT):
                act.wait_ge(d_y[k], 17)
                act.activation(yp_h[:, k, 1:1 + W, 1:1 + W], y_in[:, k, :].rearrange("p (r c) -> p r c", c=W),
                               ACT.Copy).then_inc(s_yhi, 1)

            def start(l):
                for i in range(N_OWN):
                    piece_high(act, l, i)
                act.wait_ge(s_coef, 1 + 2 * (l + 1))
                z_raw(l * B, 0)
                z_raw(l * B, 1)
                for g in range(4):
                    z_silu(l * B, g)

            def qk_high(it, p):
                def k_high(h):
                    act.wait_ge(s_kf, 1 + 2 * it + p + 1)
                    act.activation(kk[own(h), h % 2, :], kf[own(h), :], ACT.Copy).then_inc(s_khi, 1)

                def q_high(h):
                    act.wait_ge(s_qk, 1 + 4 * it + 2 * p + 2)
                    act.activation(qq[own(h), h % 2, :], two(0)[own(h)], ACT.Copy).then_inc(s_qhi, 1)

                k_high(2 * p)
                q_high(2 * p)
                q_high(2 * p + 1)
                k_high(2 * p + 1)

            def o_high(it, h):
                act.wait_ge(s_om, 1 + 4 * it + h + 1)
                act.activation(o_h[own(h), h // 2, :], os[own(h), :], ACT.Copy).then_inc(s_ohi, 1)

            def exps(it, h, t):
                T = 32 * it + 8 * h + t
                act.wait_ge(s_lt, 1 + T + 1)
                first = t < 2 and h == 0
                act.wait_ge(s_al, 1 + 32 * it if first else 1 + T - 1)
                act.wait_ge(s_avh, 1 + 32 * it if first else 1 + T - 1)
                act.activation(a_h[:, t % 2, :], two(2 * (t % 2)), ACT.Exp, scale=SCALE).then_inc(s_ah, 1)
                if first:
                    act.wait_ge(d_out[t], 1 + 32 * it)
                act.activation(a_f[:, t % 2, :], two(2 * (t % 2)), ACT.Exp, scale=SCALE).then_inc(s_af, 1)

            def o_out(it, h):
                act.wait_ge(s_avl, 1 + 32 * it + 8 * h + 8)
                act.wait_ge(s_olo, 1 + 4 * it + h)
                act.activation(os[:], two(6), ACT.Copy).then_inc(s_os, 1)

            def image(it, l, b, has_next, has_next2):
                for half in range(2):
                    if half == 1:
                        qk_high(it, 0)
                    act.wait_ge(s_v, 1 + 2 * it + half + 1)
                    src = two(6 if half == 0 else 4).rearrange("p (b e s c) -> p b e s c", b=4, e=2, s=2)
                    for e in range(2):
                        ins = act.activation(v_h[:, 4 * half:4 * half + 4, :, 2 * e, :], src[:, :, e, :, :], ACT.Copy)
                    ins.then_inc(s_vhi, 1)
                act.wait_ge(s_table, 1 + it)
                act.activation(zero[:, 1:2], zero[:, 0:1], ACT.Exp).then_inc(s_table, 1)
                for p in range(2):
                    if has_next:
                        z_raw(it + 1, p)
                    exps(it, 2 * p, 0)
                    for h in (2 * p, 2 * p + 1):
                        for t in range(8):
                            if t < 7:
                                exps(it, h, t + 1)
                            elif h % 2 == 0:
                                exps(it, h + 1, 0)
                            if h > 0 and t == 6:
                                o_high(it, h - 1)
                            if not has_next and (h, t) in NEXT_AT:
                                piece_high(act, l, NEXT_AT[h, t])
                        o_out(it, h)
                    if p == 0:
                        qk_high(it, 1)
                if has_next:
                    for g in range(4):
                        z_silu(it + 1, g)
                        if g == 2:
                            o_high(it, 3)
                else:
                    o_high(it, 3)
                for g in range(4):
                    m = g % 2
                    act.wait_ge(s_cm, 1 + 4 * it + g + 1)
                    act.wait_ge(s_al, 1 + 32 * (it + 1))
                    act.activation(a_f[:, m, px(g // 2)], bank[:, g, :], ACT.Silu, scale=coef[:, 0, 2 + m:3 + m],
                                   bias=coef[:, 1, 2 + m:3 + m]).then_inc(s_cf, 1)

            layers(act, start, image)

        @block.vector
        def _(dve):
            def z_low(i, g):
                c, m = g // 2, g % 2
                dve.wait_ge(s_zhi, 1 + 4 * i + g + 1)
                dve.tensor_tensor(z_l[:, m, px(c)], zf[:, m, :], f32(z_h[:, m, px(c)]), ALU.subtract).then_inc(s_zlo, 1)

            def y_low(i):
                for k in range(KT):
                    dve.wait_ge(s_yhi, 1 + KT * i + k + 1)
                    dve.tensor_tensor(yp_l[:, k, 1:1 + W, 1:1 + W], y_in[:, k, :].rearrange("p (r c) -> p r c", c=W),
                                      f32(yp_h[:, k, 1:1 + W, 1:1 + W]), ALU.subtract).then_inc(s_ylo, 1)

            def start(l):
                dve.wait_ge(s_cf, 1 + 4 * B * l)
                dve.tensor_copy(coef[:, 0, :], bn_s[:, bass.ds(8 + 4 * l, 4)]).then_inc(s_coef, 1)
                dve.tensor_copy(coef[:, 1, :], bn_o[:, bass.ds(8 + 4 * l, 4)]).then_inc(s_coef, 1)
                for i in range(N_OWN):
                    piece_low(dve, l, i)
                for g in range(4):
                    z_low(l * B, g)
                y_low(l * B + 1)

            def qk_out(it, p):
                def q_low(h):
                    dve.wait_ge(s_qhi, 1 + 4 * it + h + 1)
                    dve.tensor_tensor(qm[own(h), h % 2, :], two(0)[own(h)], f32(qq[own(h), h % 2, :]),
                                      ALU.subtract).then_inc(s_qlo, 1)
                dve.wait_ge(s_qk, 1 + 4 * it + 2 * p + 1)
                dve.wait_ge(s_kr, 1 + 2 * it + p + 1)
                dve.tensor_tensor(kf[:], two(2), kf[:], ALU.add).then_inc(s_kf, 1)

                def k_low(h):
                    dve.wait_ge(s_khi, 1 + 4 * it + h + 1)
                    dve.tensor_tensor(kk[other(h), h % 2, :], kf[own(h), :], f32(kk[own(h), h % 2, :]),
                                      ALU.subtract).then_inc(s_klo, 1)

                k_low(2 * p)
                q_low(2 * p)
                q_low(2 * p + 1)
                k_low(2 * p + 1)

            def reduce_block(it, h, n, b0):
                dve.wait_ge(s_mx, 1 + 32 * it + 8 * h + n + 1)
                dve.tensor_reduce(mt[:, h % 2, n:n + 1], two(b0), AX.X, ALU.max, negate=True).then_inc(s_mr, 1)

            def a_low(it, h, t):
                T = 32 * it + 8 * h + t
                dve.wait_ge(s_ah, 1 + T + 1)
                dve.wait_ge(s_af, 1 + T + 1)
                if not (h == 0 and t < 2):
                    dve.wait_ge(s_avl, 1 + T - 1)
                else:
                    dve.wait_ge(s_avl, 1 + 32 * it)
                dve.tensor_tensor(a_l[:, t % 2, :], a_f[:, t % 2, :], f32(a_h[:, t % 2, :]),
                                  ALU.subtract).then_inc(s_al, 1)

            def o_recip(it, h):
                dve.wait_ge(d_s8, 1 + 16 * (4 * it + h + 1))
                dve.reciprocal(r8i[:], r8[:]).then_inc(s_rc, 1)

            def o_mult(it, h):
                dve.wait_ge(d_rb, 1 + 16 * (4 * it + h + 1))
                dve.tensor_tensor(os[own(h), :], os[own(h), :], rb[own(h), :], ALU.mult).then_inc(s_om, 1)

            def o_low(it, h):
                dve.wait_ge(s_ohi, 1 + 4 * it + h + 1)
                dve.tensor_tensor(o_l[own(h), h // 2, :], os[own(h), :], f32(o_h[own(h), h // 2, :]),
                                  ALU.subtract).then_inc(s_olo, 1)

            y_low(0)
            for h in range(2):
                dve.memset(f32(qm[other(h), h, :]), 0.0)
                ins = dve.memset(f32(k1[other(h), h, :]), 0.0)
            ins.then_inc(s_const_rows, 1)
            dve.wait_ge(s_const_rows, 2)
            for h in range(2):
                ins = dve.memset(f32(k1[first_other(h), h, :]), 1.0)
            ins.then_inc(s_const_rows, 1)

            def image(it, l, b, has_next, has_next2):
                for half in range(2):
                    if half == 1:
                        qk_out(it, 0)
                    dve.wait_ge(s_vhi, 1 + 2 * it + half + 1)
                    src = two(6 if half == 0 else 4).rearrange("p (b e s c) -> p b e s c", b=4, e=2, s=2)
                    for e in range(2):
                        blocks = (slice(None), slice(4 * half, 4 * half + 4), slice(None), 2 * e, slice(None))
                        ins = dve.tensor_tensor(v_l[blocks], src[:, :, e, :, :], f32(v_h[blocks]), ALU.subtract)
                    ins.then_inc(s_vlo, 1)
                for p in range(2):
                    if p == 1:
                        qk_out(it, 1)
                    for n in range(8):
                        reduce_block(it, 2 * p, n, 0 if n % 2 == 0 else 6)
                    reduce_block(it, 2 * p + 1, 0, 4)
                    reduce_block(it, 2 * p + 1, 1, 4)
                    for h in (2 * p, 2 * p + 1):
                        for t in range(8):
                            if h % 2 == 0 and t <= 5:
                                reduce_block(it, h + 1, t + 2, 4)
                            a_low(it, h, t)
                            if h > 0 and t == 1:
                                o_recip(it, h - 1)
                            if h > 0 and t == 5:
                                o_mult(it, h - 1)
                            if h > 0 and t == 7:
                                o_low(it, h - 1)
                            if not has_next and (h, t) in NEXT_AT:
                                piece_low(dve, l, NEXT_AT[h, t])
                o_recip(it, 3)
                if has_next:
                    z_low(it + 1, 0)
                    z_low(it + 1, 1)
                o_mult(it, 3)
                o_low(it, 3)
                if has_next:
                    z_low(it + 1, 2)
                    z_low(it + 1, 3)
                if has_next2:
                    y_low(it + 2)
                if not has_next:
                    y_low(it + 1)

            layers(dve, start, image)

        @block.gpsimd
        def _(pool):
            def copy(dst, src):
                alone(pool, s_spare_pool)
                return pool.tensor_scalar(dst, src, 1.0, None, ALU.mult)

            for t in (yp_h, yp_l):
                pool.memset(f32(t[:]), 0.0)
            pool.memset(zero[:], 0.0).then_inc(s_const, 1)
            pool.memset(f32(v_l[:, :, :, 1, :]), 0.0)
            pool.memset(f32(v_h[:, :, :, 1, :]), 1.0).then_inc(s_const, 1)

            def y_high(i):
                for k in range(KT):
                    pool.wait_ge(d_y[k], 1 + 16 * (i + 1))
                    pool.wait_ge(s_cv, 1 + 4 * i)
                    copy(yp_h[:, k, 1:1 + W, 1:1 + W],
                         y_in[:, k, :].rearrange("p (r c) -> p r c", c=W)).then_inc(s_yhi, 1)

            def z_high(i, g):
                c, m = g // 2, g % 2
                pool.wait_ge(s_zf, 1 + 4 * i + g + 1)
                copy(z_h[:, m, px(c)], zf[:, m, :]).then_inc(s_zhi, 1)

            def k_rel(it, p):
                pool.wait_ge(s_klo, 1 + 4 * it + 2 * p)
                pool.wait_ge(s_om, 1 + 4 * it + p)
                pool.tensor_tensor(kf[:].rearrange("p (r c) -> p r c", c=W),
                                   rhs[:, p, :].unsqueeze(2).to_broadcast([P, W, W]),
                                   rws[:, p, :].unsqueeze(1).to_broadcast([P, W, W]), ALU.add).then_inc(s_kr, 1)

            def start(l):
                for g in range(4):
                    z_high(l * B, g)
                y_high(l * B + 1)
                pool.wait_ge(d_r, 1 + 32 * (l + 1))
                k_rel(l * B, 0)

            def image(it, l, b, has_next, has_next2):
                k_rel(it, 1)
                if has_next:
                    for g in range(4):
                        z_high(it + 1, g)
                        if g == 2:
                            k_rel(it + 1, 0)
                if has_next2:
                    y_high(it + 2)
                if not has_next:
                    y_high(it + 1)
                for g in range(4):
                    pool.wait_ge(s_cf, 1 + 4 * it + g + 1)
                    pool.wait_ge(d_res[g % 2], 1 + 16 * (2 * it + g // 2 + 1))
                    pool.tensor_tensor(a_f[:, g % 2, px(g // 2)], res[:, g % 2, :], a_f[:, g % 2, px(g // 2)],
                                       ALU.add).then_inc(s_res, 1)

            layers(pool, start, image)

        @block.sync
        def _(sp):
            def load_y(l, i, b):
                alone(sp, s_spare)
                for k in range(KT):
                    sp.dma_start(y_in[:, k, :], y_d[b, 2 + KT * l + k]).then_inc(d_y[k], 16)

            for k in range(KT):
                sp.dma_start(y_in[:, k, :], y_d[0, 2 + k]).then_inc(d_y[k], 16)

            def start(l):
                sp.wait_ge(s_kr, 1 + 2 * B * l)
                alone(sp, s_spare)
                sp.dma_start(rws[:], rw[bass.ds(l, 1)].rearrange("o p t c -> (o p) t c")).then_inc(d_r, 16)
                sp.dma_start(rhs[:], rh[bass.ds(l, 1)].rearrange("o p t c -> (o p) t c")).then_inc(d_r, 16)
                sp.wait_ge(s_res, 1 + 4 * B * l)
                alone(sp, s_spare)
                for i in range(N_OWN):
                    load_piece(sp, l, l, i)
                for s in range(2):
                    sp.wait_ge(d_out[s], 1 + 32 * B * l)
                alone(sp, s_spare)
                sp.wait_ge(s_ylo, 1 + KT * (B * l + 1))
                load_y(l, l * B + 1, 1)
                sp.wait_ge(s_wlo, 1 + N_ALL * l + N_OWN)
                stacks(l * B, 0)

            def stacks(it, p):
                for h in (2 * p, 2 * p + 1):
                    sp.wait_ge(s_qhi, 1 + 4 * it + h + 1)
                    sp.dma_start(f32(qq[other(h), h % 2, :]), f32(qq[own(h), h % 2, :])).then_inc(d_qq[h % 2], 16)
                for h in (2 * p, 2 * p + 1):
                    sp.wait_ge(s_khi, 1 + 4 * it + h + 1)
                    sp.dma_start(f32(k1[own(h), h % 2, :]), f32(kk[own(h), h % 2, :])).then_inc(d_k1[h % 2], 16)

            def max_row(it, h):
                sp.wait_ge(s_mr, 1 + 32 * it + 8 * h + 8)
                alone(sp, s_spare)
                sp.wait_ge(s_qlo, 1 + 4 * it + h + 1)
                sp.dma_start(f32(qm[first_other(h), h % 2, :]).rearrange("o (p c) -> o p c", c=8),
                             f32(mt[:, h % 2, :])).then_inc(d_m[h % 2], 16)

            def sums(it, h):
                sp.wait_ge(s_os, 1 + 4 * it + h + 1)
                sp.dma_start(r8[:], os[first_other(h), :].rearrange("o (p c) -> o p c", c=8)).then_inc(d_s8, 16)

            def recips(it, h):
                sp.wait_ge(s_rc, 1 + 4 * it + h + 1)
                sp.dma_start(rs_d.rearrange("o (p c) -> (o p) c", c=8), r8i[:]).then_inc(d_rc, 16)
                sp.wait_ge(d_rc, 1 + 16 * (4 * it + h + 1))
                sp.dma_start(rb[own(h), :], rs_d.to_broadcast([HD, HW])).then_inc(d_rb, 16)

            def load_res(l, b, g):
                c, m = g // 2, g % 2
                alone(sp, s_spare)
                sp.dma_start(res[:, g % 2, :], y_d[b, 2 + KT * l + m][:, px(c)]).then_inc(d_res[g % 2], 16)

            def image(it, l, b, has_next, has_next2):
                if not has_next:
                    sp.wait_ge(s_cv, 1 + 4 * (it + 1))
                    alone(sp, s_spare)
                    sp.wait_ge(s_ylo, 1 + KT * (it + 1))
                    alone(sp, s_spare)
                    for i in (4, 5):
                        load_piece(sp, l, l + 1, i)
                max_row(it, 0)
                max_row(it, 1)
                for g in range(2):
                    sp.wait_ge(s_res, 1 + 4 * it)
                    load_res(l, b, g)
                sums(it, 0)
                recips(it, 0)
                if not has_next:
                    alone(sp, s_spare)
                    for i in range(6, 11):
                        load_piece(sp, l, l + 1, i)
                sums(it, 1)
                stacks(it, 1)
                max_row(it, 2)
                recips(it, 1)
                max_row(it, 3)
                sums(it, 2)
                recips(it, 2)
                if has_next2:
                    sp.wait_ge(s_ylo, 1 + KT * (it + 2))
                    load_y(l, it + 2, b + 2)
                if not has_next:
                    alone(sp, s_spare)
                    for i in range(11, 13):
                        load_piece(sp, l, l + 1, i)
                sums(it, 3)
                recips(it, 3)
                if not has_next:
                    for s in range(2):
                        sp.wait_ge(d_out[s], 1 + 32 * it)
                    alone(sp, s_spare)
                    sp.wait_ge(s_wlo, 1 + N_ALL * (l + 1))
                    load_y(l + 1, it + 1, 0)
                for g in range(4):
                    c, m = g // 2, g % 2
                    if g == 2 and has_next:
                        stacks(it + 1, 0)
                    sp.wait_ge(s_res, 1 + 4 * it + g + 1)
                    if g < 2:
                        load_res(l, b, g + 2)
                    alone(sp, s_spare)
                    sp.dma_start(y_d[b, 4 + KT * l + m][:, px(c)], a_f[:, m, px(c)]).then_inc(d_out[m], 16)

            layers(sp, start, image)
            for s in range(2):
                sp.wait_ge(d_out[s], 1 + 32 * B * L)


def phase_d(nc, sem_, B, CT, x_v, w_hi, w_lo, y_d, x1_d, bank, bn_s, bn_o, x1_mv):
    K8 = 8
    G8 = CT * NC
    YS, XS = 2, 4

    def sem(name):
        return sem_("d_" + name)

    s_spare = sem("s_spare")
    d_y = [sem(f"d_y{i}") for i in range(YS)]
    d_y0 = [sem(f"d_y0_{k}") for k in range(K8)]
    s_yh, s_yl = sem("s_yh"), sem("s_yl")
    s_mm, s_sf, s_x1, s_st, s_ag = sem("s_mm"), sem("s_sf"), sem("s_x1"), sem("s_st"), sem("s_ag")
    s_mv = sem("s_mv")
    d_x = [sem(f"d_x{i}") for i in range(XS)]
    d_o = [sem(f"d_o{i}") for i in range(XS)]
    yield

    with ExitStack() as ctx:
        def sb(name, shape, dt):
            return ctx.enter_context(nc.sbuf_tensor("d_" + name, shape, dt))

        yin = sb("yin", [P, YS, HW], F32)
        yh = sb("yh", [P, 2, K8, HW], F32R)
        yl = sb("yl", [P, 2, K8, HW], F32R)
        sf = sb("sf", [P, 2, NB], F32)
        xr = sb("xr", [P, XS, NB], F32)
        stats = sb("stats", [P, CT, NC, 6], F32)
        mv = sb("mv", [P, CT, 2], F32)

        block = ctx.enter_context(nc.Block())

        @block.sync
        def _(sp):
            def load_y(n, k):
                alone(sp, s_spare)
                sp.dma_start(yin[:, k % YS, :], y_d[n, k]).then_inc(d_y[k % YS], 16)

            def load_x(n, g):
                alone(sp, s_spare)
                sp.dma_start(xr[:, g % XS, :], x_v[n, g // NC][:, (g % NC) * NB:(g % NC + 1) * NB]).then_inc(d_x[g % XS], 16)

            for k in range(K8):
                sp.dma_start(f32(yh[:, 1, k, :]), y_d[0, k]).then_inc(d_y0[k], 16)
            for g in range(XS):
                load_x(0, g)

            def image(j, u, left):
                n = 2 * j + u
                for g in range(G8):
                    if left:
                        sp.wait_ge(s_yl, 1 + K8 * (n + 1) + g - YS + 1)
                        load_y(n + 1, g)
                    sp.wait_ge(s_x1, 1 + G8 * n + g + 1)
                    alone(sp, s_spare)
                    sp.dma_start(x1_d[n, g // NC][:, (g % NC) * NB:(g % NC + 1) * NB], xr[:, g % XS, :]).then_inc(d_o[g % XS], 16)
                    if g >= 1 and g - 1 + XS < G8:
                        q = g - 1
                        sp.wait_ge(d_o[q % XS], 1 + 32 * n + 16 * (q // XS + 1))
                        sp.wait_ge(s_st, 1 + G8 * n + q + 1)
                        load_x(n, q + XS)
                    if g >= XS + 1 and left:
                        q = g - 1
                        sp.wait_ge(d_o[q % XS], 1 + 32 * n + 16 * (q // XS + 1))
                        sp.wait_ge(s_st, 1 + G8 * n + q + 1)
                        load_x(n + 1, q - XS)
                if left:
                    q = G8 - 1
                    sp.wait_ge(d_o[q % XS], 1 + 32 * n + 16 * (q // XS + 1))
                    sp.wait_ge(s_st, 1 + G8 * n + q + 1)
                    load_x(n + 1, q - XS)

            images(sp, B, image)
            for i in range(XS):
                sp.wait_ge(d_o[i], 1 + 16 * B * G8 // XS)

        @block.scalar
        def _(act):
            def high(after, u, k):
                act.wait_ge(d_y[k % YS], 1 + 16 * K8 // YS * after + 16 * (k // YS + 1))
                act.activation(yh[:, u, k, :], yin[:, k % YS, :], ACT.Copy).then_inc(s_yh, 1)

            act.sem_inc(s_sf, G8)
            for k in range(K8):
                act.wait_ge(d_y0[k], 17)
                act.activation(yh[:, 0, k, :], f32(yh[:, 1, k, :]), ACT.Copy).then_inc(s_yh, 1)

            def image(j, u, left):
                n = 2 * j + u
                for g in range(G8):
                    m = g // NC
                    act.wait_ge(s_mm, 1 + G8 * n + g + 1)
                    act.wait_ge(s_x1, 1 + G8 * n + max(g - 1, 0))
                    act.activation(sf[:, g % 2, :], bank[:, g % 8, :], ACT.Silu, scale=bn_s[:, 4 + m:5 + m],
                                   bias=bn_o[:, 4 + m:5 + m]).then_inc(s_sf, 1)
                    if left:
                        high(n, 1 - u, g)

            images(act, B, image)

        @block.vector
        def _(dve):
            def low(n, u, k):
                dve.wait_ge(s_yh, 1 + K8 * n + k + 1)
                dve.tensor_tensor(yl[:, u, k, :], yin[:, k % YS, :], f32(yh[:, u, k, :]), ALU.subtract).then_inc(s_yl, 1)

            for k in range(K8):
                dve.wait_ge(s_yh, 1 + k + 1)
                dve.tensor_tensor(yl[:, 0, k, :], f32(yh[:, 1, k, :]), f32(yh[:, 0, k, :]), ALU.subtract).then_inc(s_yl, 1)

            def image(j, u, left):
                n = 2 * j + u
                for g in range(G8):
                    if left:
                        low(n + 1, 1 - u, g)
                    dve.wait_ge(s_x1, 1 + G8 * n + g + 1)
                    dve.wait_ge(s_mv, 1 + n)
                    dve.bn_stats(stats[:, g // NC, g % NC, :], xr[:, g % XS, :]).then_inc(s_st, 1)
                dve.wait_ge(s_st, 1 + G8 * (n + 1))
                alone(dve, s_spare)
                for t in range(CT):
                    ins = dve.bn_aggr(mv[:, t, :], stats[:, t, :, :])
                ins.then_inc(s_ag, 1)
                dve.wait_ge(s_ag, 1 + n + 1)
                dve.tensor_copy(x1_mv[:, bass.ds(n, 1), :, :].rearrange("p o t s -> p (o t s)"),
                                mv[:].rearrange("p t s -> p (t s)")).then_inc(s_mv, 1)

            images(dve, B, image)

        @block.gpsimd
        def _(pool):
            def image(j, u, left):
                n = 2 * j + u
                for g in range(G8):
                    pool.wait_ge(s_sf, 1 + G8 + G8 * n + g + 1)
                    pool.wait_ge(d_x[g % XS], 1 + 32 * n + 16 * (g // XS + 1))
                    pool.tensor_tensor(xr[:, g % XS, :], xr[:, g % XS, :], sf[:, g % 2, :], ALU.add).then_inc(s_x1, 1)

            images(pool, B, image)

        @block.tensor
        def _(pe):
            def image(j, u, left):
                n = 2 * j + u
                for g in range(G8):
                    m, c = g // NC, g % NC
                    px = slice(c * NB, (c + 1) * NB)
                    pe.wait_ge(s_sf, 1 + G8 * n + g + 1)
                    for k in range(K8):
                        if g == 0:
                            pe.wait_ge(s_yl, 1 + K8 * n + k + 1)
                        wk = slice(k * 512 + m * P, k * 512 + (m + 1) * P)
                        pe.matmul(bank[:, g, :], w_hi[:, wk], yh[:, u, k, px], start=k == 0, stop=False)
                        pe.matmul(bank[:, g, :], w_hi[:, wk], yl[:, u, k, px], start=False, stop=False)
                        mm = pe.matmul(bank[:, g, :], w_lo[:, wk], yh[:, u, k, px], start=False, stop=k == K8 - 1)
                    mm.then_inc(s_mm, 1)

            images(pe, B, image)


def phase_l(nc, sem_, B, CT, w1_rows, w1_t, bn1, x1_d, out_v, bank, group_avg, mhalf, x1_mv):
    N = B * CT
    CIN = 32
    XB = 4

    def quads(eng, body):
        if B > 2 * XB:
            with eng.Fori(0, B // XB - 1) as j:
                for u in range(XB):
                    body(j, u, XB)
        elif B > XB:
            for u in range(XB):
                body(0, u, XB)
        for u in range(XB):
            body(B // XB - 1, u, XB - 1 - u)

    class Step:

        def __init__(self, turn, slot, kept, last=False):
            self.turn, self.slot, self.place = turn, slot, XB * turn + slot
            self.kept, self.last = kept, last
            self.image = B - XB + slot if kept else XB * (turn - 1) + slot
            self.first = kept and slot == 0
            self.reload = B > XB and not last

        def following(self):
            if self.slot < XB - 1:
                return Step(self.turn, self.slot + 1, self.kept, self.last)
            return Step(self.turn + 1, 0, False) if self.reload else None

    def output_order(eng, body):
        for u in range(XB):
            body(Step(0, u, True))
        if B > 2 * XB:
            with eng.Fori(0, B // XB - 2) as j:
                for u in range(XB):
                    body(Step(j + 1, u, False))
        if B > XB:
            for u in range(XB):
                body(Step(B // XB - 1, u, False, True))

    def sem(name):
        return sem_("l_" + name)

    d_w, s_c, s_eps, s_rs = sem("d_w"), sem("s_c"), sem("s_eps"), sem("s_rs")
    s_aff, s_gs, s_gm = sem("s_aff"), sem("s_gs"), sem("s_gm")
    s_wz, s_wb = sem("s_wz"), sem("s_wb")
    d_x = [sem(f"d_x{i}") for i in range(XB)]
    s_sg, s_mm, s_h, s_hs = sem("s_sg"), sem("s_mm"), sem("s_h"), sem("s_hs")
    s_spare = sem("s_spare")
    d_z = [sem(f"d_z{i}") for i in range(XB)]
    s_u, s_v, s_q, s_p, s_o = sem("s_u"), sem("s_v"), sem("s_q"), sem("s_p"), sem("s_o")
    s_t2 = sem("s_t2")
    d_o = [sem(f"d_o{i}") for i in range(XB)]
    yield

    with ExitStack() as ctx:
        def sb(name, shape, dt):
            return ctx.enter_context(nc.sbuf_tensor("l_" + name, shape, dt))

        wr = sb("wr", [P, CT, CIN * TAPS], F32)
        wt = sb("wt", [P, CT, TAPS, CIN], F32)
        wb = sb("wb", [P, CT, TAPS, P], BF16)
        bnp = sb("bnp", [P, 5, CT], F32)
        wst = sb("wst", [P, CT, 6], F32)
        wmv = sb("wmv", [P, CT, 2], F32)
        wab = sb("wab", [P, CT], F32)
        sw = sb("sw", [P, CT], F32)
        t1 = sb("t1", [P, N], F32)
        t2 = sb("t2", [P, N], F32)
        gmean = sb("gmean", [P, B, CT], F32)
        r_g = sb("r_g", [P, B, CT], F32)
        t_g = sb("t_g", [P, B, CT], F32)
        cm = sb("cm", [P, B, CT], F32)
        cv = sb("cv", [P, B, CT], F32)
        m1 = sb("m1", [P, CT], F32)
        v1 = sb("v1", [P, CT], F32)
        i1 = sb("i1", [P, CT], F32)
        a1 = sb("a1", [P, CT], F32)
        sa = sb("sa", [P, B, CT], F32)
        sc = sb("sc", [P, B, CT], F32)
        xs = sb("xs", [P, XB, CT, HW], F32)
        sg = sb("sg", [P, 2, CT, PW, PW], BF16)
        h = sb("h", [P, CT, B, HW], F16)
        hst = sb("hst", [P, CT, B * NC, 6], F32)
        hmv = sb("hmv", [P, CT, 2], F32)
        a2 = sb("a2", [P, CT], F32)
        b2 = sb("b2", [P, CT], F32)
        u_ = sb("u_", [P, CT, HW], F32)
        p_ = sb("p_", [P, CT, HW], F32)
        a_1 = sb("a_1", [P, CT], F32)

        G8 = CT * NC

        def h_chunk(n, g):
            return h[:, g // NC, bass.ds(n, 1), (g % NC) * NB:(g % NC + 1) * NB].rearrange("p o n -> p (o n)")

        flat = lambda t: t[:].rearrange("p b c -> p (b c)")
        over_b = lambda t: t[:].unsqueeze(1).to_broadcast([P, B, CT])
        block = ctx.enter_context(nc.Block())

        @block.sync
        def _(sp):
            sp.dma_start(bnp[:], bn1).then_inc(d_w, 16)
            sp.dma_start(wr[:], w1_rows).then_inc(d_w, 16)
            sp.dma_start(wt[:], w1_t).then_inc(d_w, 16)

            def load(n, u, d):
                alone(sp, s_spare)
                for t in range(CT):
                    sp.dma_start(xs[:, u, t, :], x1_d[n, t]).then_inc(d[u], 16)

            for u in range(XB):
                load(u, u, d_x)

            def image(j, u, left):
                if left == XB:
                    sp.wait_ge(s_sg, 1 + CT * (XB * j + u + 1))
                    load(XB * (j + 1) + u, u, d_x)

            quads(sp, image)

            def store(s):
                u, m, n = s.slot, s.place, s.image
                for t in range(CT):
                    sp.wait_ge(s_o, 1 + CT * m + t + 1)
                    alone(sp, s_spare)
                    sp.dma_start(out_v[n, t], xs[:, u, t, :]).then_inc(d_o[u], 16)
                if s.reload:
                    sp.wait_ge(d_o[u], 1 + 16 * CT * (s.turn + 1))
                    load(m, u, d_z)

            output_order(sp, store)
            for u in range(XB):
                sp.wait_ge(d_o[u], 1 + 16 * CT * B // XB)

        @block.vector
        def _(dve):
            links = [0]

            def link(ins):
                links[0] += 1
                ins.then_inc(s_c, 1)
                dve.wait_ge(s_c, 1 + links[0])

            rsq = [0]

            def rsqrt(dst, src, eps):
                rsq[0] += 1
                dve.tensor_scalar(t1[:, 0:src.free_size()], src, eps, None, ALU.add).then_inc(s_eps, 1)
                dve.wait_ge(s_rs, 1 + rsq[0])
                link(dve.tensor_copy(dst, t2[:, 0:src.free_size()]))

            link(dve.tensor_copy(flat(cm), x1_mv[:, :, :, 0].rearrange("p b c -> p (b c)")))
            dve.tensor_copy(flat(cv), x1_mv[:, :, :, 1].rearrange("p b c -> p (b c)")).then_inc(s_gs, 1)
            dve.wait_ge(s_gm, 2)
            link(dve.tensor_copy(flat(gmean), bank[:, 7, 0:N]))
            link(dve.tensor_tensor(flat(t_g), flat(cm), flat(gmean), ALU.subtract))
            link(dve.tensor_tensor(flat(r_g), flat(t_g), flat(t_g), ALU.mult))
            dve.tensor_tensor(flat(sa), flat(r_g), flat(cv), ALU.add).then_inc(s_gs, 1)
            dve.wait_ge(s_gm, 3)
            rsqrt(flat(r_g), bank[:, 7, 64:64 + N], GN_EPS)
            link(dve.tensor_tensor(flat(cm), flat(t_g), flat(r_g), ALU.mult))
            link(dve.scalar_tensor_tensor(flat(t_g), flat(gmean), -1.0, flat(r_g), ALU.mult, ALU.mult))
            link(dve.tensor_tensor(flat(cv), flat(cv), flat(r_g), ALU.mult))
            link(dve.tensor_tensor(flat(cv), flat(cv), flat(r_g), ALU.mult))
            link(dve.tensor_reduce(m1[:], cm[:].rearrange("p b c -> p c b"), AX.X, ALU.add))
            link(dve.tensor_scalar(m1[:], m1[:], 1.0 / B, None, ALU.mult))
            link(dve.tensor_tensor(cm[:], cm[:], over_b(m1), ALU.subtract))
            link(dve.tensor_tensor(flat(cm), flat(cm), flat(cm), ALU.mult))
            link(dve.tensor_tensor(flat(cm), flat(cm), flat(cv), ALU.add))
            link(dve.tensor_reduce(v1[:], cm[:].rearrange("p b c -> p c b"), AX.X, ALU.add))
            link(dve.tensor_scalar(v1[:], v1[:], 1.0 / B, None, ALU.mult))
            rsqrt(i1[:], v1[:], BN1_EPS)
            dve.wait_ge(d_w, 49)
            link(dve.tensor_tensor(a1[:], i1[:], bnp[:, 0, :], ALU.mult))
            link(dve.tensor_tensor(sa[:], r_g[:], over_b(a1), ALU.mult))
            link(dve.tensor_tensor(sc[:], t_g[:], over_b(m1), ALU.subtract))
            link(dve.tensor_tensor(sc[:], sc[:], over_b(a1), ALU.mult))
            dve.tensor_tensor(sc[:], sc[:], bnp[:, 1:2, :].to_broadcast([P, B, CT]), ALU.add).then_inc(s_aff, 1)

            n_w = CIN * TAPS
            for t in range(CT):
                ins = dve.bn_stats(wst[:, t, :], wr[:, t, :])
            link(ins)
            for t in range(CT):
                ins = dve.bn_aggr(wmv[:, t, :], wst[:, t, :])
            link(ins)
            link(dve.tensor_tensor(wr[:], wr[:], wmv[:, :, 0:1].to_broadcast([P, CT, n_w]), ALU.subtract))
            link(dve.tensor_reduce(wab[:], wr[:], AX.X, ALU.add, apply_absolute_value=True))
            link(dve.tensor_scalar(sw[:], wmv[:, :, 1], float(n_w) / (n_w - 1), None, ALU.mult))
            rsqrt(sw[:], sw[:], 0.0)
            link(dve.tensor_tensor(sw[:], sw[:], wab[:], ALU.mult))
            link(dve.tensor_scalar(sw[:], sw[:], 1.0 / n_w, None, ALU.mult))

            def stats(j, u, left):
                n = 2 * j + u
                for g in range(G8):
                    dve.wait_ge(s_h, 1 + G8 + G8 * n + g + 1)
                    dve.bn_stats(hst[:, g // NC, bass.ds(NC * n + g % NC, 1), :].rearrange("p o s -> p (o s)"),
                                 h_chunk(n, g)).then_inc(s_hs, 1)

            images(dve, B, stats)
            dve.wait_ge(s_hs, 1 + G8 * B)
            for t in range(CT):
                ins = dve.bn_aggr(hmv[:, t, :], hst[:, t, :, :])
            link(ins)
            link(dve.tensor_tensor(v1[:], sw[:], sw[:], ALU.mult))
            link(dve.tensor_tensor(v1[:], v1[:], hmv[:, :, 1], ALU.mult))
            rsqrt(i1[:], v1[:], BN1_EPS)
            link(dve.tensor_tensor(a2[:], i1[:], sw[:], ALU.mult))
            link(dve.tensor_tensor(a2[:], a2[:], bnp[:, 2, :], ALU.mult))
            link(dve.tensor_tensor(b2[:], a2[:], hmv[:, :, 0], ALU.mult))
            link(dve.tensor_tensor(b2[:], bnp[:, 3, :], b2[:], ALU.subtract))
            link(dve.tensor_scalar(a_1[:], bnp[:, 4, :], -1.0, 1.0, ALU.mult, ALU.add))
            dve.tensor_tensor(t_g[:], t_g[:], over_b(b2), ALU.add).then_inc(s_t2, 1)

            def prelu(T, t):
                dve.wait_ge(s_q, 1 + T + 1)
                dve.scalar_tensor_tensor(p_[:, t, :], p_[:, t, :], a_1[:, t:t + 1], u_[:, t, :],
                                         ALU.mult, ALU.add).then_inc(s_p, 1)

            def image(s):
                m, n = s.place, s.image
                for t in range(CT):
                    dve.wait_ge(s_u, 1 + CT * m + t + 1)
                    alone(dve, s_spare)
                    dve.scalar_tensor_tensor(u_[:, t, :], h[:, t, bass.ds(n, 1), :].rearrange("p o n -> p (o n)"),
                                             a2[:, t:t + 1], u_[:, t, :], ALU.mult, ALU.add).then_inc(s_v, 1)
                    if t > 0 or not s.first:
                        prelu(CT * m + t - 1, (t - 1) % CT)

            output_order(dve, image)
            prelu(CT * B - 1, CT - 1)

        @block.gpsimd
        def _(pool):
            for edge in (0, PW - 1):
                pool.memset(sg[:, :, :, edge, :], 0.0)
                pool.memset(sg[:, :, :, 1:1 + W, edge], 0.0).then_inc(s_wz, 1)
            for k, n in enumerate((N, CT, CT, CT)):
                if k == 1:
                    pool.memset(wb[:], 0.0).then_inc(s_wz, 1)
                pool.wait_ge(s_eps, 1 + k + 1)
                pool.tensor_tensor(t2[:, 0:n], t1[:, 0:n], mhalf[:, 0:n], ALU.pow).then_inc(s_rs, 1)

            def image(s):
                u, m = s.slot, s.place
                for t in range(CT):
                    pool.wait_ge(s_p, 1 + CT * m + t + 1)
                    pool.tensor_tensor(xs[:, u, t, :], xs[:, u, t, :], p_[:, t, :], ALU.add).then_inc(s_o, 1)

            output_order(pool, image)

        @block.scalar
        def _(act):
            act.wait_ge(d_w, 49)
            act.wait_ge(s_wz, 4)
            for g in range(4):
                rows = slice(32 * g, 32 * g + 32)
                act.activation(wb[rows, :, :, 32 * g:32 * g + 32], wt[rows, :, :, :], ACT.Sign).then_inc(s_wb, 1)
            act.wait_ge(s_aff, 2)

            def signs(j, u):
                n = XB * j + u
                act.wait_ge(d_x[u], 1 + 16 * CT * (j + 1))
                for t in range(CT):
                    act.activation(sg[:, u % 2, t, 1:1 + W, 1:1 + W], xs[:, u, t, :].rearrange("p (r c) -> p r c", c=W),
                                   ACT.Sign, scale=sa[:, bass.ds(n, 1), t], bias=sc[:, bass.ds(n, 1), t]).then_inc(s_sg, 1)

            signs(0, 0)
            act.sem_inc(s_h, G8)

            def conv_out(j, u, left):
                n = XB * j + u
                if left:
                    act.wait_ge(s_mm, 1 + G8 * n)
                    signs(j + (u + 1) // XB, (u + 1) % XB)
                for g in range(G8):
                    act.wait_ge(s_mm, 1 + G8 * n + g + 1)
                    act.activation(h_chunk(n, g), bank[:, g, :], ACT.Copy).then_inc(s_h, 1)

            quads(act, conv_out)
            act.wait_ge(s_t2, 2)

            def normalised(s, t):
                if t == 0 and not s.kept:
                    act.wait_ge(d_z[s.slot], 1 + 16 * CT * s.turn)
                if not s.first:
                    act.wait_ge(s_p, 1 + CT * (s.place - 1) + t + 1)
                act.activation(u_[:, t, :], xs[:, s.slot, t, :], ACT.Identity, scale=r_g[:, bass.ds(s.image, 1), t],
                               bias=t_g[:, bass.ds(s.image, 1), t]).then_inc(s_u, 1)

            def image(s):
                if s.first:
                    normalised(s, 0)
                for t in range(CT):
                    if t < CT - 1:
                        normalised(s, t + 1)
                    elif s.following() is not None:
                        normalised(s.following(), 0)
                    act.wait_ge(s_v, 1 + CT * s.place + t + 1)
                    if not s.first:
                        act.wait_ge(s_o, 1 + CT * (s.place - 1) + t + 1)
                    act.activation(p_[:, t, :], u_[:, t, :], ACT.Relu, scale=-1.0).then_inc(s_q, 1)

            output_order(act, image)

        @block.tensor
        def _(pe):
            pe.wait_ge(s_gs, 2)
            pe.matmul(bank[:, 7, 0:N], group_avg[:], flat(cm), start=True, stop=True).then_inc(s_gm, 1)
            pe.wait_ge(s_gs, 3)
            pe.matmul(bank[:, 7, 64:64 + N], group_avg[:], flat(sa), start=True, stop=True).then_inc(s_gm, 1)
            pe.wait_ge(s_wb, 5)
            pe.wait_ge(s_eps, 2)

            def image(j, u, left):
                n = 2 * j + u
                for g in range(G8):
                    t, c = g // NC, g % NC
                    pe.wait_ge(s_h, 1 + G8 * n + g + 1)
                    pe.wait_ge(s_sg, 1 + CT * n + t + 1)
                    for k in range(TAPS):
                        dy, dx = k // 3, k % 3
                        mm = pe.matmul(bank[:, g, :].rearrange("p (r c) -> p r c", c=W), wb[:, t, k, :],
                                       sg[:, u, t, dy + ROWS * c:dy + ROWS * (c + 1), dx:dx + W],
                                       start=k == 0, stop=k == TAPS - 1)
                    mm.then_inc(s_mm, 1)

            images(pe, B, image)


def kernel(x, L0_conv_cv1_w, L0_conv_cv1_bn, L0_conv_cv2_w, L0_conv_cv2_bn, L0_conv_m_cv1_w, L0_conv_m_cv1_bn,
           L0_conv_m_qkv_w, L0_conv_m_rw, L0_conv_m_rh, L0_conv_m_cv2_w, L0_conv_m_cv2_bn, L1_conv_conv_w,
           L1_conv_bn1_gamma, L1_conv_bn1_beta, L1_conv_bn2_gamma, L1_conv_bn2_beta, L1_conv_prelu_a):
    import numpy as np
    import concourse.bacc as bacc
    from concourse.bass_utils import run_bass_kernel_spmd as run

    x = np.ascontiguousarray(x)
    shape = x.shape
    B, C = shape[0], shape[1]

    def cols(a):
        a = np.asarray(a)
        return np.moveaxis(a.reshape(a.shape[:-1] + (-1, P)), -1, 0)

    def conv_t(w):
        w = np.asarray(w)
        o, i = w.shape[:2]
        w = w.reshape(o, i // P, P, -1)
        return w.transpose(2, 1, 3, 0).reshape(P, -1)

    cv1_bn, cv2_bn = cols(L0_conv_cv1_bn), cols(L0_conv_cv2_bn)
    m1_bn, m2_bn = cols(L0_conv_m_cv1_bn), cols(L0_conv_m_cv2_bn)
    bn0 = np.concatenate([cv1_bn, cv2_bn] + [q[:, l] for l in range(2) for q in (m1_bn, m2_bn)], axis=2)
    qkv = np.asarray(L0_conv_m_qkv_w).reshape(2, 12, HD, 256)
    qkv = qkv[:, [0, 1, 2, 3, 4, 5, 6, 7, 8, 10, 9, 11]].reshape(2, 768, 256)
    w3 = np.asarray(L0_conv_m_cv1_w)
    wm = np.asarray(L0_conv_m_cv2_w)
    cv2 = conv_t(L0_conv_cv2_w)
    cv2 = np.concatenate([cv2, np.zeros((P, WBN - cv2.shape[1]), cv2.dtype)], axis=1)
    w_b = np.stack([np.concatenate([conv_t(w3[l].reshape(256, 256, 9)), conv_t(qkv[l]), conv_t(wm[l])], axis=1)
                    for l in range(2)] + [cv2])

    def rel(r):
        r = np.asarray(r).reshape(2, 2, P, W)
        return r.transpose(0, 2, 1, 3)

    w1 = np.asarray(L1_conv_conv_w).reshape(C // P, P, 32, 9)
    w1_rows = w1.reshape(C // P, P, 288).transpose(1, 0, 2)
    w1_t = w1.reshape(C // P, 4, 32, 32, 9).transpose(1, 3, 0, 4, 2).reshape(P, C // P, 9, 32)
    bn1 = np.stack([cols(v) for v in (L1_conv_bn1_gamma, L1_conv_bn1_beta, L1_conv_bn2_gamma, L1_conv_bn2_beta,
                                      L1_conv_prelu_a)], axis=1)
    data = {
        "x": x.reshape(B, C, HW), "w_cv1": conv_t(L0_conv_cv1_w), "w_b": w_b,
        "bn0": bn0, "rw": rel(L0_conv_m_rw), "rh": rel(L0_conv_m_rh), "w1_rows": w1_rows, "w1_t": w1_t, "bn1": bn1,
    }
    data = {k: np.ascontiguousarray(v) for k, v in data.items()}
    nc = bacc.Bacc("TRN2", target_bir_lowering=False, num_devices=1)
    args = [nc.dram_tensor(k, v.shape, mybir.dt.from_np(v.dtype), kind="ExternalInput").ap() for k, v in data.items()]
    out = nc.dram_tensor("out", (B, C, HW), F32, kind="ExternalOutput").ap()
    program(nc, *args, out)
    result = run(nc, [data], core_ids=[0])
    return result.results[0]["out"].reshape(shape)
```

```python
from contextlib import ExitStack

import concourse.bass as bass
from concourse import mybir

P = 128
F32 = mybir.dt.float32
F32R = mybir.dt.float32r
F16 = mybir.dt.float16
BF16 = mybir.dt.bfloat16
ACT = mybir.ActivationFunctionType
ALU = mybir.AluOpType
AX = mybir.AxisListType

HW, W = 1024, 32
NB = 512
NC = HW // NB
ROWS = NB // W
PW = W + 2
HEADS, HD = 4, 64
SCALE = float(HD) ** -0.5
BN0_EPS, GN_EPS, BN1_EPS = 1e-3, 1e-5, 1e-5
TAPS = 9
KT = 2
W3N, WQN, WMN = KT * TAPS * 256, KT * 768, KT * 256
WBN = W3N + WQN + WMN
PIECE = 512
LEAD, STEP = [20, 22], [3, 3]


def tap_window(t, c, trim_columns=False):
    dy, dx = t // 3, t % 3
    r0 = 1 if dy == 0 and c == 0 else 0
    r1 = ROWS - 1 if dy == 2 and c == NC - 1 else ROWS
    c0, c1 = 0, W
    if trim_columns:
        c0, c1 = (1 if dx == 0 else 0), (W - 1 if dx == 2 else W)
    return (slice(r0, r1), slice(c0, c1),
            (slice(dy + ROWS * c + r0, dy + ROWS * c + r1), slice(dx + c0, dx + c1)))


def f32(ap):
    return ap.bitcast(F32)


def start_at_one(nc, sems):
    with nc.Block() as block:
        for k, engine in enumerate((block.sync, block.gpsimd, block.scalar, block.vector, block.tensor)):
            @engine
            def _(eng, k=k):
                for s in sems[k::5]:
                    eng.sem_inc(s, 1)


def alone(eng, sem):
    eng.sem_inc(sem, 1)


def images(eng, n_img, body):
    if n_img > 2:
        with eng.Fori(0, n_img // 2 - 1) as j:
            body(j, 0, 2)
            body(j, 1, 2)
    body(n_img // 2 - 1, 0, 1)
    body(n_img // 2 - 1, 1, 0)


class Split:

    def __init__(self, d_stage, s_hi, s_lo, stage):
        self.d_stage, self.s_hi, self.s_lo, self.stage = d_stage, s_hi, s_lo, stage
        self.pieces = []

    def add(self, dram, w_hi, w_lo, lo, hi):
        first = len(self.pieces)
        for a in range(lo, hi, PIECE):
            b = min(hi, a + PIECE)
            self.pieces.append((dram[:, a:b], w_hi[:, a:b], w_lo[:, a:b], b - a))
        return range(first, len(self.pieces))

    def load(self, queue, i):
        src, _, _, n = self.pieces[i]
        if i >= 2:
            queue.wait_ge(self.s_lo, 1 + i - 1)
        queue.dma_start(self.stage[:, i % 2, 0:n], src).then_inc(self.d_stage[i % 2], 16)

    def high(self, act, i):
        _, w_hi, _, n = self.pieces[i]
        act.wait_ge(self.d_stage[i % 2], 1 + 16 * (i // 2 + 1))
        act.activation(w_hi, self.stage[:, i % 2, 0:n], ACT.Copy).then_inc(self.s_hi, 1)

    def low(self, dve, i):
        _, w_hi, w_lo, n = self.pieces[i]
        dve.wait_ge(self.s_hi, 1 + i + 1)
        dve.tensor_tensor(w_lo, self.stage[:, i % 2, 0:n], f32(w_hi), ALU.subtract).then_inc(self.s_lo, 1)


def program(nc, x, w_cv1, w_b, bn0, rw, rh, w1_rows, w1_t, bn1, out):
    B = x.shape[0]
    CT = x.shape[1] // P
    x_v = x.rearrange("b (t p) n -> b t p n", p=P)
    out_v = out.rearrange("b (t p) n -> b t p n", p=P)
    y_d = nc.dram_tensor("y_d", (B, 8, P, HW), F32, kind="Internal").ap()
    x1_d = nc.dram_tensor("x1_d", (B, CT, P, HW), F32, kind="Internal").ap()
    rs_d = nc.dram_tensor("rs_d", (1, HW), F32, kind="Internal").ap()

    with ExitStack() as top:
        def keep(name, shape, dt):
            return top.enter_context(nc.sbuf_tensor(name, shape, dt))

        bank = top.enter_context(nc.psum_tensor("bank", [P, 8, NB], F32))
        bn_s = keep("bn_s", [P, 16], F32)
        bn_o = keep("bn_o", [P, 16], F32)
        group_avg = keep("group_avg", [P, P], F32)
        mhalf = keep("mhalf", [P, 4 * B], F32)
        x1_mv = keep("x1_mv", [P, B, CT, 2], F32)

        weights = ExitStack()
        w_hi = weights.enter_context(nc.sbuf_tensor("w_hi", [P, WBN], F32R))
        w_lo = weights.enter_context(nc.sbuf_tensor("w_lo", [P, WBN], F32R))
        sems = []

        def sem(name):
            sems.append(top.enter_context(nc.semaphore(name)))
            return sems[-1]

        layer0 = [
            phase_a(nc, sem, B, CT, x_v, w_cv1, w_b, w_hi, w_lo, bn0, y_d, bank, bn_s, bn_o, group_avg, mhalf),
            phase_b(nc, sem, B, w_b, w_hi, w_lo, rw, rh, y_d, rs_d, bank, bn_s, bn_o),
            phase_d(nc, sem, B, CT, x_v, w_hi, w_lo, y_d, x1_d, bank, bn_s, bn_o, x1_mv),
        ]
        layer1 = phase_l(nc, sem, B, CT, w1_rows, w1_t, bn1, x1_d, out_v, bank, group_avg, mhalf, x1_mv)
        for phase in layer0 + [layer1]:
            next(phase)
        start_at_one(nc, sems)
        with weights:
            for phase in layer0:
                next(phase, None)
        next(layer1, None)


def phase_a(nc, sem_, B, CT, x_v, w_cv1, w_b, wb_hi, wb_lo, bn0, y_d, bank, bn_s, bn_o, group_avg, mhalf):
    def sem(name):
        return sem_("a_" + name)

    d_bn = sem("d_bn")
    s_spare = sem("s_spare")
    d_stage = [sem(f"d_stage{i}") for i in range(2)]
    s_whi, s_wlo = sem("s_whi"), sem("s_wlo")
    d_x = [sem(f"d_x{i}") for i in range(2)]
    s_chain = sem("s_chain")
    s_setup = sem("s_setup")
    s_eps, s_rs = sem("s_eps"), sem("s_rs")
    s_mv, s_gm, s_dev, s_gv = sem("s_mv"), sem("s_gm"), sem("s_dev"), sem("s_gv")
    s_xf, s_xh, s_xl = sem("s_xf"), sem("s_xh"), sem("s_xl")
    s_mm, s_y = sem("s_mm"), sem("s_y")
    d_y = [sem(f"d_y{i}") for i in range(4)]
    yield

    with ExitStack() as ctx:
        def sb(name, shape, dt):
            return ctx.enter_context(nc.sbuf_tensor("a_" + name, shape, dt))

        w_hi = sb("w_hi", [P, CT * 512], F32R)
        w_lo = sb("w_lo", [P, CT * 512], F32R)
        stage = sb("stage", [P, 2, PIECE], F32)
        bn_in = sb("bn_in", [P, 4, 16], F32)
        bn_t = sb("bn_t", [P, 2, 16], F32)
        xin = sb("xin", [P, 2, CT, HW], F32)
        xh = sb("xh", [P, 2, CT, HW], F32R)
        xl = sb("xl", [P, 2, CT, HW], F32R)
        stats = sb("stats", [P, CT, NC, 6], F32)
        mv = sb("mv", [P, CT, 2], F32)
        dev = sb("dev", [P, CT], F32)
        gm = sb("gm", [P, CT], F32)
        var = sb("var", [P, CT], F32)
        rg = sb("rg", [P, CT], F32)
        sh = sb("sh", [P, CT], F32)
        y_sb = sb("y_sb", [P, 4, NB], F32)

        G8 = CT * NC
        SLOTS = 4
        stat_bank = 7
        split = Split(d_stage, s_whi, s_wlo, stage)
        own = split.add(w_cv1, w_hi, w_lo, 0, CT * 512)
        ahead = split.add(w_b[0], wb_hi, wb_lo, 0, W3N)

        LATE = 2

        def piece_at(left, g, late=0):
            k = (1 - left) * G8 + g - (2 * G8 - len(ahead) - LATE) - late
            return ahead[k] if left < 2 and 0 <= k < len(ahead) else None

        block = ctx.enter_context(nc.Block())

        @block.sync
        def _(sp):
            sp.dma_start(bn_in[:], bn0).then_inc(d_bn, 16)
            for t in range(CT):
                sp.dma_start(xin[:, 0, t, :], x_v[0, t]).then_inc(d_x[0], 16)
            for i in own:
                split.load(sp, i)
            for t in range(CT):
                sp.dma_start(xin[:, 1, t, :], x_v[1, t]).then_inc(d_x[1], 16)

            def image(j, u, left):
                n = 2 * j + u
                if left == 2:
                    sp.wait_ge(s_xl, 1 + CT * (n + 1))
                    alone(sp, s_spare)
                    for t in range(CT):
                        sp.dma_start(xin[:, u, t, :], x_v[n + 2, t]).then_inc(d_x[u], 16)
                for g in range(G8):
                    sp.wait_ge(s_y, 1 + SLOTS + G8 * n + g + 1)
                    alone(sp, s_spare)
                    sp.dma_start(y_d[n, g // NC][:, (g % NC) * NB:(g % NC + 1) * NB],
                                 y_sb[:, g % SLOTS, :]).then_inc(d_y[g % SLOTS], 16)
                    if piece_at(left, g) is not None:
                        split.load(sp, piece_at(left, g))

            images(sp, B, image)
            for i in range(SLOTS):
                sp.wait_ge(d_y[i], 1 + 16 * B * G8 // SLOTS)

        @block.gpsimd
        def _(pool):
            pool.memset(mhalf[:], -0.5).then_inc(s_setup, 1)
            pool.memset(group_avg[:], 1.0 / 16).then_inc(s_setup, 1)
            pool.wait_ge(s_setup, 3)
            g3 = group_avg[:].rearrange("p (g c) -> p g c", c=16)
            pool.affine_select(out=g3, in_=g3, compare_op=ALU.is_ge, fill=0.0, base=0,
                               pattern=[[-16, 8], [0, 16]], channel_multiplier=1).then_inc(s_setup, 1)
            pool.wait_ge(s_setup, 4)
            pool.affine_select(out=g3, in_=g3, compare_op=ALU.is_ge, fill=0.0, base=15,
                               pattern=[[16, 8], [0, 16]], channel_multiplier=-1).then_inc(s_setup, 1)
            pool.wait_ge(s_eps, 2)
            pool.tensor_tensor(bn_t[:, 1, :], bn_t[:, 0, :], mhalf[:, 0:16] if 4 * B >= 16 else mhalf[:, 0:1].to_broadcast([P, 16]),
                               ALU.pow).then_inc(s_rs, 1)

            def stat(n):
                pool.wait_ge(s_eps, 1 + n + 2)
                pool.wait_ge(s_xf, 1 + CT * n)
                pool.tensor_tensor(rg[:], var[:], mhalf[:, 0:CT], ALU.pow).then_inc(s_rs, 1)

            stat(0)
            images(pool, B, lambda j, u, left: stat(2 * j + u + 1) if left else None)

        @block.vector
        def _(dve):
            links = [0]

            def link(ins):
                links[0] += 1
                ins.then_inc(s_chain, 1)
                dve.wait_ge(s_chain, 1 + links[0])

            dve.wait_ge(d_bn, 17)
            dve.tensor_scalar(bn_t[:, 0, :], bn_in[:, 3, :], BN0_EPS, None, ALU.add).then_inc(s_eps, 1)
            dve.wait_ge(s_rs, 2)
            link(dve.tensor_tensor(bn_s[:], bn_in[:, 0, :], bn_t[:, 1, :], ALU.mult))
            link(dve.tensor_tensor(bn_t[:, 0, :], bn_in[:, 2, :], bn_s[:], ALU.mult))
            link(dve.tensor_tensor(bn_o[:], bn_in[:, 1, :], bn_t[:, 0, :], ALU.subtract))
            LINKS = 4
            base = links[0]

            def statistics(n, pairs, u, early=(), late=()):
                dve.wait_ge(d_x[u], 1 + 16 * CT * pairs)
                c = base + LINKS * n
                for t in range(CT):
                    for k in range(NC):
                        ins = dve.bn_stats(stats[:, t, k, :], xin[:, u, t, k * NB:(k + 1) * NB])
                ins.then_inc(s_chain, 1)
                dve.wait_ge(s_chain, 1 + c + 1)
                alone(dve, s_spare)
                for t in range(CT):
                    ins = dve.bn_aggr(mv[:, t, :], stats[:, t, :, :])
                ins.then_inc(s_mv, 1)
                for i in early:
                    split.low(dve, i)
                dve.wait_ge(s_gm, 1 + n + 1)
                dve.tensor_copy(gm[:], bank[:, stat_bank, 0:CT]).then_inc(s_chain, 1)
                dve.wait_ge(s_chain, 1 + c + 2)
                dve.tensor_tensor(dev[:], mv[:, :, 0], gm[:], ALU.subtract).then_inc(s_chain, 1)
                dve.wait_ge(s_chain, 1 + c + 3)
                dve.tensor_tensor(sh[:], dev[:], dev[:], ALU.mult).then_inc(s_chain, 1)
                dve.wait_ge(s_chain, 1 + c + 4)
                dve.tensor_tensor(dev[:], mv[:, :, 1], sh[:], ALU.add).then_inc(s_dev, 1)
                dve.wait_ge(s_gv, 1 + n + 1)
                dve.tensor_scalar(var[:], bank[:, stat_bank, 8:8 + CT], GN_EPS, None, ALU.add).then_inc(s_eps, 1)
                dve.wait_ge(s_rs, 1 + n + 2)
                for t in range(CT):
                    dve.tensor_scalar(xin[:, u, t, :], xin[:, u, t, :], gm[:, t:t + 1], rg[:, t:t + 1],
                                      ALU.subtract, ALU.mult).then_inc(s_xf, 1)
                for t in range(CT):
                    dve.wait_ge(s_xh, 1 + CT * n + t + 1)
                    dve.tensor_tensor(xl[:, u, t, :], xin[:, u, t, :], f32(xh[:, u, t, :]),
                                      ALU.subtract).then_inc(s_xl, 1)
                    if t < len(late):
                        split.low(dve, late[t])

            statistics(0, 1, 0, early=own[:2], late=own[2:])
            images(dve, B, lambda j, u, left: statistics(2 * j + u + 1, j + u + 1, 1 - u) if left else None)
            for i in ahead:
                split.low(dve, i)

        @block.scalar
        def _(act):
            def high(n, u, late=()):
                for t in range(CT):
                    act.wait_ge(s_xf, 1 + CT * n + t + 1)
                    act.activation(xh[:, u, t, :], xin[:, u, t, :], ACT.Copy).then_inc(s_xh, 1)
                    if t < len(late):
                        split.high(act, late[t])

            def group(n, j, u, g):
                m = g // NC
                act.wait_ge(s_mm, 1 + G8 * n + g + 1)
                act.wait_ge(d_y[g % SLOTS], 1 + 32 * n + 16 * (g // SLOTS))
                act.activation(y_sb[:, g % SLOTS, :], bank[:, g % SLOTS, :], ACT.Silu, scale=bn_s[:, m:m + 1],
                               bias=bn_o[:, m:m + 1]).then_inc(s_y, 1)

            act.sem_inc(s_y, SLOTS)
            for i in own[:2]:
                split.high(act, i)
            high(0, 0, own[2:])
            act.wait_ge(s_chain, 4)

            def image(j, u, left):
                n = 2 * j + u
                for g in range(G8):
                    group(n, j, u, g)
                    if piece_at(left, g, LATE) is not None:
                        split.high(act, piece_at(left, g, LATE))
                    if g == 2 and left:
                        act.wait_ge(s_mm, 1 + G8 * n)
                        high(n + 1, 1 - u)

            images(act, B, image)

        @block.tensor
        def _(pe):
            def mean(n):
                pe.wait_ge(s_mv, 1 + n + 1)
                pe.matmul(bank[:, stat_bank, 0:CT], group_avg[:], mv[:, :, 0], start=True, stop=True).then_inc(s_gm, 1)

            def variance(n):
                pe.wait_ge(s_dev, 1 + n + 1)
                pe.matmul(bank[:, stat_bank, 8:8 + CT], group_avg[:], dev[:], start=True, stop=True).then_inc(s_gv, 1)

            def group(n, u, g):
                m, c = g // NC, g % NC
                pe.wait_ge(s_y, 1 + G8 * n + g + 1)
                px = slice(c * NB, (c + 1) * NB)
                ps = bank[:, g % SLOTS, :]
                for k in range(CT):
                    wk = slice(k * 512 + m * P, k * 512 + (m + 1) * P)
                    if g == 0:
                        pe.wait_ge(s_xl, 1 + CT * n + k + 1)
                        pe.wait_ge(s_wlo, 1 + own[k] + 1)
                    pe.matmul(ps, w_hi[:, wk], xh[:, u, k, px], start=k == 0, stop=False)
                    pe.matmul(ps, w_hi[:, wk], xl[:, u, k, px], start=False, stop=False)
                    mm = pe.matmul(ps, w_lo[:, wk], xh[:, u, k, px], start=False, stop=k == CT - 1)
                mm.then_inc(s_mm, 1)

            pe.wait_ge(s_setup, 5)
            mean(0)
            variance(0)
            def image(j, u, left):
                n = 2 * j + u
                for g in range(G8):
                    group(n, u, g)
                    if left and g == 1:
                        mean(n + 1)
                    if left and g == 3:
                        variance(n + 1)

            images(pe, B, image)


def phase_b(nc, sem_, B, w_b, w_hi, w_lo, rw, rh, y_d, rs_d, bank, bn_s, bn_o):
    L = w_b.shape[0] - 1

    def sem(name):
        return sem_("b_" + name)

    def sem2(name):
        return [sem(name + "0"), sem(name + "1")]

    s_table = sem("s_table")
    d_w = sem2("d_w")
    s_whi, s_wlo = sem("s_whi"), sem("s_wlo")
    s_coef, d_r = sem("s_coef"), sem("d_r")
    s_const, s_const_rows = sem("s_const"), sem("s_const_rows")
    s_spare, s_spare_pool, s_spare_pe = sem("s_spare"), sem("s_spare_pool"), sem("s_spare_pe")
    d_y = sem2("d_y")
    s_yhi, s_ylo = sem("s_yhi"), sem("s_ylo")
    s_cv, s_raw, s_zf, s_zhi, s_zlo = sem("s_cv"), sem("s_raw"), sem("s_zf"), sem("s_zhi"), sem("s_zlo")
    s_qk, s_v = sem("s_qk"), sem("s_v")
    s_qhi, s_qlo = sem("s_qhi"), sem("s_qlo")
    s_kr, s_kf, s_khi, s_klo = sem("s_kr"), sem("s_kf"), sem("s_khi"), sem("s_klo")
    d_qq, d_k1, d_m = sem2("d_qq"), sem2("d_k1"), sem2("d_m")
    s_vhi, s_vlo = sem("s_vhi"), sem("s_vlo")
    s_mx, s_mr = sem("s_mx"), sem("s_mr")
    s_lt, s_af, s_ah, s_al = sem("s_lt"), sem("s_af"), sem("s_ah"), sem("s_al")
    s_avh, s_avl = sem("s_avh"), sem("s_avl")
    s_os, d_s8, s_rc, d_rc, d_rb = sem("s_os"), sem("d_s8"), sem("s_rc"), sem("d_rc"), sem("d_rb")
    s_om, s_ohi, s_olo = sem("s_om"), sem("s_ohi"), sem("s_olo")
    s_cm, s_cf = sem("s_cm"), sem("s_cf")
    d_res, s_res, d_out = sem2("d_res"), sem("s_res"), sem2("d_out")
    yield

    with ExitStack() as ctx:
        def sb(name, shape, dt):
            return ctx.enter_context(nc.sbuf_tensor("b_" + name, shape, dt))

        coef = sb("coef", [P, 2, 4], F32)
        rws = sb("rws", [P, 2, W], F32)
        rhs = sb("rhs", [P, 2, W], F32)
        y_in = sb("y_in", [P, KT, HW], F32)
        yp_h = sb("yp_h", [P, KT, PW, PW], F32R)
        yp_l = sb("yp_l", [P, KT, PW, PW], F32R)
        z_h = sb("z_h", [P, KT, HW], F32R)
        z_l = sb("z_l", [P, KT, HW], F32R)
        zf = sb("zf", [P, 2, NB], F32)
        kf = sb("kf", [P, HW], F32)
        qq = sb("qq", [P, 2, HW], F32R)
        qm = sb("qm", [P, 2, HW], F32R)
        kk = sb("kk", [P, 2, HW], F32R)
        k1 = sb("k1", [P, 2, HW], F32R)
        v_h = sb("v_h", [P, 8, 2, 3, HD], F32R)
        v_l = sb("v_l", [P, 8, 2, 3, HD], F32R)
        a_f = sb("a_f", [P, 2, HW], F32)
        a_h = sb("a_h", [P, 2, HW], F32R)
        a_l = sb("a_l", [P, 2, HW], F32R)
        mt = sb("mt", [P, 2, 8], F32R)
        os = sb("os", [P, HW], F32)
        r8 = sb("r8", [P, 8], F32)
        r8i = sb("r8i", [P, 8], F32)
        rb = kf
        o_h = sb("o_h", [P, KT, HW], F32R)
        o_l = sb("o_l", [P, KT, HW], F32R)
        res = sb("res", [P, 2, NB], F32)

        zero = sb("zero", [P, 2], F32)

        N_OWN, N_NEXT = (WBN - W3N) // PIECE, W3N // PIECE
        N_ALL = N_OWN + N_NEXT
        w3 = lambda w: w[:, 0:W3N].rearrange("p (k t c) -> p k t c", k=KT, t=TAPS)
        wq = lambda w: w[:, W3N:W3N + WQN].rearrange("p (k c) -> p k c", k=KT)
        wm = lambda w: w[:, W3N + WQN:WBN].rearrange("p (k c) -> p k c", k=KT)
        w3h, w3l, wqh, wql, wmh, wml = w3(w_hi), w3(w_lo), wq(w_hi), wq(w_lo), wm(w_hi), wm(w_lo)

        W_SLOT = [N_ALL - N_ALL // 2, N_ALL // 2]

        def piece(i):
            if i < N_OWN:
                return slice(W3N + i * PIECE, W3N + (i + 1) * PIECE), res[:, i % 2, :]
            return slice((i - N_OWN) * PIECE, (i - N_OWN + 1) * PIECE), y_in[:, i % 2, 0:PIECE]

        NEXT_AT = {(1, 2): 4, (1, 3): 5, (1, 4): 6, (1, 5): 7, (1, 6): 8, (3, 2): 9, (3, 3): 10, (3, 4): 11, (3, 5): 12}
        assert sorted(NEXT_AT.values()) == list(range(N_OWN, N_ALL))

        def load_piece(sp, l, l_w, i):
            cols, stage = piece(i)
            if i >= 2:
                sp.wait_ge(s_wlo, 1 + N_ALL * l + i - 1)
            alone(sp, s_spare)
            sp.dma_start(stage, w_b[bass.ds(l_w, 1), :, cols].rearrange("o p n -> (o p) n")).then_inc(d_w[i % 2], 16)

        def piece_high(act, l, i):
            cols, stage = piece(i)
            act.wait_ge(d_w[i % 2], 1 + 16 * (i // 2 + 1) + 16 * W_SLOT[i % 2] * l)
            act.activation(w_hi[:, cols], stage, ACT.Copy).then_inc(s_whi, 1)

        def piece_low(dve, l, i):
            cols, stage = piece(i)
            dve.wait_ge(s_whi, 1 + N_ALL * l + i + 1)
            dve.tensor_tensor(w_lo[:, cols], stage, f32(w_hi[:, cols]), ALU.subtract).then_inc(s_wlo, 1)

        def own(h):
            return slice(HD * (h % 2), HD * (h % 2) + HD)

        def other(h):
            return own(h + 1)

        def first_other(h):
            return slice(HD * (1 - h % 2), HD * (1 - h % 2) + 1)

        def px(c):
            return slice(c * NB, (c + 1) * NB)

        def two(b0):
            return bank[:, b0:b0 + 2, :].rearrange("p a n -> p (a n)")

        def layers(eng, start, image):
            with eng.Fori(0, L) as l:
                start(l)
                if B > 2:
                    with eng.Fori(0, B - 2) as b:
                        image(l * B + b, l, b, True, True)
                image(l * B + B - 2, l, B - 2, True, False)
                image(l * B + B - 1, l, B - 1, False, False)

        block = ctx.enter_context(nc.Block())

        @block.tensor
        def _(pe):
            CONV_BANK = [2, 3, 4, 5]

            def conv_terms(g):
                c, m = g // 2, g % 2
                co = slice(m * P, (m + 1) * P)
                terms = []
                for k in range(KT):
                    for t in (4, 0, 1, 2, 3, 5, 6, 7, 8) if k < KT - 1 else (0, 1, 2, 3, 5, 6, 7, 8, 4):
                        rows, cols, win = tap_window(t, c)
                        for w, yp in ((w3h, yp_h), (w3h, yp_l), (w3l, yp_h)):
                            terms.append((rows, cols, w[:, k, t, co], yp[(slice(None), k) + win]))
                return terms

            def conv(i, g, lo, hi):
                terms = conv_terms(g)
                ps = bank[:, CONV_BANK[g], :].rearrange("p (r c) -> p r c", c=W)
                if lo == 0:
                    pe.wait_ge(s_yhi, 1 + KT * (i + 1))
                    pe.wait_ge(s_ylo, 1 + KT * (i + 1))
                for n in range(lo, min(hi, len(terms))):
                    rows, cols, w, y = terms[n]
                    mm = pe.matmul(ps[:, rows, cols], w, y, start=n == 0, stop=n == len(terms) - 1)
                if lo < len(terms) <= hi:
                    mm.then_inc(s_cv, 1)

            def start(l):
                pe.wait_ge(s_whi, 1 + N_ALL * l)
                pe.wait_ge(s_wlo, 1 + N_ALL * l)
                pe.wait_ge(s_cf, 1 + 4 * B * l)
                pe.wait_ge(s_mr, 1 + 32 * B * l)
                for g in range(4):
                    conv(l * B, g, 0, 54)
                pe.wait_ge(s_const, 3)
                pe.wait_ge(s_const_rows, 3)
                pe.wait_ge(s_whi, 1 + N_ALL * l + N_OWN)
                pe.wait_ge(s_wlo, 1 + N_ALL * l + N_OWN)
                alone(pe, s_spare_pe)

            def qk(it, p, part, c):
                if c == 0 and p == 0:
                    pe.wait_ge(s_cf, 1 + 4 * it)
                elif c == 0:
                    pe.wait_ge(s_af, 1 + 32 * it + 15 + part)
                    pe.wait_ge(s_ah, 1 + 32 * it + 15 + part)
                co = slice(part * 256 + p * P, part * 256 + (p + 1) * P)
                ps = bank[:, 2 * part + c, :]
                for k in range(KT):
                    pe.matmul(ps, wqh[:, k, co], z_h[:, k, px(c)], start=k == 0, stop=False)
                    pe.matmul(ps, wqh[:, k, co], z_l[:, k, px(c)], start=False, stop=False)
                    mm = pe.matmul(ps, wql[:, k, co], z_h[:, k, px(c)], start=False, stop=k == KT - 1)
                if c == NC - 1:
                    mm.then_inc(s_qk, 1)

            def values(it, half):
                if half == 0:
                    pe.wait_ge(s_zhi, 1 + 4 * (it + 1))
                    pe.wait_ge(s_zlo, 1 + 4 * (it + 1))
                    pe.wait_ge(s_os, 1 + 4 * it)
                else:
                    pe.wait_ge(s_mr, 1 + 32 * it)
                for jb in range(4):
                    j = slice((4 * half + jb) * P, (4 * half + jb + 1) * P)
                    ps = bank[:, (6 if half == 0 else 4) + jb // 2, (jb % 2) * 256:(jb % 2 + 1) * 256]
                    for k in range(KT):
                        pe.matmul(ps, z_h[:, k, j], wqh[:, k, 512:768], start=k == 0, stop=False)
                        pe.matmul(ps, z_h[:, k, j], wql[:, k, 512:768], start=False, stop=False)
                        mm = pe.matmul(ps, z_l[:, k, j], wqh[:, k, 512:768], start=False, stop=k == KT - 1)
                mm.then_inc(s_v, 1)

            def max_block(it, h, n, b0):
                for c in range(NC):
                    mm = pe.matmul(bank[:, b0 + c, :], qq[:, h % 2, n:HW:8], kk[:, h % 2, px(c)], start=True, stop=True)
                mm.then_inc(s_mx, 1)

            def logits(it, h, t):
                b0 = 2 * (t % 2)
                if t >= 2 or h % 2 == 1:
                    pe.wait_ge(s_af, 1 + 32 * it + 8 * h + t - 1)
                    pe.wait_ge(s_ah, 1 + 32 * it + 8 * h + t - 1)
                j = slice(t * P, (t + 1) * P)
                for c in range(NC):
                    pe.matmul(bank[:, b0 + c, :], kk[:, h % 2, j], qq[:, h % 2, px(c)], start=True, stop=False)
                if t == 0:
                    pe.wait_ge(s_qlo, 1 + 4 * it + h + 1)
                    pe.wait_ge(d_k1[h % 2], 1 + 16 * (2 * it + h // 2 + 1))
                    pe.wait_ge(d_m[h % 2], 1 + 16 * (2 * it + h // 2 + 1))
                for c in range(NC):
                    mm = pe.matmul(bank[:, b0 + c, :], k1[:, h % 2, j], qm[:, h % 2, px(c)], start=False, stop=True)
                mm.then_inc(s_lt, 1)

            def weighted_high(it, h, t):
                if h % 2 == 0:
                    vl, rows = v_l[:, t, h // 2, 0, :], slice(0, HD)
                else:
                    vl, rows = v_l[:, t, h // 2, 1:3, :].rearrange("p s c -> p (s c)"), slice(0, P)
                vh = v_h[:, t, h // 2, h % 2:h % 2 + 2, :].rearrange("p s c -> p (s c)")
                pe.wait_ge(s_ah, 1 + 32 * it + 8 * h + t + 1)
                for c in range(NC):
                    pe.matmul(bank[:, 6 + c, :], vh, a_h[:, t % 2, px(c)], start=t == 0, stop=False)
                for c in range(NC):
                    mm = pe.matmul(bank[rows, 6 + c, :], vl, a_h[:, t % 2, px(c)], start=False, stop=False)
                mm.then_inc(s_avh, 1)

            def weighted_low(it, h, t):
                vh = v_h[:, t, h // 2, h % 2:h % 2 + 2, :].rearrange("p s c -> p (s c)")
                pe.wait_ge(s_al, 1 + 32 * it + 8 * h + t + 1)
                for c in range(NC):
                    mm = pe.matmul(bank[:, 6 + c, :], vh, a_l[:, t % 2, px(c)], start=False, stop=t == 7)
                mm.then_inc(s_avl, 1)

            def pair(it, p, filler, between=0):
                ha, hb = 2 * p, 2 * p + 1
                lead, step = LEAD[p], STEP[p]
                if filler:
                    pe.wait_ge(s_kf, 1 + 2 * it + p + 1)
                    conv(*filler, 0, lead)
                pe.wait_ge(d_qq[0], 1 + 16 * (2 * it + p + 1))
                pe.wait_ge(s_khi, 1 + 4 * it + ha + 1)
                pe.wait_ge(s_klo, 1 + 4 * it + ha + 1)
                for n in range(8):
                    m = 32 * it + 8 * ha + n
                    if n == 0:
                        pe.wait_ge(s_qhi, 1 + 4 * it + hb + 1)
                        pe.wait_ge(s_qlo, 1 + 4 * it + hb + 1)
                    elif n == 1 and p == 0:
                        pe.wait_ge(s_vhi, 1 + 2 * it + 1)
                        pe.wait_ge(s_vlo, 1 + 2 * it + 1)
                    elif n == 1:
                        pe.wait_ge(s_os, 1 + 4 * it + ha)
                    else:
                        pe.wait_ge(s_mr, 1 + m - 1)
                    max_block(it, ha, n, 0 if n % 2 == 0 else 6)
                    if filler:
                        conv(*filler, lead + n * step, lead + (n + 1) * step)

                def max_of_second(n):
                    if n == 0:
                        pe.wait_ge(d_qq[1], 1 + 16 * (2 * it + p + 1))
                        pe.wait_ge(s_khi, 1 + 4 * it + hb + 1)
                        pe.wait_ge(s_klo, 1 + 4 * it + hb + 1)
                        if p == 0:
                            pe.wait_ge(s_vhi, 1 + 2 * it + 2)
                            pe.wait_ge(s_vlo, 1 + 2 * it + 2)
                    else:
                        pe.wait_ge(s_mr, 1 + 32 * it + 8 * hb + n)
                    max_block(it, hb, n, 4)

                max_of_second(0)
                if filler:
                    conv(*filler, lead + 8 * step, 54)
                max_of_second(1)
                pe.wait_ge(s_mr, 1 + 32 * it + 8 * ha + 7)
                logits(it, ha, 0)
                pe.wait_ge(s_kf, 1 + 2 * it + p + 1)
                if filler:
                    pe.wait_ge(s_raw, 1 + 2 * (it + 1) + p + 1)
                for h in (ha, hb):
                    for t in range(8 if h == ha else 7):
                        if h == ha and 2 <= t <= 5:
                            max_of_second(t + 2)
                        if h == hb and t == 0:
                            weighted_low(it, ha, 7)
                        if t < 7:
                            logits(it, h, t + 1)
                        elif h == ha:
                            logits(it, hb, 0)
                        if t <= 1 and h == ha:
                            max_of_second(t + 2)
                        if t == 0 and h == ha:
                            pe.wait_ge(s_mr, 1 + 32 * it + 8 * ha + 8)
                        elif t == 0:
                            if between:
                                pe.wait_ge(s_mr, 1 + 32 * (it + 1))
                                conv(it + 1, 2, 0, between)
                            pe.wait_ge(s_os, 1 + 4 * it + h)
                        weighted_high(it, h, t)
                        if t > 0:
                            weighted_low(it, h, t - 1)

            def out_conv(it):
                pe.wait_ge(s_ohi, 1 + 4 * (it + 1))
                pe.wait_ge(s_olo, 1 + 4 * (it + 1))
                pe.wait_ge(s_af, 1 + 32 * (it + 1))
                pe.wait_ge(s_ah, 1 + 32 * (it + 1))
                for g in range(4):
                    c, co = g // 2, slice((g % 2) * P, (g % 2 + 1) * P)
                    for k in range(KT):
                        pe.matmul(bank[:, g, :], wmh[:, k, co], o_h[:, k, px(c)], start=k == 0, stop=False)
                        pe.matmul(bank[:, g, :], wmh[:, k, co], o_l[:, k, px(c)], start=False, stop=False)
                        mm = pe.matmul(bank[:, g, :], wml[:, k, co], o_h[:, k, px(c)], start=False, stop=k == KT - 1)
                    mm.then_inc(s_cm, 1)

            def image(it, l, b, has_next, has_next2):
                values(it, 0)
                for part in (1, 0):
                    for c in range(NC):
                        qk(it, 0, part, c)
                values(it, 1)
                pair(it, 0, (it + 1, 0) if has_next else None)
                qk(it, 1, 0, 0)
                weighted_high(it, 1, 7)
                weighted_low(it, 1, 6)
                qk(it, 1, 1, 0)
                weighted_low(it, 1, 7)
                qk(it, 1, 1, 1)
                qk(it, 1, 0, 1)
                pair(it, 1, (it + 1, 1) if has_next else None, 4 if has_next else 0)
                if has_next:
                    conv(it + 1, 2, 4, 9)
                weighted_high(it, 3, 7)
                weighted_low(it, 3, 6)
                if has_next:
                    conv(it + 1, 2, 9, 14)
                weighted_low(it, 3, 7)
                if has_next:
                    conv(it + 1, 2, 14, 54)
                    conv(it + 1, 3, 0, 54)
                out_conv(it)

            layers(pe, start, image)

        @block.scalar
        def _(act):
            def z_raw(i, g):
                act.wait_ge(s_cv, 1 + 4 * i + g + 1)
                act.wait_ge(s_zlo, 1 + 4 * i)
                act.activation(zf[:, g, :], bank[:, 2 + g, :], ACT.Copy).then_inc(s_raw, 1)

            def z_silu(i, g):
                m = g % 2
                if g < 2:
                    act.wait_ge(s_raw, 1 + 2 * i + g + 1)
                    src = zf[:, g, :]
                else:
                    act.wait_ge(s_cv, 1 + 4 * i + g + 1)
                    act.wait_ge(s_zlo, 1 + 4 * i + g - 1)
                    src = bank[:, 2 + g, :]
                act.activation(zf[:, m, :], src, ACT.Silu, scale=coef[:, 0, m:m + 1],
                               bias=coef[:, 1, m:m + 1]).then_inc(s_zf, 1)

            act.wait_ge(s_const, 2)
            for k in range(KT):
                act.wait_ge(d_y[k], 17)
                act.activation(yp_h[:, k, 1:1 + W, 1:1 + W], y_in[:, k, :].rearrange("p (r c) -> p r c", c=W),
                               ACT.Copy).then_inc(s_yhi, 1)

            def start(l):
                for i in range(N_OWN):
                    piece_high(act, l, i)
                act.wait_ge(s_coef, 1 + 2 * (l + 1))
                z_raw(l * B, 0)
                z_raw(l * B, 1)
                for g in range(4):
                    z_silu(l * B, g)

            def qk_high(it, p):
                def k_high(h):
                    act.wait_ge(s_kf, 1 + 2 * it + p + 1)
                    act.activation(kk[own(h), h % 2, :], kf[own(h), :], ACT.Copy).then_inc(s_khi, 1)

                def q_high(h):
                    act.wait_ge(s_qk, 1 + 4 * it + 2 * p + 2)
                    act.activation(qq[own(h), h % 2, :], two(0)[own(h)], ACT.Copy).then_inc(s_qhi, 1)

                k_high(2 * p)
                q_high(2 * p)
                q_high(2 * p + 1)
                k_high(2 * p + 1)

            def o_high(it, h):
                act.wait_ge(s_om, 1 + 4 * it + h + 1)
                act.activation(o_h[own(h), h // 2, :], os[own(h), :], ACT.Copy).then_inc(s_ohi, 1)

            def exps(it, h, t):
                T = 32 * it + 8 * h + t
                act.wait_ge(s_lt, 1 + T + 1)
                first = t < 2 and h == 0
                act.wait_ge(s_al, 1 + 32 * it if first else 1 + T - 1)
                act.wait_ge(s_avh, 1 + 32 * it if first else 1 + T - 1)
                act.activation(a_h[:, t % 2, :], two(2 * (t % 2)), ACT.Exp, scale=SCALE).then_inc(s_ah, 1)
                if first:
                    act.wait_ge(d_out[t], 1 + 32 * it)
                act.activation(a_f[:, t % 2, :], two(2 * (t % 2)), ACT.Exp, scale=SCALE).then_inc(s_af, 1)

            def o_out(it, h):
                act.wait_ge(s_avl, 1 + 32 * it + 8 * h + 8)
                act.wait_ge(s_olo, 1 + 4 * it + h)
                act.activation(os[:], two(6), ACT.Copy).then_inc(s_os, 1)

            def image(it, l, b, has_next, has_next2):
                for half in range(2):
                    if half == 1:
                        qk_high(it, 0)
                    act.wait_ge(s_v, 1 + 2 * it + half + 1)
                    src = two(6 if half == 0 else 4).rearrange("p (b e s c) -> p b e s c", b=4, e=2, s=2)
                    for e in range(2):
                        ins = act.activation(v_h[:, 4 * half:4 * half + 4, :, 2 * e, :], src[:, :, e, :, :], ACT.Copy)
                    ins.then_inc(s_vhi, 1)
                act.wait_ge(s_table, 1 + it)
                act.activation(zero[:, 1:2], zero[:, 0:1], ACT.Exp).then_inc(s_table, 1)
                for p in range(2):
                    if has_next:
                        z_raw(it + 1, p)
                    exps(it, 2 * p, 0)
                    for h in (2 * p, 2 * p + 1):
                        for t in range(8):
                            if t < 7:
                                exps(it, h, t + 1)
                            elif h % 2 == 0:
                                exps(it, h + 1, 0)
                            if h > 0 and t == 6:
                                o_high(it, h - 1)
                            if not has_next and (h, t) in NEXT_AT:
                                piece_high(act, l, NEXT_AT[h, t])
                        o_out(it, h)
                    if p == 0:
                        qk_high(it, 1)
                if has_next:
                    for g in range(4):
                        z_silu(it + 1, g)
                        if g == 2:
                            o_high(it, 3)
                else:
                    o_high(it, 3)
                for g in range(4):
                    m = g % 2
                    act.wait_ge(s_cm, 1 + 4 * it + g + 1)
                    act.wait_ge(s_al, 1 + 32 * (it + 1))
                    act.activation(a_f[:, m, px(g // 2)], bank[:, g, :], ACT.Silu, scale=coef[:, 0, 2 + m:3 + m],
                                   bias=coef[:, 1, 2 + m:3 + m]).then_inc(s_cf, 1)

            layers(act, start, image)

        @block.vector
        def _(dve):
            def z_low(i, g):
                c, m = g // 2, g % 2
                dve.wait_ge(s_zhi, 1 + 4 * i + g + 1)
                dve.tensor_tensor(z_l[:, m, px(c)], zf[:, m, :], f32(z_h[:, m, px(c)]), ALU.subtract).then_inc(s_zlo, 1)

            def y_low(i):
                for k in range(KT):
                    dve.wait_ge(s_yhi, 1 + KT * i + k + 1)
                    dve.tensor_tensor(yp_l[:, k, 1:1 + W, 1:1 + W], y_in[:, k, :].rearrange("p (r c) -> p r c", c=W),
                                      f32(yp_h[:, k, 1:1 + W, 1:1 + W]), ALU.subtract).then_inc(s_ylo, 1)

            def start(l):
                dve.wait_ge(s_cf, 1 + 4 * B * l)
                dve.tensor_copy(coef[:, 0, :], bn_s[:, bass.ds(8 + 4 * l, 4)]).then_inc(s_coef, 1)
                dve.tensor_copy(coef[:, 1, :], bn_o[:, bass.ds(8 + 4 * l, 4)]).then_inc(s_coef, 1)
                for i in range(N_OWN):
                    piece_low(dve, l, i)
                for g in range(4):
                    z_low(l * B, g)
                y_low(l * B + 1)

            def qk_out(it, p):
                def q_low(h):
                    dve.wait_ge(s_qhi, 1 + 4 * it + h + 1)
                    dve.tensor_tensor(qm[own(h), h % 2, :], two(0)[own(h)], f32(qq[own(h), h % 2, :]),
                                      ALU.subtract).then_inc(s_qlo, 1)
                dve.wait_ge(s_qk, 1 + 4 * it + 2 * p + 1)
                dve.wait_ge(s_kr, 1 + 2 * it + p + 1)
                dve.tensor_tensor(kf[:], two(2), kf[:], ALU.add).then_inc(s_kf, 1)

                def k_low(h):
                    dve.wait_ge(s_khi, 1 + 4 * it + h + 1)
                    dve.tensor_tensor(kk[other(h), h % 2, :], kf[own(h), :], f32(kk[own(h), h % 2, :]),
                                      ALU.subtract).then_inc(s_klo, 1)

                k_low(2 * p)
                q_low(2 * p)
                q_low(2 * p + 1)
                k_low(2 * p + 1)

            def reduce_block(it, h, n, b0):
                dve.wait_ge(s_mx, 1 + 32 * it + 8 * h + n + 1)
                dve.tensor_reduce(mt[:, h % 2, n:n + 1], two(b0), AX.X, ALU.max, negate=True).then_inc(s_mr, 1)

            def a_low(it, h, t):
                T = 32 * it + 8 * h + t
                dve.wait_ge(s_ah, 1 + T + 1)
                dve.wait_ge(s_af, 1 + T + 1)
                if not (h == 0 and t < 2):
                    dve.wait_ge(s_avl, 1 + T - 1)
                else:
                    dve.wait_ge(s_avl, 1 + 32 * it)
                dve.tensor_tensor(a_l[:, t % 2, :], a_f[:, t % 2, :], f32(a_h[:, t % 2, :]),
                                  ALU.subtract).then_inc(s_al, 1)

            def o_recip(it, h):
                dve.wait_ge(d_s8, 1 + 16 * (4 * it + h + 1))
                dve.reciprocal(r8i[:], r8[:]).then_inc(s_rc, 1)

            def o_mult(it, h):
                dve.wait_ge(d_rb, 1 + 16 * (4 * it + h + 1))
                dve.tensor_tensor(os[own(h), :], os[own(h), :], rb[own(h), :], ALU.mult).then_inc(s_om, 1)

            def o_low(it, h):
                dve.wait_ge(s_ohi, 1 + 4 * it + h + 1)
                dve.tensor_tensor(o_l[own(h), h // 2, :], os[own(h), :], f32(o_h[own(h), h // 2, :]),
                                  ALU.subtract).then_inc(s_olo, 1)

            y_low(0)
            for h in range(2):
                dve.memset(f32(qm[other(h), h, :]), 0.0)
                ins = dve.memset(f32(k1[other(h), h, :]), 0.0)
            ins.then_inc(s_const_rows, 1)
            dve.wait_ge(s_const_rows, 2)
            for h in range(2):
                ins = dve.memset(f32(k1[first_other(h), h, :]), 1.0)
            ins.then_inc(s_const_rows, 1)

            def image(it, l, b, has_next, has_next2):
                for half in range(2):
                    if half == 1:
                        qk_out(it, 0)
                    dve.wait_ge(s_vhi, 1 + 2 * it + half + 1)
                    src = two(6 if half == 0 else 4).rearrange("p (b e s c) -> p b e s c", b=4, e=2, s=2)
                    for e in range(2):
                        blocks = (slice(None), slice(4 * half, 4 * half + 4), slice(None), 2 * e, slice(None))
                        ins = dve.tensor_tensor(v_l[blocks], src[:, :, e, :, :], f32(v_h[blocks]), ALU.subtract)
                    ins.then_inc(s_vlo, 1)
                for p in range(2):
                    if p == 1:
                        qk_out(it, 1)
                    for n in range(8):
                        reduce_block(it, 2 * p, n, 0 if n % 2 == 0 else 6)
                    reduce_block(it, 2 * p + 1, 0, 4)
                    reduce_block(it, 2 * p + 1, 1, 4)
                    for h in (2 * p, 2 * p + 1):
                        for t in range(8):
                            if h % 2 == 0 and t <= 5:
                                reduce_block(it, h + 1, t + 2, 4)
                            a_low(it, h, t)
                            if h > 0 and t == 1:
                                o_recip(it, h - 1)
                            if h > 0 and t == 5:
                                o_mult(it, h - 1)
                            if h > 0 and t == 7:
                                o_low(it, h - 1)
                            if not has_next and (h, t) in NEXT_AT:
                                piece_low(dve, l, NEXT_AT[h, t])
                o_recip(it, 3)
                if has_next:
                    z_low(it + 1, 0)
                    z_low(it + 1, 1)
                o_mult(it, 3)
                o_low(it, 3)
                if has_next:
                    z_low(it + 1, 2)
                    z_low(it + 1, 3)
                if has_next2:
                    y_low(it + 2)
                if not has_next:
                    y_low(it + 1)

            layers(dve, start, image)

        @block.gpsimd
        def _(pool):
            def copy(dst, src):
                alone(pool, s_spare_pool)
                return pool.tensor_scalar(dst, src, 1.0, None, ALU.mult)

            for t in (yp_h, yp_l):
                pool.memset(f32(t[:]), 0.0)
            pool.memset(zero[:], 0.0).then_inc(s_const, 1)
            pool.memset(f32(v_l[:, :, :, 1, :]), 0.0)
            pool.memset(f32(v_h[:, :, :, 1, :]), 1.0).then_inc(s_const, 1)

            def y_high(i):
                for k in range(KT):
                    pool.wait_ge(d_y[k], 1 + 16 * (i + 1))
                    pool.wait_ge(s_cv, 1 + 4 * i)
                    copy(yp_h[:, k, 1:1 + W, 1:1 + W],
                         y_in[:, k, :].rearrange("p (r c) -> p r c", c=W)).then_inc(s_yhi, 1)

            def z_high(i, g):
                c, m = g // 2, g % 2
                pool.wait_ge(s_zf, 1 + 4 * i + g + 1)
                copy(z_h[:, m, px(c)], zf[:, m, :]).then_inc(s_zhi, 1)

            def k_rel(it, p):
                pool.wait_ge(s_klo, 1 + 4 * it + 2 * p)
                pool.wait_ge(s_om, 1 + 4 * it + p)
                pool.tensor_tensor(kf[:].rearrange("p (r c) -> p r c", c=W),
                                   rhs[:, p, :].unsqueeze(2).to_broadcast([P, W, W]),
                                   rws[:, p, :].unsqueeze(1).to_broadcast([P, W, W]), ALU.add).then_inc(s_kr, 1)

            def start(l):
                for g in range(4):
                    z_high(l * B, g)
                y_high(l * B + 1)
                pool.wait_ge(d_r, 1 + 32 * (l + 1))
                k_rel(l * B, 0)

            def image(it, l, b, has_next, has_next2):
                k_rel(it, 1)
                if has_next:
                    for g in range(4):
                        z_high(it + 1, g)
                        if g == 2:
                            k_rel(it + 1, 0)
                if has_next2:
                    y_high(it + 2)
                if not has_next:
                    y_high(it + 1)
                for g in range(4):
                    pool.wait_ge(s_cf, 1 + 4 * it + g + 1)
                    pool.wait_ge(d_res[g % 2], 1 + 16 * (2 * it + g // 2 + 1))
                    pool.tensor_tensor(a_f[:, g % 2, px(g // 2)], res[:, g % 2, :], a_f[:, g % 2, px(g // 2)],
                                       ALU.add).then_inc(s_res, 1)

            layers(pool, start, image)

        @block.sync
        def _(sp):
            def load_y(l, i, b):
                alone(sp, s_spare)
                for k in range(KT):
                    sp.dma_start(y_in[:, k, :], y_d[b, 2 + KT * l + k]).then_inc(d_y[k], 16)

            for k in range(KT):
                sp.dma_start(y_in[:, k, :], y_d[0, 2 + k]).then_inc(d_y[k], 16)

            def start(l):
                sp.wait_ge(s_kr, 1 + 2 * B * l)
                alone(sp, s_spare)
                sp.dma_start(rws[:], rw[bass.ds(l, 1)].rearrange("o p t c -> (o p) t c")).then_inc(d_r, 16)
                sp.dma_start(rhs[:], rh[bass.ds(l, 1)].rearrange("o p t c -> (o p) t c")).then_inc(d_r, 16)
                sp.wait_ge(s_res, 1 + 4 * B * l)
                alone(sp, s_spare)
                for i in range(N_OWN):
                    load_piece(sp, l, l, i)
                for s in range(2):
                    sp.wait_ge(d_out[s], 1 + 32 * B * l)
                alone(sp, s_spare)
                sp.wait_ge(s_ylo, 1 + KT * (B * l + 1))
                load_y(l, l * B + 1, 1)
                sp.wait_ge(s_wlo, 1 + N_ALL * l + N_OWN)
                stacks(l * B, 0)

            def stacks(it, p):
                for h in (2 * p, 2 * p + 1):
                    sp.wait_ge(s_qhi, 1 + 4 * it + h + 1)
                    sp.dma_start(f32(qq[other(h), h % 2, :]), f32(qq[own(h), h % 2, :])).then_inc(d_qq[h % 2], 16)
                for h in (2 * p, 2 * p + 1):
                    sp.wait_ge(s_khi, 1 + 4 * it + h + 1)
                    sp.dma_start(f32(k1[own(h), h % 2, :]), f32(kk[own(h), h % 2, :])).then_inc(d_k1[h % 2], 16)

            def max_row(it, h):
                sp.wait_ge(s_mr, 1 + 32 * it + 8 * h + 8)
                alone(sp, s_spare)
                sp.wait_ge(s_qlo, 1 + 4 * it + h + 1)
                sp.dma_start(f32(qm[first_other(h), h % 2, :]).rearrange("o (p c) -> o p c", c=8),
                             f32(mt[:, h % 2, :])).then_inc(d_m[h % 2], 16)

            def sums(it, h):
                sp.wait_ge(s_os, 1 + 4 * it + h + 1)
                sp.dma_start(r8[:], os[first_other(h), :].rearrange("o (p c) -> o p c", c=8)).then_inc(d_s8, 16)

            def recips(it, h):
                sp.wait_ge(s_rc, 1 + 4 * it + h + 1)
                sp.dma_start(rs_d.rearrange("o (p c) -> (o p) c", c=8), r8i[:]).then_inc(d_rc, 16)
                sp.wait_ge(d_rc, 1 + 16 * (4 * it + h + 1))
                sp.dma_start(rb[own(h), :], rs_d.to_broadcast([HD, HW])).then_inc(d_rb, 16)

            def load_res(l, b, g):
                c, m = g // 2, g % 2
                alone(sp, s_spare)
                sp.dma_start(res[:, g % 2, :], y_d[b, 2 + KT * l + m][:, px(c)]).then_inc(d_res[g % 2], 16)

            def image(it, l, b, has_next, has_next2):
                if not has_next:
                    sp.wait_ge(s_cv, 1 + 4 * (it + 1))
                    alone(sp, s_spare)
                    sp.wait_ge(s_ylo, 1 + KT * (it + 1))
                    alone(sp, s_spare)
                    for i in (4, 5):
                        load_piece(sp, l, l + 1, i)
                max_row(it, 0)
                max_row(it, 1)
                for g in range(2):
                    sp.wait_ge(s_res, 1 + 4 * it)
                    load_res(l, b, g)
                sums(it, 0)
                recips(it, 0)
                if not has_next:
                    alone(sp, s_spare)
                    for i in range(6, 11):
                        load_piece(sp, l, l + 1, i)
                sums(it, 1)
                stacks(it, 1)
                max_row(it, 2)
                recips(it, 1)
                max_row(it, 3)
                sums(it, 2)
                recips(it, 2)
                if has_next2:
                    sp.wait_ge(s_ylo, 1 + KT * (it + 2))
                    load_y(l, it + 2, b + 2)
                if not has_next:
                    alone(sp, s_spare)
                    for i in range(11, 13):
                        load_piece(sp, l, l + 1, i)
                sums(it, 3)
                recips(it, 3)
                if not has_next:
                    for s in range(2):
                        sp.wait_ge(d_out[s], 1 + 32 * it)
                    alone(sp, s_spare)
                    sp.wait_ge(s_wlo, 1 + N_ALL * (l + 1))
                    load_y(l + 1, it + 1, 0)
                for g in range(4):
                    c, m = g // 2, g % 2
                    if g == 2 and has_next:
                        stacks(it + 1, 0)
                    sp.wait_ge(s_res, 1 + 4 * it + g + 1)
                    if g < 2:
                        load_res(l, b, g + 2)
                    alone(sp, s_spare)
                    sp.dma_start(y_d[b, 4 + KT * l + m][:, px(c)], a_f[:, m, px(c)]).then_inc(d_out[m], 16)

            layers(sp, start, image)
            for s in range(2):
                sp.wait_ge(d_out[s], 1 + 32 * B * L)


def phase_d(nc, sem_, B, CT, x_v, w_hi, w_lo, y_d, x1_d, bank, bn_s, bn_o, x1_mv):
    K8 = 8
    G8 = CT * NC
    YS, XS = 2, 4

    def sem(name):
        return sem_("d_" + name)

    s_spare = sem("s_spare")
    d_y = [sem(f"d_y{i}") for i in range(YS)]
    d_y0 = [sem(f"d_y0_{k}") for k in range(K8)]
    s_yh, s_yl = sem("s_yh"), sem("s_yl")
    s_mm, s_sf, s_x1, s_st, s_ag = sem("s_mm"), sem("s_sf"), sem("s_x1"), sem("s_st"), sem("s_ag")
    s_mv = sem("s_mv")
    d_x = [sem(f"d_x{i}") for i in range(XS)]
    d_o = [sem(f"d_o{i}") for i in range(XS)]
    yield

    with ExitStack() as ctx:
        def sb(name, shape, dt):
            return ctx.enter_context(nc.sbuf_tensor("d_" + name, shape, dt))

        yin = sb("yin", [P, YS, HW], F32)
        yh = sb("yh", [P, 2, K8, HW], F32R)
        yl = sb("yl", [P, 2, K8, HW], F32R)
        sf = sb("sf", [P, 2, NB], F32)
        xr = sb("xr", [P, XS, NB], F32)
        stats = sb("stats", [P, CT, NC, 6], F32)
        mv = sb("mv", [P, CT, 2], F32)

        block = ctx.enter_context(nc.Block())

        @block.sync
        def _(sp):
            def load_y(n, k):
                alone(sp, s_spare)
                sp.dma_start(yin[:, k % YS, :], y_d[n, k]).then_inc(d_y[k % YS], 16)

            def load_x(n, g):
                alone(sp, s_spare)
                sp.dma_start(xr[:, g % XS, :], x_v[n, g // NC][:, (g % NC) * NB:(g % NC + 1) * NB]).then_inc(d_x[g % XS], 16)

            for k in range(K8):
                sp.dma_start(f32(yh[:, 1, k, :]), y_d[0, k]).then_inc(d_y0[k], 16)
            for g in range(XS):
                load_x(0, g)

            def image(j, u, left):
                n = 2 * j + u
                for g in range(G8):
                    if left:
                        sp.wait_ge(s_yl, 1 + K8 * (n + 1) + g - YS + 1)
                        load_y(n + 1, g)
                    sp.wait_ge(s_x1, 1 + G8 * n + g + 1)
                    alone(sp, s_spare)
                    sp.dma_start(x1_d[n, g // NC][:, (g % NC) * NB:(g % NC + 1) * NB], xr[:, g % XS, :]).then_inc(d_o[g % XS], 16)
                    if g >= 1 and g - 1 + XS < G8:
                        q = g - 1
                        sp.wait_ge(d_o[q % XS], 1 + 32 * n + 16 * (q // XS + 1))
                        sp.wait_ge(s_st, 1 + G8 * n + q + 1)
                        load_x(n, q + XS)
                    if g >= XS + 1 and left:
                        q = g - 1
                        sp.wait_ge(d_o[q % XS], 1 + 32 * n + 16 * (q // XS + 1))
                        sp.wait_ge(s_st, 1 + G8 * n + q + 1)
                        load_x(n + 1, q - XS)
                if left:
                    q = G8 - 1
                    sp.wait_ge(d_o[q % XS], 1 + 32 * n + 16 * (q // XS + 1))
                    sp.wait_ge(s_st, 1 + G8 * n + q + 1)
                    load_x(n + 1, q - XS)

            images(sp, B, image)
            for i in range(XS):
                sp.wait_ge(d_o[i], 1 + 16 * B * G8 // XS)

        @block.scalar
        def _(act):
            def high(after, u, k):
                act.wait_ge(d_y[k % YS], 1 + 16 * K8 // YS * after + 16 * (k // YS + 1))
                act.activation(yh[:, u, k, :], yin[:, k % YS, :], ACT.Copy).then_inc(s_yh, 1)

            act.sem_inc(s_sf, G8)
            for k in range(K8):
                act.wait_ge(d_y0[k], 17)
                act.activation(yh[:, 0, k, :], f32(yh[:, 1, k, :]), ACT.Copy).then_inc(s_yh, 1)

            def image(j, u, left):
                n = 2 * j + u
                for g in range(G8):
                    m = g // NC
                    act.wait_ge(s_mm, 1 + G8 * n + g + 1)
                    act.wait_ge(s_x1, 1 + G8 * n + max(g - 1, 0))
                    act.activation(sf[:, g % 2, :], bank[:, g % 8, :], ACT.Silu, scale=bn_s[:, 4 + m:5 + m],
                                   bias=bn_o[:, 4 + m:5 + m]).then_inc(s_sf, 1)
                    if left:
                        high(n, 1 - u, g)

            images(act, B, image)

        @block.vector
        def _(dve):
            def low(n, u, k):
                dve.wait_ge(s_yh, 1 + K8 * n + k + 1)
                dve.tensor_tensor(yl[:, u, k, :], yin[:, k % YS, :], f32(yh[:, u, k, :]), ALU.subtract).then_inc(s_yl, 1)

            for k in range(K8):
                dve.wait_ge(s_yh, 1 + k + 1)
                dve.tensor_tensor(yl[:, 0, k, :], f32(yh[:, 1, k, :]), f32(yh[:, 0, k, :]), ALU.subtract).then_inc(s_yl, 1)

            def image(j, u, left):
                n = 2 * j + u
                for g in range(G8):
                    if left:
                        low(n + 1, 1 - u, g)
                    dve.wait_ge(s_x1, 1 + G8 * n + g + 1)
                    dve.wait_ge(s_mv, 1 + n)
                    dve.bn_stats(stats[:, g // NC, g % NC, :], xr[:, g % XS, :]).then_inc(s_st, 1)
                dve.wait_ge(s_st, 1 + G8 * (n + 1))
                alone(dve, s_spare)
                for t in range(CT):
                    ins = dve.bn_aggr(mv[:, t, :], stats[:, t, :, :])
                ins.then_inc(s_ag, 1)
                dve.wait_ge(s_ag, 1 + n + 1)
                dve.tensor_copy(x1_mv[:, bass.ds(n, 1), :, :].rearrange("p o t s -> p (o t s)"),
                                mv[:].rearrange("p t s -> p (t s)")).then_inc(s_mv, 1)

            images(dve, B, image)

        @block.gpsimd
        def _(pool):
            def image(j, u, left):
                n = 2 * j + u
                for g in range(G8):
                    pool.wait_ge(s_sf, 1 + G8 + G8 * n + g + 1)
                    pool.wait_ge(d_x[g % XS], 1 + 32 * n + 16 * (g // XS + 1))
                    pool.tensor_tensor(xr[:, g % XS, :], xr[:, g % XS, :], sf[:, g % 2, :], ALU.add).then_inc(s_x1, 1)

            images(pool, B, image)

        @block.tensor
        def _(pe):
            def image(j, u, left):
                n = 2 * j + u
                for g in range(G8):
                    m, c = g // NC, g % NC
                    px = slice(c * NB, (c + 1) * NB)
                    pe.wait_ge(s_sf, 1 + G8 * n + g + 1)
                    for k in range(K8):
                        if g == 0:
                            pe.wait_ge(s_yl, 1 + K8 * n + k + 1)
                        wk = slice(k * 512 + m * P, k * 512 + (m + 1) * P)
                        pe.matmul(bank[:, g, :], w_hi[:, wk], yh[:, u, k, px], start=k == 0, stop=False)
                        pe.matmul(bank[:, g, :], w_hi[:, wk], yl[:, u, k, px], start=False, stop=False)
                        mm = pe.matmul(bank[:, g, :], w_lo[:, wk], yh[:, u, k, px], start=False, stop=k == K8 - 1)
                    mm.then_inc(s_mm, 1)

            images(pe, B, image)


def phase_l(nc, sem_, B, CT, w1_rows, w1_t, bn1, x1_d, out_v, bank, group_avg, mhalf, x1_mv):
    N = B * CT
    CIN = 32

    def turn_images(eng, body):
        body(0, 0, True, False)
        if B > 4:
            with eng.Fori(0, B // 2 - 1) as j:
                body(2 * j + 1, 1, False, False)
                body(2 * j + 2, 0, False, False)
        else:
            for n in range(1, B - 1):
                body(n, n % 2, False, False)
        body(B - 1, 1, False, True)

    def sem(name):
        return sem_("l_" + name)

    d_w, s_c, s_eps, s_rs = sem("d_w"), sem("s_c"), sem("s_eps"), sem("s_rs")
    s_aff, s_gs, s_gm = sem("s_aff"), sem("s_gs"), sem("s_gm")
    s_wz, s_wb = sem("s_wz"), sem("s_wb")
    d_x = [sem(f"d_x{i}") for i in range(2)]
    s_sg, s_mm, s_h, s_hs = sem("s_sg"), sem("s_mm"), sem("s_h"), sem("s_hs")
    s_spare, s_spare_pool = sem("s_spare"), sem("s_spare_pool")
    s_u, s_v, s_q, s_p, s_o = sem("s_u"), sem("s_v"), sem("s_q"), sem("s_p"), sem("s_o")
    s_t2 = sem("s_t2")
    d_o = [sem(f"d_o{i}") for i in range(2)]
    yield

    with ExitStack() as ctx:
        def sb(name, shape, dt):
            return ctx.enter_context(nc.sbuf_tensor("l_" + name, shape, dt))

        wr = sb("wr", [P, CT, CIN * TAPS], F32)
        wt = sb("wt", [P, CT, TAPS, CIN], F32)
        wb = sb("wb", [P, CT, TAPS, P], BF16)
        bnp = sb("bnp", [P, 5, CT], F32)
        wst = sb("wst", [P, CT, 6], F32)
        wmv = sb("wmv", [P, CT, 2], F32)
        wab = sb("wab", [P, CT], F32)
        sw = sb("sw", [P, CT], F32)
        t1 = sb("t1", [P, N], F32)
        t2 = sb("t2", [P, N], F32)
        gmean = sb("gmean", [P, B, CT], F32)
        r_g = sb("r_g", [P, B, CT], F32)
        t_g = sb("t_g", [P, B, CT], F32)
        cm = sb("cm", [P, B, CT], F32)
        cv = sb("cv", [P, B, CT], F32)
        m1 = sb("m1", [P, CT], F32)
        v1 = sb("v1", [P, CT], F32)
        i1 = sb("i1", [P, CT], F32)
        a1 = sb("a1", [P, CT], F32)
        sa = sb("sa", [P, B, CT], F32)
        sc = sb("sc", [P, B, CT], F32)
        xs = sb("xs", [P, 3, B, HW], F32)
        sg = sb("sg", [P, 2, PW, PW], BF16)
        h = sb("h", [P, 2, B, HW], F16)
        hst = sb("hst", [P, CT, B * NC, 6], F32)
        hmv = sb("hmv", [P, CT, 2], F32)
        a2 = sb("a2", [P, CT], F32)
        b2 = sb("b2", [P, CT], F32)
        sw2 = sb("sw2", [P, CT], F32)
        swg = sb("swg", [P, CT], F32)
        u_ = sb("u_", [P, 2, HW], F32)
        v_ = sb("v_", [P, 2, HW], F32)
        p_ = sb("p_", [P, 2, HW], F32)
        a_1 = sb("a_1", [P, CT], F32)

        def of_image(tile, slot, n):
            return tile[:, slot, bass.ds(n, 1), :].rearrange("p o n -> p (o n)")

        def px(c):
            return slice(c * NB, (c + 1) * NB)

        flat = lambda t: t[:].rearrange("p b c -> p (b c)")
        over_b = lambda t: t[:].unsqueeze(1).to_broadcast([P, B, CT])
        block = ctx.enter_context(nc.Block())

        @block.sync
        def _(sp):
            sp.dma_start(bnp[:], bn1).then_inc(d_w, 16)
            sp.dma_start(wr[:], w1_rows).then_inc(d_w, 16)
            sp.dma_start(wt[:], w1_t).then_inc(d_w, 16)

            def load(t, n, u):
                sp.wait_ge(d_x[u], 1 + 8 * (t * B + n - u))
                alone(sp, s_spare)
                sp.dma_start(of_image(xs, t % 3, n), x1_d[n, t]).then_inc(d_x[u], 16)

            turn_images(sp, lambda n, u, first, last: load(0, n, u))
            for t in range(CT + 1):
                if t >= 2:
                    for u in range(2):
                        sp.wait_ge(d_o[u], 1 + 8 * B * (t - 1))

                def image(n, u, first, last):
                    if t >= 1:
                        sp.wait_ge(s_o, 1 + (t - 1) * B + n + 1)
                        alone(sp, s_spare)
                        sp.dma_start(out_v[n, t - 1], of_image(xs, (t - 1) % 3, n)).then_inc(d_o[u], 16)
                    if t + 1 < CT:
                        load(t + 1, n, u)

                turn_images(sp, image)
            for u in range(2):
                sp.wait_ge(d_o[u], 1 + 8 * B * CT)

        @block.vector
        def _(dve):
            links = [0]

            def link(ins):
                links[0] += 1
                ins.then_inc(s_c, 1)
                dve.wait_ge(s_c, 1 + links[0])

            rsq = [0]

            def rsqrt(dst, src, eps):
                rsq[0] += 1
                dve.tensor_scalar(t1[:, 0:src.free_size()], src, eps, None, ALU.add).then_inc(s_eps, 1)
                dve.wait_ge(s_rs, 1 + rsq[0])
                link(dve.tensor_copy(dst, t2[:, 0:src.free_size()]))

            link(dve.tensor_copy(flat(cm), x1_mv[:, :, :, 0].rearrange("p b c -> p (b c)")))
            dve.tensor_copy(flat(cv), x1_mv[:, :, :, 1].rearrange("p b c -> p (b c)")).then_inc(s_gs, 1)
            dve.wait_ge(s_gm, 2)
            link(dve.tensor_copy(flat(gmean), bank[:, 7, 0:N]))
            link(dve.tensor_tensor(flat(t_g), flat(cm), flat(gmean), ALU.subtract))
            link(dve.tensor_tensor(flat(r_g), flat(t_g), flat(t_g), ALU.mult))
            dve.tensor_tensor(flat(sa), flat(r_g), flat(cv), ALU.add).then_inc(s_gs, 1)
            dve.wait_ge(s_gm, 3)
            rsqrt(flat(r_g), bank[:, 7, 64:64 + N], GN_EPS)
            link(dve.tensor_tensor(flat(cm), flat(t_g), flat(r_g), ALU.mult))
            link(dve.scalar_tensor_tensor(flat(t_g), flat(gmean), -1.0, flat(r_g), ALU.mult, ALU.mult))
            link(dve.tensor_tensor(flat(cv), flat(cv), flat(r_g), ALU.mult))
            link(dve.tensor_tensor(flat(cv), flat(cv), flat(r_g), ALU.mult))
            link(dve.tensor_reduce(m1[:], cm[:].rearrange("p b c -> p c b"), AX.X, ALU.add))
            link(dve.tensor_scalar(m1[:], m1[:], 1.0 / B, None, ALU.mult))
            link(dve.tensor_tensor(cm[:], cm[:], over_b(m1), ALU.subtract))
            link(dve.tensor_tensor(flat(cm), flat(cm), flat(cm), ALU.mult))
            link(dve.tensor_tensor(flat(cm), flat(cm), flat(cv), ALU.add))
            link(dve.tensor_reduce(v1[:], cm[:].rearrange("p b c -> p c b"), AX.X, ALU.add))
            link(dve.tensor_scalar(v1[:], v1[:], 1.0 / B, None, ALU.mult))
            rsqrt(i1[:], v1[:], BN1_EPS)
            dve.wait_ge(d_w, 49)
            link(dve.tensor_tensor(a1[:], i1[:], bnp[:, 0, :], ALU.mult))
            link(dve.tensor_tensor(sa[:], r_g[:], over_b(a1), ALU.mult))
            link(dve.tensor_tensor(sc[:], t_g[:], over_b(m1), ALU.subtract))
            link(dve.tensor_tensor(sc[:], sc[:], over_b(a1), ALU.mult))
            dve.tensor_tensor(sc[:], sc[:], bnp[:, 1:2, :].to_broadcast([P, B, CT]), ALU.add).then_inc(s_aff, 1)

            n_w = CIN * TAPS
            for t in range(CT):
                ins = dve.bn_stats(wst[:, t, :], wr[:, t, :])
            link(ins)
            for t in range(CT):
                ins = dve.bn_aggr(wmv[:, t, :], wst[:, t, :])
            link(ins)
            link(dve.tensor_tensor(wr[:], wr[:], wmv[:, :, 0:1].to_broadcast([P, CT, n_w]), ALU.subtract))
            link(dve.tensor_reduce(wab[:], wr[:], AX.X, ALU.add, apply_absolute_value=True))
            link(dve.tensor_scalar(sw[:], wmv[:, :, 1], float(n_w) / (n_w - 1), None, ALU.mult))
            rsqrt(sw[:], sw[:], 0.0)
            link(dve.tensor_tensor(sw[:], sw[:], wab[:], ALU.mult))
            link(dve.tensor_scalar(sw[:], sw[:], 1.0 / n_w, None, ALU.mult))

            link(dve.tensor_tensor(sw2[:], sw[:], sw[:], ALU.mult))
            link(dve.tensor_tensor(swg[:], sw[:], bnp[:, 2, :], ALU.mult))
            link(dve.tensor_scalar(a_1[:], bnp[:, 4, :], -1.0, 1.0, ALU.mult, ALU.add))

            def batch_norm_2(t):
                col = slice(t, t + 1)
                dve.wait_ge(s_hs, 1 + NC * B * (t + 1))
                link(dve.bn_aggr(hmv[:, t, :], hst[:, t, :, :]))
                link(dve.tensor_tensor(v1[:, col], sw2[:, col], hmv[:, t, 1:2], ALU.mult))
                rsqrt(i1[:, col], v1[:, col], BN1_EPS)
                link(dve.tensor_tensor(a2[:, col], i1[:, col], swg[:, col], ALU.mult))
                link(dve.tensor_tensor(b2[:, col], a2[:, col], hmv[:, t, 0:1], ALU.mult))
                link(dve.tensor_tensor(b2[:, col], bnp[:, 3, col], b2[:, col], ALU.subtract))
                dve.tensor_tensor(t_g[:, :, t], t_g[:, :, t], b2[:, col].to_broadcast([P, B]), ALU.add).then_inc(s_t2, 1)

            def prelu(t, n, u):
                dve.wait_ge(s_q, 1 + t * B + n + 1)
                dve.scalar_tensor_tensor(p_[:, u, :], p_[:, u, :], a_1[:, t:t + 1], v_[:, u, :],
                                         ALU.mult, ALU.add).then_inc(s_p, 1)

            for t in range(CT + 1):
                def image(n, u, first, last):
                    for c in range(NC if t < CT else 0):
                        dve.wait_ge(s_h, 1 + 2 * NC + NC * (t * B + n) + c + 1)
                        dve.bn_stats(hst[:, t, bass.ds(NC * n + c, 1), :].rearrange("p o s -> p (o s)"),
                                     of_image(h, t % 2, n)[:, px(c)]).then_inc(s_hs, 1)
                    if t >= 1:
                        dve.wait_ge(s_u, 1 + (t - 1) * B + n + 1)
                        if t > 1 or not first:
                            dve.wait_ge(s_p, 1 + (t - 1) * B + n - 1)
                        alone(dve, s_spare)
                        dve.scalar_tensor_tensor(v_[:, u, :], of_image(h, (t - 1) % 2, n), a2[:, t - 1:t], u_[:, u, :],
                                                 ALU.mult, ALU.add).then_inc(s_v, 1)
                        if not first:
                            prelu(t - 1, n - 1, 1 - u)
                    if last and t < CT:
                        batch_norm_2(t)
                    if last and t >= 1:
                        prelu(t - 1, n, u)

                turn_images(dve, image)

        @block.gpsimd
        def _(pool):
            for edge in (0, PW - 1):
                pool.memset(sg[:, :, edge, :], 0.0)
                pool.memset(sg[:, :, 1:1 + W, edge], 0.0).then_inc(s_wz, 1)

            powers = [0]

            def power(n):
                powers[0] += 1
                pool.wait_ge(s_eps, 1 + powers[0])
                pool.tensor_tensor(t2[:, 0:n], t1[:, 0:n], mhalf[:, 0:n], ALU.pow).then_inc(s_rs, 1)

            pool.memset(wb[:], 0.0).then_inc(s_wz, 1)
            power(N)
            power(CT)
            power(CT)
            for t in range(CT + 1):
                def image(n, u, first, last):
                    if last and t < CT:
                        power(1)
                    if t >= 1:
                        pool.wait_ge(s_p, 1 + (t - 1) * B + n + 1)
                        alone(pool, s_spare_pool)
                        x = of_image(xs, (t - 1) % 3, n)
                        pool.tensor_tensor(x, x, p_[:, u, :], ALU.add).then_inc(s_o, 1)

                if t >= 1:
                    turn_images(pool, image)
                else:
                    power(1)

        @block.scalar
        def _(act):
            act.wait_ge(d_w, 49)
            act.wait_ge(s_wz, 4)
            for g in range(4):
                rows = slice(32 * g, 32 * g + 32)
                act.activation(wb[rows, :, :, 32 * g:32 * g + 32], wt[rows, :, :, :], ACT.Sign).then_inc(s_wb, 1)
            act.wait_ge(s_aff, 2)

            def signs(t, n, u):
                act.wait_ge(d_x[u], 1 + 8 * (t * B + n - u) + 16)
                if (t, u) != (0, 0) or not (isinstance(n, int) and n == 0):
                    act.wait_ge(s_mm, 1 + NC * (t * B + n - 1))
                act.activation(sg[:, u, 1:1 + W, 1:1 + W], of_image(xs, t % 3, n).rearrange("p (r c) -> p r c", c=W),
                               ACT.Sign, scale=sa[:, bass.ds(n, 1), t], bias=sc[:, bass.ds(n, 1), t]).then_inc(s_sg, 1)

            signs(0, 0, 0)
            act.sem_inc(s_h, 2 * NC)
            for t in range(CT + 1):
                o = (t - 1) * B

                def negated(n, u):
                    act.wait_ge(s_v, 1 + o + n + 1)
                    if o > 0 or not (isinstance(n, int) and n == 0):
                        act.wait_ge(s_o, 1 + o + n - 1)
                    act.activation(p_[:, u, :], v_[:, u, :], ACT.Relu, scale=-1.0).then_inc(s_q, 1)

                def image(n, u, first, last):
                    if t < CT and not last:
                        signs(t, n + 1, 1 - u)
                    elif t + 1 < CT:
                        signs(t + 1, 0, 0)
                    for c in range(NC if t < CT else 0):
                        act.wait_ge(s_mm, 1 + NC * (t * B + n) + c + 1)
                        if t >= 2 and first and c == 0:
                            act.wait_ge(s_v, 1 + o)
                        act.activation(of_image(h, t % 2, n)[:, px(c)], bank[:, NC * u + c, :],
                                       ACT.Copy).then_inc(s_h, 1)
                    if t >= 1:
                        if first:
                            act.wait_ge(s_t2, 1 + t)
                        if t > 1 or not first:
                            act.wait_ge(s_v, 1 + o + n - 1)
                        act.activation(u_[:, u, :], of_image(xs, (t - 1) % 3, n), ACT.Identity,
                                       scale=r_g[:, bass.ds(n, 1), t - 1],
                                       bias=t_g[:, bass.ds(n, 1), t - 1]).then_inc(s_u, 1)
                        if not first:
                            negated(n - 1, 1 - u)
                        if last:
                            negated(n, u)

                turn_images(act, image)

        @block.tensor
        def _(pe):
            pe.wait_ge(s_gs, 2)
            pe.matmul(bank[:, 7, 0:N], group_avg[:], flat(cm), start=True, stop=True).then_inc(s_gm, 1)
            pe.wait_ge(s_gs, 3)
            pe.matmul(bank[:, 7, 64:64 + N], group_avg[:], flat(sa), start=True, stop=True).then_inc(s_gm, 1)
            pe.wait_ge(s_wb, 5)
            taps = (4, 0, 1, 2, 3, 5, 6, 7, 8)
            for t in range(CT):
                def image(n, u, first, last):
                    q = t * B + n
                    pe.wait_ge(s_sg, 1 + q + 1)
                    for c in range(NC):
                        pe.wait_ge(s_h, 1 + NC * q + c + 1)
                        for k in taps:
                            rows, cols, win = tap_window(k, c, trim_columns=True)
                            mm = pe.matmul(bank[:, NC * u + c, :].rearrange("p (r c) -> p r c", c=W)[:, rows, cols],
                                           wb[:, t, k, :], sg[(slice(None), u) + win],
                                           start=k == taps[0], stop=k == taps[-1])
                        mm.then_inc(s_mm, 1)

                turn_images(pe, image)


def kernel(x, L0_conv_cv1_w, L0_conv_cv1_bn, L0_conv_cv2_w, L0_conv_cv2_bn, L0_conv_m_cv1_w, L0_conv_m_cv1_bn,
           L0_conv_m_qkv_w, L0_conv_m_rw, L0_conv_m_rh, L0_conv_m_cv2_w, L0_conv_m_cv2_bn, L1_conv_conv_w,
           L1_conv_bn1_gamma, L1_conv_bn1_beta, L1_conv_bn2_gamma, L1_conv_bn2_beta, L1_conv_prelu_a):
    import numpy as np
    import concourse.bacc as bacc
    from concourse.bass_utils import run_bass_kernel_spmd as run

    x = np.ascontiguousarray(x)
    shape = x.shape
    B, C = shape[0], shape[1]

    def cols(a):
        a = np.asarray(a)
        return np.moveaxis(a.reshape(a.shape[:-1] + (-1, P)), -1, 0)

    def conv_t(w):
        w = np.asarray(w)
        o, i = w.shape[:2]
        w = w.reshape(o, i // P, P, -1)
        return w.transpose(2, 1, 3, 0).reshape(P, -1)

    cv1_bn, cv2_bn = cols(L0_conv_cv1_bn), cols(L0_conv_cv2_bn)
    m1_bn, m2_bn = cols(L0_conv_m_cv1_bn), cols(L0_conv_m_cv2_bn)
    bn0 = np.concatenate([cv1_bn, cv2_bn] + [q[:, l] for l in range(2) for q in (m1_bn, m2_bn)], axis=2)
    qkv = np.asarray(L0_conv_m_qkv_w).reshape(2, 12, HD, 256)
    qkv = qkv[:, [0, 1, 2, 3, 4, 5, 6, 7, 8, 10, 9, 11]].reshape(2, 768, 256)
    w3 = np.asarray(L0_conv_m_cv1_w)
    wm = np.asarray(L0_conv_m_cv2_w)
    cv2 = conv_t(L0_conv_cv2_w)
    cv2 = np.concatenate([cv2, np.zeros((P, WBN - cv2.shape[1]), cv2.dtype)], axis=1)
    w_b = np.stack([np.concatenate([conv_t(w3[l].reshape(256, 256, 9)), conv_t(qkv[l]), conv_t(wm[l])], axis=1)
                    for l in range(2)] + [cv2])

    def rel(r):
        r = np.asarray(r).reshape(2, 2, P, W)
        return r.transpose(0, 2, 1, 3)

    w1 = np.asarray(L1_conv_conv_w).reshape(C // P, P, 32, 9)
    w1_rows = w1.reshape(C // P, P, 288).transpose(1, 0, 2)
    w1_t = w1.reshape(C // P, 4, 32, 32, 9).transpose(1, 3, 0, 4, 2).reshape(P, C // P, 9, 32)
    bn1 = np.stack([cols(v) for v in (L1_conv_bn1_gamma, L1_conv_bn1_beta, L1_conv_bn2_gamma, L1_conv_bn2_beta,
                                      L1_conv_prelu_a)], axis=1)
    data = {
        "x": x.reshape(B, C, HW), "w_cv1": conv_t(L0_conv_cv1_w), "w_b": w_b,
        "bn0": bn0, "rw": rel(L0_conv_m_rw), "rh": rel(L0_conv_m_rh), "w1_rows": w1_rows, "w1_t": w1_t, "bn1": bn1,
    }
    data = {k: np.ascontiguousarray(v) for k, v in data.items()}
    nc = bacc.Bacc("TRN2", target_bir_lowering=False, num_devices=1)
    args = [nc.dram_tensor(k, v.shape, mybir.dt.from_np(v.dtype), kind="ExternalInput").ap() for k, v in data.items()]
    out = nc.dram_tensor("out", (B, C, HW), F32, kind="ExternalOutput").ap()
    program(nc, *args, out)
    result = run(nc, [data], core_ids=[0])
    return result.results[0]["out"].reshape(shape)
```
